# Optimizing a Trainium2 kernel written in Bass

```python
import numpy as np
import jax
import jax.numpy as jnp

def _softmax(x, axis=-1):
    return jax.nn.softmax(x, axis=axis)

def _gelu(x):
    return jax.nn.gelu(x, approximate=True)

def _silu(x):
    return jax.nn.silu(x)

def _sigmoid(x):
    return jax.nn.sigmoid(x)

def _layernorm(x, axis=-1, eps=1e-05):
    m = jnp.mean(x, axis=axis, keepdims=True)
    v = jnp.var(x, axis=axis, keepdims=True)
    return (x - m) / jnp.sqrt(v + eps)

def _scatter_add(tgt, idx, src, axis=0):
    return tgt.at[idx].add(src)

def _segment_sum(src, seg, n):
    return jax.ops.segment_sum(src, seg, n)
kernel_name = 'mk_perceiver_d1_seqx_r2_d12919'

def setup_inputs(seed: int=0):
    np.random.seed(seed)
    _w = jnp.asarray

    def _rec_inputs():
        import jax
        import jax.numpy as jnp
        _rk = jax.random.key(seed)
        x = -9.806e-05 + 1 * jax.random.normal(jax.random.fold_in(_rk, 1), (16, 128, 512), jnp.float32)
        _lenS = 128 - jax.random.randint(jax.random.fold_in(_rk, 7), (16,), 0, max(1, 128 // 4) + 1, jnp.int32)
        _lenS2 = 2048 - jax.random.randint(jax.random.fold_in(_rk, 8), (16,), 0, max(1, 2048 // 4) + 1, jnp.int32)
        _ctx_1024P = jax.random.normal(jax.random.fold_in(_rk, 11), (16, 16, 512), jnp.float32)
        _ctx_1024c = jax.random.dirichlet(jax.random.fold_in(_rk, 511), 0.3 * jnp.ones((16,), jnp.float32), (16, 2048))
        _ctx_1024t = jnp.einsum('bsk,bkd->bsd', _ctx_1024c, _ctx_1024P)
        _ctx_1024t = _ctx_1024t * jax.lax.rsqrt(jnp.mean(jnp.square(_ctx_1024t)) + 1e-12) * 0.953939
        ctx_1024 = -1.52775e-05 + 0.999936 * (_ctx_1024t + 0.3 * jax.random.normal(jax.random.fold_in(_rk, 611), (16, 2048, 512), jnp.float32))
        return (x, ctx_1024)
    x, ctx_1024 = _rec_inputs()

    def _L0_xattn_setup():
        import jax, jax.numpy as jnp
        import numpy as np
        D_MODEL = 512
        N_HEADS = 16
        HEAD_DIM = D_MODEL // N_HEADS
        key = jax.random.key(seed)
        ks = jax.random.split(key, 10)
        B, NQ, S = (8, 64, 2048)
        inv = 1.0 / np.sqrt(D_MODEL)
        inp = {'queries': jax.random.normal(ks[0], (B, NQ, D_MODEL), dtype=jnp.float32), 'context': jax.random.normal(ks[1], (B, S, D_MODEL), dtype=jnp.float32), 'wq': jax.random.normal(ks[2], (D_MODEL, D_MODEL), dtype=jnp.float32) * inv, 'bq': jnp.zeros((D_MODEL,), dtype=jnp.float32), 'wk': jax.random.normal(ks[3], (D_MODEL, D_MODEL), dtype=jnp.float32) * inv, 'bk': jnp.zeros((D_MODEL,), dtype=jnp.float32), 'wv': jax.random.normal(ks[4], (D_MODEL, D_MODEL), dtype=jnp.float32) * inv, 'bv': jnp.zeros((D_MODEL,), dtype=jnp.float32), 'wo': jax.random.normal(ks[5], (D_MODEL, D_MODEL), dtype=jnp.float32) * inv, 'bo': jnp.zeros((D_MODEL,), dtype=jnp.float32)}
        return inp
    _L0_xattn_all = _L0_xattn_setup()
    _L0_xattn_in = {k: v for k, v in _L0_xattn_all.items() if k in ('wq', 'bq', 'wk', 'bk', 'wv', 'bv', 'wo', 'bo')}
    del _L0_xattn_all

    def _L0_attn_setup():
        import jax, jax.numpy as jnp
        import numpy as np
        B_, L_, DM, DS, DFF = (2, 512, 512, 16, 2048)
        DI = 2 * DM
        DTR = (DM + 15) // 16
        K = 4

        def _rmsnorm(x, w, eps=1e-06):
            return x * jax.lax.rsqrt(jnp.mean(x * x, axis=-1, keepdims=True) + eps) * w

        def _causal_dw_conv(x, w, b):
            xp = jnp.pad(x, ((0, 0), (K - 1, 0), (0, 0)))
            out = jax.lax.conv_general_dilated(xp.transpose(0, 2, 1), w[:, None, :], window_strides=(1,), padding='VALID', dimension_numbers=('NCL', 'OIL', 'NCL'), feature_group_count=x.shape[-1])
            return out.transpose(0, 2, 1) + b

        def _mamba(Z, in_proj_w, conv_w, conv_b, x_proj_w, dt_proj_w, dt_proj_b, A_log, D, out_proj_w):
            xz = jnp.einsum('bld,ed->ble', Z, in_proj_w)
            x, z = jnp.split(xz, 2, axis=-1)
            x = jax.nn.silu(_causal_dw_conv(x, conv_w, conv_b))
            x_dbl = jnp.einsum('bld,ed->ble', x, x_proj_w)
            dt, Bm, Cm = jnp.split(x_dbl, [DTR, DTR + DS], axis=-1)
            dt = jax.nn.softplus(jnp.einsum('blr,dr->bld', dt, dt_proj_w) + dt_proj_b)
            A = -jnp.exp(A_log)
            deltaA = jnp.exp(dt[..., None] * A)
            deltaBx = dt[..., None] * Bm[:, :, None, :] * x[..., None]

            def step(h, xs):
                dA, dBx, C = xs
                h = dA * h + dBx
                y = jnp.einsum('bdn,bn->bd', h, C)
                return (h, y)
            h0 = jnp.zeros((Z.shape[0], DI, DS), Z.dtype)
            xs = (deltaA.transpose(1, 0, 2, 3), deltaBx.transpose(1, 0, 2, 3), Cm.transpose(1, 0, 2))
            _, ys = jax.lax.scan(step, h0, xs)
            y = ys.transpose(1, 0, 2) + x * D
            y = y * jax.nn.silu(z)
            return jnp.einsum('bld,ed->ble', y, out_proj_w)
        key = jax.random.key(seed)
        ks = jax.random.split(key, 12)
        r = lambda k, s: jax.random.normal(k, s, dtype=jnp.float32) * 0.02
        return {'Z': jax.random.normal(ks[0], (B_, L_, DM), dtype=jnp.float32), 'in_proj_w': r(ks[1], (2 * DI, DM)), 'conv_w': r(ks[2], (DI, K)), 'conv_b': jnp.zeros((DI,), jnp.float32), 'x_proj_w': r(ks[3], (DTR + 2 * DS, DI)), 'dt_proj_w': r(ks[4], (DI, DTR)), 'dt_proj_b': jax.random.uniform(ks[5], (DI,), jnp.float32, -4.0, -2.0), 'A_log': jnp.log(jnp.tile(jnp.arange(1, DS + 1, dtype=jnp.float32), (DI, 1))), 'D': jnp.ones((DI,), jnp.float32), 'out_proj_w': r(ks[6], (DM, DI)), 'mlp_w1': r(ks[7], (DFF, DM)), 'mlp_b1': jnp.zeros((DFF,), jnp.float32), 'mlp_w2': r(ks[8], (DM, DFF)), 'mlp_b2': jnp.zeros((DM,), jnp.float32), 'norm1_w': jnp.ones((DM,), jnp.float32)}
    _L0_attn_all = _L0_attn_setup()
    _L0_attn_in = {k: v for k, v in _L0_attn_all.items() if k in ('in_proj_w', 'conv_w', 'conv_b', 'x_proj_w', 'dt_proj_w', 'dt_proj_b', 'A_log', 'D', 'out_proj_w', 'mlp_w1', 'mlp_b1', 'mlp_w2', 'mlp_b2', 'norm1_w')}
    del _L0_attn_all

    def _L0_ffn_setup():
        import jax, jax.numpy as jnp
        import numpy as np
        E = 8
        K = 2
        D = 512
        B, N = (4, 2048)
        DC = 256
        key = jax.random.key(seed)
        ks = jax.random.split(key, 6)
        x = jax.random.normal(ks[0], (B, N, D), jnp.float32)
        cond = jax.random.normal(ks[1], (B, N, DC), jnp.float32)
        mask = jnp.ones((B, N), jnp.float32)
        W_shared = jax.random.normal(ks[2], (D, D), jnp.float32) * 0.02
        W_expert = jax.random.normal(ks[3], (D, D), jnp.float32) * 0.02
        W_gate = jax.random.normal(ks[4], (D, E - 1), jnp.float32) * 0.02
        bias = jnp.zeros((D,), jnp.float32)
        return dict(x=x, cond=cond, mask=mask, W_shared=W_shared, W_expert=W_expert, W_gate=W_gate, bias=bias)
    _L0_ffn_all = _L0_ffn_setup()
    _L0_ffn_in = {k: v for k, v in _L0_ffn_all.items() if k in ('cond', 'mask', 'W_shared', 'W_expert', 'W_gate', 'bias')}
    del _L0_ffn_all
    return {'x': x, 'ctx_1024': ctx_1024, 'L0_xattn_wq': _L0_xattn_in['wq'], 'L0_xattn_bq': _L0_xattn_in['bq'], 'L0_xattn_wk': _L0_xattn_in['wk'], 'L0_xattn_bk': _L0_xattn_in['bk'], 'L0_xattn_wv': _L0_xattn_in['wv'], 'L0_xattn_bv': _L0_xattn_in['bv'], 'L0_xattn_wo': _L0_xattn_in['wo'], 'L0_xattn_bo': _L0_xattn_in['bo'], 'L0_attn_in_proj_w': _L0_attn_in['in_proj_w'], 'L0_attn_conv_w': _L0_attn_in['conv_w'], 'L0_attn_conv_b': _L0_attn_in['conv_b'], 'L0_attn_x_proj_w': _L0_attn_in['x_proj_w'], 'L0_attn_dt_proj_w': _L0_attn_in['dt_proj_w'], 'L0_attn_dt_proj_b': _L0_attn_in['dt_proj_b'], 'L0_attn_A_log': _L0_attn_in['A_log'], 'L0_attn_D': _L0_attn_in['D'], 'L0_attn_out_proj_w': _L0_attn_in['out_proj_w'], 'L0_attn_mlp_w1': _L0_attn_in['mlp_w1'], 'L0_attn_mlp_b1': _L0_attn_in['mlp_b1'], 'L0_attn_mlp_w2': _L0_attn_in['mlp_w2'], 'L0_attn_mlp_b2': _L0_attn_in['mlp_b2'], 'L0_attn_norm1_w': _L0_attn_in['norm1_w'], 'L0_ffn_cond': _L0_ffn_in['cond'], 'L0_ffn_mask': _L0_ffn_in['mask'], 'L0_ffn_W_shared': _L0_ffn_in['W_shared'], 'L0_ffn_W_expert': _L0_ffn_in['W_expert'], 'L0_ffn_W_gate': _L0_ffn_in['W_gate'], 'L0_ffn_bias': _L0_ffn_in['bias']}

def reference(x, ctx_1024, L0_xattn_wq, L0_xattn_bq, L0_xattn_wk, L0_xattn_bk, L0_xattn_wv, L0_xattn_bv, L0_xattn_wo, L0_xattn_bo, L0_attn_in_proj_w, L0_attn_conv_w, L0_attn_conv_b, L0_attn_x_proj_w, L0_attn_dt_proj_w, L0_attn_dt_proj_b, L0_attn_A_log, L0_attn_D, L0_attn_out_proj_w, L0_attn_mlp_w1, L0_attn_mlp_b1, L0_attn_mlp_w2, L0_attn_mlp_b2, L0_attn_norm1_w, L0_ffn_cond, L0_ffn_mask, L0_ffn_W_shared, L0_ffn_W_expert, L0_ffn_W_gate, L0_ffn_bias):
    import jax
    import jax.numpy as jnp

    def _L0_xattn_ref(queries, context, wq, bq, wk, bk, wv, bv, wo, bo):
        import jax, jax.numpy as jnp
        import numpy as np
        D_MODEL = 512
        N_HEADS = 16
        HEAD_DIM = D_MODEL // N_HEADS
        B, NQ, D = queries.shape
        S = context.shape[1]
        H, HD = (N_HEADS, HEAD_DIM)
        scale = HD ** (-0.5)
        q = queries @ wq.T + bq
        k = context @ wk.T + bk
        v = context @ wv.T + bv
        q = q.reshape(B, NQ, H, HD).transpose(0, 2, 1, 3)
        k = k.reshape(B, S, H, HD).transpose(0, 2, 1, 3)
        v = v.reshape(B, S, H, HD).transpose(0, 2, 1, 3)
        attn = jnp.einsum('bhnd,bhsd->bhns', q, k) * scale
        attn = jax.nn.softmax(attn, axis=-1)
        out = jnp.einsum('bhns,bhsd->bhnd', attn, v)
        out = out.transpose(0, 2, 1, 3).reshape(B, NQ, D)
        return out @ wo.T + bo

    def _L0_attn_ref(Z, in_proj_w, conv_w, conv_b, x_proj_w, dt_proj_w, dt_proj_b, A_log, D, out_proj_w, mlp_w1, mlp_b1, mlp_w2, mlp_b2, norm1_w):
        import jax, jax.numpy as jnp
        import numpy as np
        B_, L_, DM, DS, DFF = (2, 512, 512, 16, 2048)
        DI = 2 * DM
        DTR = (DM + 15) // 16
        K = 4

        def _rmsnorm(x, w, eps=1e-06):
            return x * jax.lax.rsqrt(jnp.mean(x * x, axis=-1, keepdims=True) + eps) * w

        def _causal_dw_conv(x, w, b):
            xp = jnp.pad(x, ((0, 0), (K - 1, 0), (0, 0)))
            out = jax.lax.conv_general_dilated(xp.transpose(0, 2, 1), w[:, None, :], window_strides=(1,), padding='VALID', dimension_numbers=('NCL', 'OIL', 'NCL'), feature_group_count=x.shape[-1])
            return out.transpose(0, 2, 1) + b

        def _mamba(Z, in_proj_w, conv_w, conv_b, x_proj_w, dt_proj_w, dt_proj_b, A_log, D, out_proj_w):
            xz = jnp.einsum('bld,ed->ble', Z, in_proj_w)
            x, z = jnp.split(xz, 2, axis=-1)
            x = jax.nn.silu(_causal_dw_conv(x, conv_w, conv_b))
            x_dbl = jnp.einsum('bld,ed->ble', x, x_proj_w)
            dt, Bm, Cm = jnp.split(x_dbl, [DTR, DTR + DS], axis=-1)
            dt = jax.nn.softplus(jnp.einsum('blr,dr->bld', dt, dt_proj_w) + dt_proj_b)
            A = -jnp.exp(A_log)
            deltaA = jnp.exp(dt[..., None] * A)
            deltaBx = dt[..., None] * Bm[:, :, None, :] * x[..., None]

            def step(h, xs):
                dA, dBx, C = xs
                h = dA * h + dBx
                y = jnp.einsum('bdn,bn->bd', h, C)
                return (h, y)
            h0 = jnp.zeros((Z.shape[0], DI, DS), Z.dtype)
            xs = (deltaA.transpose(1, 0, 2, 3), deltaBx.transpose(1, 0, 2, 3), Cm.transpose(1, 0, 2))
            _, ys = jax.lax.scan(step, h0, xs)
            y = ys.transpose(1, 0, 2) + x * D
            y = y * jax.nn.silu(z)
            return jnp.einsum('bld,ed->ble', y, out_proj_w)
        y = _mamba(Z, in_proj_w, conv_w, conv_b, x_proj_w, dt_proj_w, dt_proj_b, A_log, D, out_proj_w)
        Z_mam = _rmsnorm(y + Z, norm1_w)
        h = jax.nn.gelu(jnp.einsum('bld,fd->blf', Z_mam, mlp_w1) + mlp_b1, approximate=False)
        mlp = jnp.einsum('blf,df->bld', h, mlp_w2) + mlp_b2
        return _rmsnorm(mlp + Z_mam, norm1_w)

    def _L0_ffn_ref(x, cond, mask, W_shared, W_expert, W_gate, bias):
        import jax, jax.numpy as jnp
        import numpy as np
        E = 8
        K = 2
        D = 512
        B, N = (4, 2048)
        DC = 256
        b, n, d = x.shape
        T = b * n
        xf = x.reshape(T, d)
        scores = jax.nn.softmax(xf @ W_gate, axis=-1)
        expert_weights, _ = jax.lax.top_k(scores, K)
        expert_weights = expert_weights / expert_weights.sum(-1, keepdims=True)
        expert_indices = (jnp.arange(T * K) % E).reshape(T, K)
        te = expert_indices.reshape(-1)
        w = expert_weights.reshape(-1)
        capacity = K * T // E
        order = jnp.argsort(te, stable=True)
        sorted_e = te[order]
        hist = jnp.bincount(te, length=E)
        starts = jnp.concatenate([jnp.zeros((1,), hist.dtype), jnp.cumsum(hist)[:-1]])
        pos = jnp.arange(T * K) - starts[sorted_e]
        valid = pos < capacity
        dest = jnp.where(valid, sorted_e * capacity + pos, E * capacity)
        tok = order // K
        gathered = jnp.zeros((E * capacity + 1, d), x.dtype).at[dest].set(xf[tok])
        gathered = gathered[:-1]
        y = gathered @ W_expert.T
        contrib = w[order][:, None] * y[jnp.minimum(dest, E * capacity - 1)]
        moe_out = jnp.zeros((T, d), x.dtype).at[tok].add(jnp.where(valid[:, None], contrib, 0.0))
        shared = xf @ W_shared.T
        out = (shared + moe_out + bias).reshape(b, n, d)
        return out
    x = x + _L0_xattn_ref(_layernorm(x, axis=-1), ctx_1024, L0_xattn_wq, L0_xattn_bq, L0_xattn_wk, L0_xattn_bk, L0_xattn_wv, L0_xattn_bv, L0_xattn_wo, L0_xattn_bo)
    x = x + _L0_attn_ref(_layernorm(x, axis=-1), L0_attn_in_proj_w, L0_attn_conv_w, L0_attn_conv_b, L0_attn_x_proj_w, L0_attn_dt_proj_w, L0_attn_dt_proj_b, L0_attn_A_log, L0_attn_D, L0_attn_out_proj_w, L0_attn_mlp_w1, L0_attn_mlp_b1, L0_attn_mlp_w2, L0_attn_mlp_b2, L0_attn_norm1_w)
    x = x + _L0_ffn_ref(_layernorm(x, axis=-1), L0_ffn_cond, L0_ffn_mask, L0_ffn_W_shared, L0_ffn_W_expert, L0_ffn_W_gate, L0_ffn_bias)
    return x

_drawn_inputs = setup_inputs


def setup_inputs(seed=0):
    import zlib

    import numpy as np

    out = dict(_drawn_inputs(seed))
    spreads = {'L0_xattn_bq': (0.0, 0.451),
     'L0_xattn_bk': (0.0, 0.8),
     'L0_xattn_bv': (0.0, 0.1),
     'L0_xattn_bo': (0.0, 0.1),
     'L0_attn_conv_b': (0.0, 0.8),
     'L0_attn_D': (1.0, 0.6),
     'L0_attn_mlp_b1': (0.0, 0.357),
     'L0_attn_mlp_b2': (0.0, 0.1),
     'L0_attn_norm1_w': (1.0, 0.2),
     'L0_ffn_bias': (0.0, 0.1)}
    factors = {'L0_attn_in_proj_w': 8.0,
     'L0_attn_conv_w': 8.0,
     'L0_attn_x_proj_w': 8.0,
     'L0_attn_dt_proj_w': 8.0,
     'L0_attn_dt_proj_b': 8.0,
     'L0_attn_A_log': 8.0,
     'L0_attn_out_proj_w': 8.0,
     'L0_ffn_W_gate': 8.0}
    for name, (base, spread) in spreads.items():
        noise = np.random.default_rng([zlib.crc32(name.encode()), seed]).standard_normal(out[name].shape)
        drawn = base * np.exp(spread * noise) if base else spread * noise
        out[name] = jnp.asarray(drawn.astype(out[name].dtype))
    for name, factor in factors.items():
        out[name] = (out[name] * factor).astype(out[name].dtype)
    return out
```

```python
from contextlib import ExitStack

import numpy as np

import concourse.bass as bass
from concourse import mybir

F32 = mybir.dt.float32
F32R = mybir.dt.float32r
ALU = mybir.AluOpType
ACT = mybir.ActivationFunctionType
AX = mybir.AxisListType

P = 128
LN_EPS = 1e-5
RMS_EPS = 1e-6


class Chain:

    def __init__(self, eng, sem):
        self.eng, self.sem, self.base, self.n = eng, sem, 0, 0

    def __call__(self, ins):
        self.n += 1
        ins.then_inc(self.sem, 1)
        self.eng.wait_ge(self.sem, self.base + self.n)

    def enter(self, i, per_iteration, before):
        self.base, self.n = i * per_iteration + before, 0

    def leave(self, per_iteration, iterations, before):
        assert self.n == per_iteration, (self.n, per_iteration)
        self.base, self.n = 0, before + per_iteration * iterations


def project_queries(nc, x, wq_t, bq, q_dram):
    batches, _, width = x.shape
    chunks = width // P
    group = 4
    steps = batches // group
    T = group * P

    with ExitStack() as ctx:
        def sb(name, shape, dt=F32):
            return ctx.enter_context(nc.sbuf_tensor(name, shape, dt))

        def sem(name):
            return ctx.enter_context(nc.semaphore(name))

        wq = sb("wq_sb", [P, chunks, width])
        bq_sb = sb("bq_sb", [P, chunks])
        ident = sb("q_ident", [P, P])
        eps = sb("q_eps", [P, 1])
        wait_taker = sb("q_wait_taker", [P, 1])
        x_sb = sb("q_x", [P, group, width])
        xn = sb("q_xn", [P, group, width])
        xn_t = sb("q_xn_t", [P, chunks, T])
        q_sb = sb("q_out", [P, group, chunks, P])
        stats = sb("q_stats", [P, group, 6])
        moments = sb("q_moments", [P, group, 2])
        std = sb("q_std", [P, group])
        rstd = sb("q_rstd", [P, group])
        turned_ps = ctx.enter_context(nc.psum_tensor("q_turned_ps", [P, 2, T], F32))
        q_ps = ctx.enter_context(nc.psum_tensor("q_ps", [P, 2, T], F32))

        weights_loaded, x_loaded = sem("q_weights_loaded"), sem("q_x_loaded")
        ident_ready, moments_ready, std_ready = sem("q_ident_ready"), sem("q_moments_ready"), sem("q_std_ready")
        xn_ready, turned, xn_t_ready = sem("q_xn_ready"), sem("q_turned"), sem("q_xn_t_ready")
        product_ready, q_ready = sem("q_product_ready"), sem("q_ready")
        q_stored = sem("q_stored")
        dve_order = sem("q_dve_order")

        block = ctx.enter_context(nc.Block())
        x_v = x.rearrange("(s b) t d -> s t b d", b=group)
        q_v = q_dram.rearrange("(s b) p g t -> s p b g t", b=group)

        @block.sync
        def _(sp):
            sp.sem_inc(q_stored, 16)
            sp.dma_start(x_sb[:], x_v[0]).then_inc(x_loaded, 16)
            sp.dma_start(wq[:], wq_t.rearrange("(k p) o -> p k o", p=P)).then_inc(weights_loaded, 16)
            sp.dma_start(bq_sb[:], bq).then_inc(weights_loaded, 16)

            def step(i, last):
                if not last:
                    sp.wait_ge(xn_ready, i + 1)
                    sp.dma_start(x_sb[:], x_v[i + 1]).then_inc(x_loaded, 16)
                sp.wait_ge(q_ready, (i + 1) * chunks)
                sp.dma_start(q_v[i], q_sb[:]).then_inc(q_stored, 16)

            with sp.Fori(0, steps - 1) as i:
                step(i, False)
            step(steps - 1, True)
            sp.wait_ge(q_stored, 16 * (steps + 1))

        @block.gpsimd
        def _(pool):
            pool.memset(ident[:], 0.0).then_inc(ident_ready, 1)
            pool.memset(eps[:], LN_EPS).then_inc(ident_ready, 1)
            pool.wait_ge(ident_ready, 2)
            pool.affine_select(out=ident[:], in_=ident[:], compare_op=ALU.not_equal, fill=1.0, base=0,
                               pattern=[[-1, P]], channel_multiplier=1).then_inc(ident_ready, 1)

        @block.vector
        def _(dve):
            chain = Chain(dve, dve_order)

            with dve.Fori(0, steps) as i:
                chain.enter(i, 2, 0)
                dve.wait_ge(x_loaded, i * 16 + 16)
                for b in range(group):
                    ins = dve.bn_stats(stats[:, b, :], x_sb[:, b, :])
                chain(ins)
                dve.memset(wait_taker[:], 0.0)
                for b in range(group):
                    ins = dve.bn_aggr(moments[:, b, :], stats[:, b, :])
                ins.then_inc(moments_ready, 1)
                dve.wait_ge(std_ready, i + 1)
                chain(dve.reciprocal(rstd[:], std[:]))
                for b in range(group):
                    ins = dve.tensor_scalar(xn[:, b, :], x_sb[:, b, :], moments[:, b, 0:1], rstd[:, b:b + 1],
                                            ALU.subtract, ALU.mult)
                ins.then_inc(xn_ready, 1)
            chain.leave(2, steps, 0)

        @block.scalar
        def _(act):
            act.wait_ge(ident_ready, 3)
            act.wait_ge(weights_loaded, 32)
            with act.Fori(0, steps) as i:
                act.wait_ge(moments_ready, i + 1)
                act.activation(std[:], moments[:, :, 1], ACT.Sqrt, bias=eps[:, 0:1]).then_inc(std_ready, 1)
                for b in range(group):
                    act.wait_ge(turned, i * group + b + 1)
                    act.copy(xn_t[:, :, b * P:(b + 1) * P],
                             turned_ps[:, b % 2, :].rearrange("p (k t) -> p k t", t=P)).then_inc(xn_t_ready, 1)
                act.wait_ge(q_stored, i * 16 + 16)
                for g in range(chunks):
                    act.wait_ge(product_ready, i * chunks + g + 1)
                    act.activation(q_sb[:, :, g, :], q_ps[:, g % 2, :].rearrange("p (b t) -> p b t", t=P),
                                   ACT.Identity, bias=bq_sb[:, g:g + 1]).then_inc(q_ready, 1)

        @block.tensor
        def _(pe):
            pe.wait_ge(ident_ready, 3)
            pe.wait_ge(weights_loaded, 32)
            pe.sem_inc(xn_t_ready, 2)
            with pe.Fori(0, steps) as i:
                pe.wait_ge(xn_ready, i + 1)
                for b in range(group):
                    pe.wait_ge(xn_t_ready, i * group + b + 1)
                    for k in range(chunks):
                        ins = pe.transpose(turned_ps[:, b % 2, k * P:(k + 1) * P],
                                           xn[:, b, k * P:(k + 1) * P], ident[:])
                    ins.then_inc(turned, 1)
                pe.wait_ge(xn_t_ready, (i + 1) * group + 2)
                for g in range(chunks):
                    if g >= 2:
                        pe.wait_ge(q_ready, i * chunks + g - 1)
                    for k in range(chunks):
                        ins = pe.matmul(q_ps[:, g % 2, :], wq[:, k, g * P:(g + 1) * P], xn_t[:, k, :],
                                        start=(k == 0), stop=(k == chunks - 1))
                    ins.then_inc(product_ready, 1)


def cross_attention(nc, ctx_t, wk_t, wv_t, bk, bv, q_dram, attn_dram, heads):
    batches, width, keys = ctx_t.shape
    chunks = width // P
    block_keys = 512
    blocks = keys // block_keys
    per_block = block_keys // P
    tiles = keys // P
    hd = width // heads
    row_tiles = P // hd
    scale = float(hd) ** -0.5
    queries = P
    assert heads == chunks * row_tiles and per_block == chunks and row_tiles == 4
    QW = chunks * queries

    k_per_batch = blocks * chunks
    max_units = blocks * chunks * 2
    exp_units = tiles * 2

    with ExitStack() as ctx:
        def sb(name, shape, dt=F32):
            return ctx.enter_context(nc.sbuf_tensor(name, shape, dt))

        def sem(name):
            return ctx.enter_context(nc.semaphore(name))

        wk_hi, wk_lo = sb("wk_hi", [P, chunks, width], F32R), sb("wk_lo", [P, chunks, width], F32R)
        wv_hi, wv_lo = sb("wv_hi", [P, chunks, width], F32R), sb("wv_lo", [P, chunks, width], F32R)
        c_raw = sb("c_raw", [P, chunks, block_keys])
        c_hi = sb("c_hi", [P, 2, chunks, block_keys], F32R)
        c_lo = sb("c_lo", [P, 2, chunks, block_keys], F32R)
        k_hi, k_lo = sb("k_hi", [P, chunks, keys], F32R), sb("k_lo", [P, chunks, keys], F32R)
        v_sb = sb("v_sb", [P, tiles, width])
        probs = sb("probs", [P, 2, 2, QW])
        prob_sums = sb("prob_sums", [P, chunks, QW])
        q_raw = prob_sums[:, 0, :].rearrange("p (g q) -> p g q", q=queries)
        q_hi, q_lo = sb("q_hi", [P, chunks, QW], F32R), sb("q_lo", [P, chunks, QW], F32R)
        max_parts = sb("max_parts", [P, row_tiles, chunks, blocks])
        neg_max_pad = sb("neg_max_pad", [P, chunks * row_tiles, hd])
        neg_max = sb("neg_max", [P, QW], F32R)
        out_sb = sb("attn_out_sb", [P, chunks, queries])
        ident = sb("a_ident", [P, P])
        ident_r = sb("ident_r", [P, P], F32R)
        ones_f = sb("ones_f", [P, hd])
        bk_sb, bv_sb = sb("bk_sb", [P, chunks]), sb("bv_sb", [P, chunks])

        scores = ctx.enter_context(nc.psum_tensor("scores", [P, chunks, QW], F32))
        proj = ctx.enter_context(nc.psum_tensor("proj", [P, 2, 512], F32))
        o_acc = ctx.enter_context(nc.psum_tensor("o_acc", [P, QW], F32))
        misc = ctx.enter_context(nc.psum_tensor("misc", [P, QW], F32))

        weights_loaded, bias_loaded = sem("a_weights_loaded"), sem("a_bias_loaded")
        weights_split, ident_ready = sem("a_weights_split"), sem("a_ident_ready")
        ctx_loaded = sem("ctx_loaded")
        q_loaded, q_split = sem("q_loaded"), sem("q_split")
        c_hi_ready, c_lo_ready = sem("c_hi_ready"), sem("c_lo_ready")
        proj_ready = sem("proj_ready")
        k_hi_ready, k_lo_ready = sem("k_hi_ready"), sem("k_lo_ready")
        v_ready = sem("v_ready")
        max_scores = sem("max_scores")
        max_taken = sem("max_taken")
        pad_ready, pad_turned, neg_max_ready = sem("pad_ready"), sem("pad_turned"), sem("neg_max_ready")
        scores_ready = sem("scores_ready")
        exp_done = sem("exp_done")
        pv_done = sem("pv_done")
        summed = sem("summed")
        den_ready, attn_ready = sem("den_ready"), sem("attn_ready")
        attn_stored = sem("attn_stored")
        dve_order = sem("a_dve_order")

        block = ctx.enter_context(nc.Block())
        ctx_v = ctx_t.rearrange("b (k p) s -> b p k s", p=P)

        @block.sync
        def _(sp):
            sp.sem_inc(attn_stored, 16)
            for n, w in enumerate((wk_t, wv_t)):
                sp.dma_start(v_sb[:, n * chunks:(n + 1) * chunks, :],
                             w.rearrange("(k p) o -> p k o", p=P)).then_inc(weights_loaded, 16)
            sp.dma_start(q_raw, q_dram[0]).then_inc(q_loaded, 16)
            sp.dma_start(bk_sb[:], bk).then_inc(bias_loaded, 16)
            sp.dma_start(bv_sb[:], bv).then_inc(bias_loaded, 16)

            def load(b, s):
                sp.dma_start(c_raw[:], ctx_v[b, :, :, s * block_keys:(s + 1) * block_keys]
                             ).then_inc(ctx_loaded, 16)

            load(0, 0)
            sp.wait_ge(c_lo_ready, 1)
            load(0, 1)

            def batch(i, last):
                for s in range(blocks - 2):
                    sp.wait_ge(c_lo_ready, i * blocks + s + 2)
                    load(i, s + 2)
                if not last:
                    for s in range(2):
                        sp.wait_ge(c_lo_ready, i * blocks + blocks + s)
                        load(i + 1, s)
                    sp.wait_ge(den_ready, i + 1)
                    sp.dma_start(q_raw, q_dram[i + 1]).then_inc(q_loaded, 16)
                sp.wait_ge(attn_ready, i + 1)
                sp.dma_start(attn_dram[i], out_sb[:]).then_inc(attn_stored, 16)

            with sp.Fori(0, batches - 1) as i:
                batch(i, False)
            batch(batches - 1, True)
            sp.wait_ge(attn_stored, 16 * (batches + 1))

        @block.gpsimd
        def _(pool):
            pool.memset(ident[:], 0.0).then_inc(ident_ready, 1)
            pool.wait_ge(ident_ready, 1)
            pool.affine_select(out=ident[:], in_=ident[:], compare_op=ALU.not_equal, fill=1.0, base=0,
                               pattern=[[-1, P]], channel_multiplier=1).then_inc(ident_ready, 1)
            pool.memset(neg_max_pad[:], 0.0).then_inc(ident_ready, 1)
            pool.memset(ones_f[:], 1.0).then_inc(ident_ready, 1)

            def low_part(n, s, block_before=None):
                pool.wait_ge(ctx_loaded, (n + 1) * 16)
                pool.wait_ge(c_hi_ready, n + 1)
                if block_before is not None:
                    pool.wait_ge(proj_ready, (block_before + 1) * 2 * chunks)
                pool.tensor_tensor(c_lo[:, s % 2], c_raw[:], c_hi[:, s % 2].bitcast(F32),
                                   ALU.subtract).then_inc(c_lo_ready, 1)

            low_part(0, 0)
            low_part(1, 1)

            def batch(i, last):
                for s in range(blocks if not last else blocks - 2):
                    low_part(i * blocks + s + 2, s, i * blocks + s)

            with pool.Fori(0, batches - 1) as i:
                batch(i, False)
            batch(batches - 1, True)

        @block.scalar
        def _(act):
            act.sem_inc(exp_done, 2)
            act.sem_inc(v_ready, chunks)
            act.wait_ge(bias_loaded, 32)

            def batch(i):
                for s in range(blocks):
                    n = i * blocks + s
                    for g in range(chunks):
                        act.wait_ge(proj_ready, n * 2 * chunks + g + 1)
                        act.activation(k_hi[:, g, s * block_keys:(s + 1) * block_keys], proj[:, g % 2, :],
                                       ACT.Identity, bias=bk_sb[:, g:g + 1]).then_inc(k_hi_ready, 1)
                    for r in range(per_block):
                        act.wait_ge(proj_ready, n * 2 * chunks + chunks + r + 1)
                        act.copy(v_sb[:, s * per_block + r, :], proj[:, r % 2, :]).then_inc(v_ready, 1)
                for u in range(exp_units):
                    pair = u % 2
                    act.wait_ge(scores_ready, i * exp_units + u + 1)
                    act.wait_ge(pv_done, i * exp_units + u + 1)
                    act.wait_ge(summed, i * exp_units + u + 1)
                    act.activation(probs[:, pair], scores[:, 2 * pair:2 * pair + 2, :], ACT.Exp,
                                   scale=scale).then_inc(exp_done, 1)

            with act.Fori(0, batches) as i:
                batch(i)

        @block.vector
        def _(dve):
            chain = Chain(dve, dve_order)
            dve.sem_inc(max_taken, 2)
            dve.sem_inc(summed, 2)
            dve.wait_ge(ident_ready, 4)
            dve.tensor_copy(ident_r[:], ident[:])
            dve.memset(q_hi[:].bitcast(mybir.dt.uint32), 0)
            dve.memset(q_lo[:].bitcast(mybir.dt.uint32), 0).then_inc(weights_split, 1)
            dve.wait_ge(weights_loaded, 32)
            for n, (hi, lo) in enumerate(((wk_hi, wk_lo), (wv_hi, wv_lo))):
                raw = v_sb[:, n * chunks:(n + 1) * chunks, :]
                chain(dve.tensor_copy(hi[:], raw))
                dve.tensor_tensor(lo[:], raw, hi[:].bitcast(F32), ALU.subtract).then_inc(weights_split, 1)

            def high_part(n, s, block_before=None):
                dve.wait_ge(ctx_loaded, (n + 1) * 16)
                if block_before is not None:
                    dve.wait_ge(proj_ready, (block_before + 1) * 2 * chunks)
                dve.tensor_copy(c_hi[:, s % 2], c_raw[:]).then_inc(c_hi_ready, 1)

            high_part(0, 0)
            high_part(1, 1)

            def batch(i, last):
                dve.wait_ge(q_loaded, i * 16 + 16)
                diagonal = [(slice(j * hd, (j + 1) * hd), slice(j * queries, (j + 1) * queries))
                            for j in range(row_tiles)]
                for js, qs in diagonal:
                    ins = dve.tensor_copy(q_hi[js, :, qs], q_raw[js])
                ins.then_inc(q_split, 1)
                dve.wait_ge(q_split, i * 2 + 1)
                for js, qs in diagonal:
                    ins = dve.tensor_tensor(q_lo[js, :, qs], q_raw[js], q_hi[js, :, qs].bitcast(F32),
                                            ALU.subtract)
                ins.then_inc(q_split, 1)
                for s in range(blocks):
                    n = i * blocks + s
                    cols = slice(s * block_keys, (s + 1) * block_keys)
                    for g in range(chunks):
                        dve.wait_ge(k_hi_ready, n * chunks + g + 1)
                        dve.scalar_tensor_tensor(k_lo[:, g, cols], proj[:, g % 2, :], bk_sb[:, g:g + 1],
                                                 k_hi[:, g, cols].bitcast(F32), ALU.add,
                                                 ALU.subtract).then_inc(k_lo_ready, 1)
                    for g in range(chunks):
                        for pair in range(2):
                            u = (s * chunks + g) * 2 + pair
                            dve.wait_ge(max_scores, i * max_units + u + 1)
                            dve.tensor_reduce(max_parts[:, 2 * pair:2 * pair + 2, g, s],
                                              scores[:, 2 * pair:2 * pair + 2, :], AX.X,
                                              ALU.max).then_inc(max_taken, 1)
                    if s < blocks - 2 or not last:
                        high_part(n + 2, s, n)
                dve.wait_ge(max_taken, (i + 1) * max_units + 2)
                dve.tensor_reduce(neg_max_pad[:, :, 0], max_parts[:].rearrange("p j g s -> p (j g) s"),
                                  AX.X, ALU.max, negate=True).then_inc(pad_ready, 1)
                dve.wait_ge(pad_turned, i + 1)
                dve.tensor_copy(neg_max[:], misc[:]).then_inc(neg_max_ready, 1)
                for u in range(exp_units):
                    t, pair = u // 2, u % 2
                    part = prob_sums[:, 2 * pair:2 * pair + 2, :]
                    new = probs[:, pair]
                    dve.wait_ge(exp_done, i * exp_units + u + 1 + 2)
                    if t == 0:
                        dve.tensor_copy(part, new).then_inc(summed, 1)
                    else:
                        dve.wait_ge(summed, i * exp_units + u - 1 + 2)
                        dve.tensor_tensor(part, part, new, ALU.add).then_inc(summed, 1)
                dve.wait_ge(den_ready, i + 1)
                dve.wait_ge(attn_stored, (i + 1) * 16)
                chain(dve.reciprocal(out_sb[:], misc[:].rearrange("p (g q) -> p g q", q=queries)))
                chain(dve.tensor_tensor(out_sb[:], o_acc[:].rearrange("p (g q) -> p g q", q=queries),
                                        out_sb[:], ALU.mult))
                dve.tensor_tensor(out_sb[:], out_sb[:], bv_sb[:].unsqueeze(2).to_broadcast([P, chunks, queries]),
                                  ALU.add).then_inc(attn_ready, 1)

            before = chain.n
            with dve.Fori(0, batches - 1) as i:
                chain.enter(i, 2, before)
                batch(i, False)
            chain.leave(2, batches - 1, before)
            batch(batches - 1, True)

        @block.tensor
        def _(pe):
            pe.sem_inc(pv_done, 2)
            pe.wait_ge(ident_ready, 4)
            pe.wait_ge(weights_split, 3)

            def project(out, products):
                steps = [(lhs(k), rhs(k)) for lhs, rhs in products for k in range(chunks)]
                for m, (lhs, rhs) in enumerate(steps):
                    ins = pe.matmul(out, lhs, rhs, start=(m == 0), stop=(m == len(steps) - 1))
                ins.then_inc(proj_ready, 1)

            def batch(i):
                for s in range(blocks):
                    n, slot = i * blocks + s, s % 2
                    pe.wait_ge(c_hi_ready, n + 1)
                    pe.wait_ge(c_lo_ready, n + 1)
                    for g in range(chunks):
                        if g < 2:
                            pe.wait_ge(v_ready, n * chunks + g + 3)
                        else:
                            pe.wait_ge(k_lo_ready, n * chunks + g - 1)
                        gs = slice(g * P, (g + 1) * P)
                        project(proj[:, g % 2, :], [
                            (lambda k: wk_hi[:, k, gs], lambda k: c_hi[:, slot, k, :]),
                            (lambda k: wk_lo[:, k, gs], lambda k: c_hi[:, slot, k, :]),
                            (lambda k: wk_hi[:, k, gs], lambda k: c_lo[:, slot, k, :])])
                    for r in range(per_block):
                        if r < 2:
                            pe.wait_ge(k_lo_ready, n * chunks + r + 3)
                        else:
                            pe.wait_ge(v_ready, n * chunks + r - 1 + chunks)
                        rs = slice(r * P, (r + 1) * P)
                        project(proj[:, r % 2, :], [
                            (lambda k: c_hi[:, slot, k, rs], lambda k: wv_hi[:, k, :]),
                            (lambda k: c_hi[:, slot, k, rs], lambda k: wv_lo[:, k, :]),
                            (lambda k: c_lo[:, slot, k, rs], lambda k: wv_hi[:, k, :])])
                        if s == 0 and r == 0:
                            pe.wait_ge(q_split, i * 2 + 2)
                            pe.wait_ge(exp_done, i * exp_units + 2)
                        for pair in range(2):
                            u = (s * chunks + r) * 2 + pair
                            pe.wait_ge(max_taken, i * max_units + u + 1)
                            for j in (2 * pair, 2 * pair + 1):
                                ins = pe.matmul(scores[:, j, :], q_hi[:, r, j * queries:(j + 1) * queries],
                                                k_hi[:, r, s * block_keys:(s + 1) * block_keys],
                                                start=True, stop=True)
                            ins.then_inc(max_scores, 1)
                pe.wait_ge(pad_ready, i + 1)
                for j in range(row_tiles):
                    ins = pe.transpose(misc[:, j * P:(j + 1) * P],
                                       neg_max_pad[:, j * chunks:(j + 1) * chunks, :].rearrange(
                                           "p g d -> p (g d)"), ident[:])
                ins.then_inc(pad_turned, 1)
                pe.wait_ge(neg_max_ready, i + 1)

                def score_unit(u):
                    t, pair = u // 2, u % 2
                    ts = slice(t * P, (t + 1) * P)
                    pe.wait_ge(exp_done, i * exp_units + u + 1)
                    for g in (2 * pair, 2 * pair + 1):
                        pe.matmul(scores[:, g, :], ident_r[:, g * hd:g * hd + 1].to_broadcast([P, P]),
                                  neg_max[:], start=True, stop=False)
                        for step, (lhs, rhs) in enumerate(((k_hi, q_hi), (k_lo, q_hi), (k_hi, q_lo))):
                            ins = pe.matmul(scores[:, g, :], lhs[:, g, ts], rhs[:, g, :], start=False,
                                            stop=(step == 2))
                    ins.then_inc(scores_ready, 1)

                def values(u):
                    t, pair = u // 2, u % 2
                    pe.wait_ge(exp_done, i * exp_units + u + 1 + 2)
                    for g in (2 * pair, 2 * pair + 1):
                        for j in range(row_tiles):
                            h = g * row_tiles + j
                            ins = pe.matmul(o_acc[j * hd:(j + 1) * hd, g * queries:(g + 1) * queries],
                                            v_sb[:, t, h * hd:(h + 1) * hd],
                                            probs[:, pair, g % 2, j * queries:(j + 1) * queries],
                                            start=(u == 0 and g == 0), stop=(t == tiles - 1),
                                            skip_group_check=True, tile_position=(0, j * hd))
                    ins.then_inc(pv_done, 1)

                for u in range(exp_units):
                    score_unit(u)
                    if u == 1:
                        pe.wait_ge(v_ready, (i + 1) * k_per_batch + chunks)
                    if u >= 1:
                        values(u - 1)
                values(exp_units - 1)
                pe.wait_ge(summed, (i + 1) * exp_units + 2)
                for j in range(row_tiles):
                    ins = pe.matmul(misc[j * hd:(j + 1) * hd, :], ones_f[:],
                                    prob_sums[:, :, j * queries:(j + 1) * queries],
                                    start=True, stop=True, tile_position=(0, j * hd))
                ins.then_inc(den_ready, 1)

            with pe.Fori(0, batches) as i:
                batch(i)


def mamba(nc, x, attn_dram, wo_t, bo, w_in_t, conv_w, conv_b, w_x_t, w_dt_t, dt_b, a_log, d_skip,
          w_out_t, norm_w, x1_dram, zm_dram):
    batches, seq, width = x.shape
    inner = w_out_t.shape[0]
    taps = conv_w.shape[2]
    rank = w_dt_t.shape[0]
    states = a_log.shape[2]
    chunks, inner_chunks = width // P, inner // P
    group = 2
    steps = batches // group
    T = group * seq
    SG = 4
    groups = states // SG
    units = inner_chunks * groups
    pairs = inner_chunks // 2
    bc_rows = 2 * states
    ones_row = rank + bc_rows
    assert seq == P and inner_chunks == 2 * chunks == 8 and rank % 32 == 0

    with ExitStack() as ctx:
        def sb(name, shape, dt=F32):
            return ctx.enter_context(nc.sbuf_tensor(name, shape, dt))

        def psum(name, shape):
            return ctx.enter_context(nc.psum_tensor(name, shape, F32))

        def sem(name):
            return ctx.enter_context(nc.semaphore(name))

        wo = sb("b_wo", [P, chunks, width])
        w_in = sb("b_w_in", [P, chunks, 2 * inner])
        w_x = sb("b_w_x", [P, inner_chunks, rank + bc_rows])
        w_dt = sb("b_w_dt", [ones_row + 1, inner])
        w_out = sb("b_w_out", [P, inner_chunks, width])
        bo_sb, norm_sb = sb("b_bo", [P, width]), sb("b_norm", [P, width])
        conv_w_sb, conv_b_sb = sb("b_conv_w", [P, inner_chunks, taps]), sb("b_conv_b", [P, inner_chunks])
        a_neg, d_sb = sb("b_a", [P, inner_chunks, states]), sb("b_d", [P, inner_chunks])
        ident = sb("b_ident", [P, P])
        eps_ln, eps_rms = sb("b_eps_ln", [P, 1]), sb("b_eps_rms", [P, 1])
        wait_taker = sb("b_wait_taker", [P, 1])

        attn = sb("b_attn", [P, group, chunks, P])
        x_sb = sb("b_x", [P, group, width])
        x1 = sb("b_x1", [P, group, width])
        x_mix = x1
        xn = sb("b_xn", [P, group, width])
        xn_t = sb("b_xn_t", [P, chunks, T])
        padded = sb("b_padded", [P, inner_chunks * group, taps - 1 + seq])
        conv = sb("b_conv", [P, 2, group, seq])
        u = sb("b_u", [P, inner_chunks, T])
        gate = sb("b_gate", [P, inner_chunks, T])
        dbc = sb("b_dbc", [ones_row + 1, T])
        dt = sb("b_dt", [P, inner_chunks, T])
        dt_u = sb("b_dt_u", [P, inner_chunks, T])
        bc = sb("b_bc", [P, bc_rows, T])
        exp_neg = bc[:, 0:inner_chunks, :]
        one_plus = bc[:, inner_chunks:2 * inner_chunks, :]
        decay = sb("b_decay", [P, 2, SG, T])
        drive = sb("b_drive", [P, 3, SG, T])
        state = sb("b_state", [P, SG, T])
        stats, moments = sb("b_stats", [P, group, 6]), sb("b_moments", [P, group, 2])
        std, rstd = sb("b_std", [P, group]), sb("b_rstd", [P, group])
        squares, mean_sq = sb("b_squares", [P, width]), sb("b_mean_sq", [P, group])

        ring = psum("b_ring", [P, 4, 512])
        turned_ps = psum("b_turned", [P, 2, 512])
        y_ps = psum("b_y", [P, 2, 512])

        loaded, ready = sem("b_loaded"), sem("b_ready")
        attn_loaded, x_loaded = sem("b_attn_loaded"), sem("b_x_loaded")
        o_ready = sem("b_o_ready")
        x1_ready, x1_stored = sem("b_x1_ready"), sem("b_x1_stored")
        moments_ready, std_ready, xn_ready = sem("b_moments_ready"), sem("b_std_ready"), sem("b_xn_ready")
        turned, xn_t_ready = sem("b_turned_ready"), sem("b_xn_t_ready")
        in_ready, in_taken = sem("b_in_ready"), sem("b_in_taken")
        conv_ready, u_ready = sem("b_conv_ready"), sem("b_u_ready")
        dbc_product, dbc_ready = sem("b_dbc_product"), sem("b_dbc_ready")
        dt_product = sem("b_dt_product")
        exp_ready, one_plus_ready, log_ready = sem("b_exp_ready"), sem("b_one_plus"), sem("b_log_ready")
        dt_ready, dt_u_ready = sem("b_dt_ready"), sem("b_dt_u_ready")
        bc_product, bc_ready = sem("b_bc_product"), sem("b_bc_ready")
        decay_ready = sem("b_decay_ready")
        drive_ready = sem("b_drive_ready")
        scanned = sem("b_scanned")
        y_part = sem("b_y_part")
        summed = sem("b_summed")
        y_ready = sem("b_y_ready")
        out_ready, sum_ready, squared, rms_ready = (sem("b_out_ready"), sem("b_sum_ready"), sem("b_squared"),
                                                    sem("b_rms_ready"))
        zm_ready, zm_stored = sem("b_zm_ready"), sem("b_zm_stored")
        dve_order = sem("b_dve_order")

        block = ctx.enter_context(nc.Block())
        attn_v = attn_dram.rearrange("(s b) p g t -> s p b g t", b=group)
        x_v, x1_v, zm_v = (t.rearrange("(s b) t d -> s t b d", b=group) for t in (x, x1_dram, zm_dram))

        @block.sync
        def _(sp):
            sp.sem_inc(x1_stored, 16)
            sp.sem_inc(zm_stored, 16)
            sp.dma_start(attn[:], attn_v[0]).then_inc(attn_loaded, 16)
            sp.dma_start(x_sb[:], x_v[0]).then_inc(x_loaded, 16)
            for dst, src in ((wo[:], wo_t.rearrange("(k p) o -> p k o", p=P)),
                             (w_in[:], w_in_t.rearrange("(k p) o -> p k o", p=P)),
                             (w_x[:], w_x_t.rearrange("(k p) o -> p k o", p=P)),
                             (w_out[:], w_out_t.rearrange("(k p) o -> p k o", p=P)),
                             (w_dt[0:rank, :], w_dt_t), (w_dt[ones_row:ones_row + 1, :], dt_b),
                             (bo_sb[:], bo.partition_broadcast(P)), (norm_sb[:], norm_w.partition_broadcast(P)),
                             (conv_w_sb[:], conv_w), (conv_b_sb[:], conv_b), (a_neg[:], a_log), (d_sb[:], d_skip)):
                sp.dma_start(dst, src).then_inc(loaded, 16)

            def step(i, last):
                if not last:
                    sp.wait_ge(o_ready, (i + 1) * group)
                    sp.dma_start(attn[:], attn_v[i + 1]).then_inc(attn_loaded, 16)
                    sp.wait_ge(x1_ready, i + 1)
                    sp.dma_start(x_sb[:], x_v[i + 1]).then_inc(x_loaded, 16)
                sp.wait_ge(x1_ready, i + 1)
                sp.dma_start(x1_v[i], x1[:]).then_inc(x1_stored, 16)
                sp.wait_ge(zm_ready, i + 1)
                sp.dma_start(zm_v[i], xn[:]).then_inc(zm_stored, 16)

            with sp.Fori(0, steps - 1) as i:
                step(i, False)
            step(steps - 1, True)
            sp.wait_ge(x1_stored, 16 * (steps + 1))
            sp.wait_ge(zm_stored, 16 * (steps + 1))

        LOADED = 12 * 16

        @block.gpsimd
        def _(pool):
            pool.memset(w_dt[rank:ones_row, :], 0.0).then_inc(ready, 1)
            pool.memset(dbc[ones_row:ones_row + 1, :], 1.0).then_inc(ready, 1)
            pool.wait_ge(ready, 2)
            pool.memset(padded[:], 0.0).then_inc(ready, 1)
            pool.memset(eps_ln[:], LN_EPS).then_inc(ready, 1)
            pool.memset(eps_rms[:], RMS_EPS).then_inc(ready, 1)
            pool.memset(ident[:], 0.0).then_inc(ready, 1)
            pool.wait_ge(ready, 6)
            pool.affine_select(out=ident[:], in_=ident[:], compare_op=ALU.not_equal, fill=1.0, base=0,
                               pattern=[[-1, P]], channel_multiplier=1).then_inc(ready, 1)
            with pool.Fori(0, steps) as i:
                pool.wait_ge(dt_u_ready, i + 1)
                for m in range(units):
                    c, g = m // groups, m % groups
                    if c == 0:
                        pool.wait_ge(bc_ready, i * states + (g + 1) * SG // 2)
                    pool.wait_ge(summed, i * units + m + 1)
                    pool.tensor_tensor(drive[:, m % 3], dt_u[:, c, :].unsqueeze(1).to_broadcast([P, SG, T]),
                                       bc[:, g * SG:(g + 1) * SG, :], ALU.mult).then_inc(drive_ready, 1)

        @block.scalar
        def _(act):
            act.wait_ge(ready, 7)
            act.wait_ge(loaded, LOADED)
            act.activation(a_neg[:], a_neg[:], ACT.Exp).then_inc(ready, 1)
            act.sem_inc(u_ready, 2)
            with act.Fori(0, steps) as i:
                act.wait_ge(moments_ready, i + 1)
                act.activation(std[:], moments[:, :, 1], ACT.Sqrt, bias=eps_ln[:, 0:1]).then_inc(std_ready, 1)
                for b in range(group):
                    act.wait_ge(turned, i * group + b + 1)
                    act.copy(xn_t[:, :, b * P:(b + 1) * P],
                             turned_ps[:, b, :].rearrange("p (k t) -> p k t", t=P)).then_inc(xn_t_ready, 1)
                for m in range(2 * pairs):
                    act.wait_ge(in_ready, i * 2 * pairs + m + 1)
                    if m < pairs:
                        rows = padded[:, m * 2 * group:(m + 1) * 2 * group, taps - 1:]
                        act.copy(rows, ring[:, m % 4, :].rearrange("p (r t) -> p r t", t=seq)
                                 ).then_inc(in_taken, 1)
                    else:
                        mm = m - pairs
                        act.activation(gate[:, 2 * mm:2 * mm + 2, :],
                                       ring[:, m % 4, :].rearrange("p (c t) -> p c t", t=T),
                                       ACT.Silu).then_inc(in_taken, 1)
                for c in range(inner_chunks):
                    act.wait_ge(conv_ready, i * inner_chunks + c + 1)
                    act.activation(u[:, c, :], conv[:, c % 2].rearrange("p b t -> p (b t)"), ACT.Silu,
                                   bias=conv_b_sb[:, c:c + 1]).then_inc(u_ready, 1)
                act.wait_ge(dbc_product, i + 1)
                act.copy(dbc[0:ones_row, :], turned_ps[0:ones_row, 0, 0:T]).then_inc(dbc_ready, 1)
                act.wait_ge(dt_product, i + 1)
                t_all = ring[:].rearrange("p r (c t) -> p (r c) t", t=T)
                act.activation(exp_neg, t_all, ACT.Abs).then_inc(exp_ready, 1)
                act.wait_ge(exp_ready, 2 * i + 1)
                act.activation(exp_neg, exp_neg, ACT.Exp, scale=-1.0).then_inc(exp_ready, 1)
                act.wait_ge(one_plus_ready, 2 * i + 2)
                act.activation(one_plus, one_plus, ACT.Ln).then_inc(log_ready, 1)
                act.wait_ge(dt_ready, i + 1)
                for m in range(states):
                    act.wait_ge(bc_product, i * states + m + 1)
                    act.copy(bc[:, 2 * m:2 * m + 2, :],
                             ring[:, m % 4, :].rearrange("p (r t) -> p r t", t=T)).then_inc(bc_ready, 1)
                for m in range(units):
                    c, g = m // groups, m % groups
                    act.wait_ge(scanned, i * units + m + 1)
                    for s in range(SG):
                        ins = act.activation(decay[:, m % 2, s, :], dt[:, c, :], ACT.Exp,
                                             scale=a_neg[:, c, g * SG + s:g * SG + s + 1])
                    ins.then_inc(decay_ready, 1)
                for b in range(group):
                    act.wait_ge(sum_ready, i * group + b + 1 + group)
                    act.activation(squares[:], x_mix[:, b, :], ACT.Square, scale=float(width) ** -0.5,
                                   accum_out=mean_sq[:, b:b + 1]).then_inc(squared, 1)
                    act.wait_ge(squared, i * group + b + 1)
                act.activation(std[:], mean_sq[:], ACT.Sqrt, bias=eps_rms[:, 0:1]).then_inc(rms_ready, 1)

        def finish(dve, chain, i, c):
            dve.wait_ge(summed, i * units + (c + 1) * groups + 3)
            chain(dve.scalar_tensor_tensor(u[:, c, :], u[:, c, :], d_sb[:, c:c + 1], y_ps[:, c % 2, 0:T],
                                           ALU.mult, ALU.add))
            dve.tensor_tensor(gate[:, c, :], u[:, c, :], gate[:, c, :], ALU.mult).then_inc(y_ready, 1)

        @block.vector
        def _(dve):
            chain = Chain(dve, dve_order)
            dve.sem_inc(scanned, 2)
            dve.sem_inc(y_ready, 2)
            dve.sem_inc(sum_ready, group)
            dve.wait_ge(ready, 8)
            dve.tensor_scalar(a_neg[:], a_neg[:], -1.0, None, ALU.mult).then_inc(ready, 1)
            dve.wait_ge(loaded, LOADED)
            links = group + 4 + inner_chunks * (taps - 1) + units + inner_chunks
            with dve.Fori(0, steps) as i:
                chain.enter(i, links, 0)
                dve.wait_ge(x_loaded, i * 16 + 16)
                dve.wait_ge(x1_stored, i * 16 + 16)
                for b in range(group):
                    dve.wait_ge(o_ready, i * group + b + 1)
                    ins = dve.tensor_tensor(x1[:, b, :], ring[:, b, :], x_sb[:, b, :], ALU.add)
                    chain(ins)
                dve.tensor_tensor(x1[:], x1[:], bo_sb[:].unsqueeze(1).to_broadcast([P, group, width]),
                                  ALU.add).then_inc(x1_ready, 1)
                dve.wait_ge(x1_ready, i + 1)
                for b in range(group):
                    ins = dve.bn_stats(stats[:, b, :], x1[:, b, :])
                chain(ins)
                dve.memset(wait_taker[:], 0.0)
                for b in range(group):
                    ins = dve.bn_aggr(moments[:, b, :], stats[:, b, :])
                ins.then_inc(moments_ready, 1)
                dve.wait_ge(std_ready, i + 1)
                chain(dve.reciprocal(rstd[:], std[:]))
                dve.wait_ge(zm_stored, i * 16 + 16)
                for b in range(group):
                    ins = dve.tensor_scalar(xn[:, b, :], x1[:, b, :], moments[:, b, 0:1], rstd[:, b:b + 1],
                                            ALU.subtract, ALU.mult)
                ins.then_inc(xn_ready, 1)
                for c in range(inner_chunks):
                    if c % 2 == 0:
                        dve.wait_ge(in_taken, i * 2 * pairs + c // 2 + 1)
                    dve.wait_ge(u_ready, i * inner_chunks + c + 1)
                    rows = padded[:, c * group:(c + 1) * group, :]
                    out = conv[:, c % 2]
                    chain(dve.tensor_scalar(out, rows[:, :, 0:seq], conv_w_sb[:, c, 0:1], None, ALU.mult))
                    for k in range(1, taps):
                        ins = dve.scalar_tensor_tensor(out, rows[:, :, k:k + seq], conv_w_sb[:, c, k:k + 1], out,
                                                       ALU.mult, ALU.add)
                        if k < taps - 1:
                            chain(ins)
                    ins.then_inc(conv_ready, 1)
                dve.wait_ge(exp_ready, 2 * i + 2)
                dve.tensor_scalar(one_plus, exp_neg, 1.0, None, ALU.add).then_inc(one_plus_ready, 1)
                dve.wait_ge(one_plus_ready, 2 * i + 1)
                dve.scalar_tensor_tensor(exp_neg, one_plus, -1.0, exp_neg, ALU.add,
                                         ALU.subtract).then_inc(one_plus_ready, 1)
                dve.wait_ge(log_ready, i + 1)
                t_all = ring[:].rearrange("p r (c t) -> p (r c) t", t=T)
                chain(dve.scalar_tensor_tensor(dt[:], t_all, 0.0, one_plus, ALU.max, ALU.add))
                dve.tensor_tensor(dt[:], dt[:], exp_neg, ALU.subtract).then_inc(dt_ready, 1)
                dve.wait_ge(dt_ready, i + 1)
                dve.tensor_tensor(dt_u[:], dt[:], u[:], ALU.mult).then_inc(dt_u_ready, 1)
                for m in range(units):
                    c, g = m // groups, m % groups
                    dve.wait_ge(decay_ready, i * units + m + 1)
                    starts = decay[:, m % 2].rearrange("p n (b t) -> p (n b) t", t=seq)[:, :, 0]
                    chain(dve.memset(starts, 0.0))
                    dve.wait_ge(drive_ready, i * units + m + 1)
                    dve.tensor_tensor_scan(state[:].rearrange("p n t -> p (n t)"),
                                           decay[:, m % 2].rearrange("p n t -> p (n t)"),
                                           drive[:, m % 3].rearrange("p n t -> p (n t)"),
                                           0.0, ALU.mult, ALU.add).then_inc(scanned, 1)
                    dve.wait_ge(scanned, i * units + m + 1 + 2)
                    if c == 0:
                        dve.wait_ge(bc_ready, i * states + states // 2 + (g + 1) * SG // 2)
                    dve.tensor_tensor(drive[:, m % 3], state[:], bc[:, states + g * SG:states + (g + 1) * SG, :],
                                      ALU.mult).then_inc(y_part, 1)
                    if g == 1 and c > 0:
                        finish(dve, chain, i, c - 1)
                finish(dve, chain, i, inner_chunks - 1)
                for b in range(group):
                    dve.wait_ge(out_ready, i * group + b + 1)
                    if b == 0:
                        dve.wait_ge(x1_stored, (i + 1) * 16 + 16)
                    dve.tensor_tensor(x_mix[:, b, :], ring[:, b, :], xn[:, b, :], ALU.add).then_inc(sum_ready, 1)
                dve.wait_ge(rms_ready, i + 1)
                chain(dve.reciprocal(rstd[:], std[:]))
                for b in range(group):
                    ins = dve.scalar_tensor_tensor(xn[:, b, :], x_mix[:, b, :], rstd[:, b:b + 1], norm_sb[:],
                                                   ALU.mult, ALU.mult)
                ins.then_inc(zm_ready, 1)
                dve.wait_ge(zm_ready, i + 1)
            chain.leave(links, steps, 0)

        @block.tensor
        def _(pe):
            pe.sem_inc(summed, 3)
            pe.wait_ge(ready, 9)
            pe.wait_ge(loaded, LOADED)
            with pe.Fori(0, steps) as i:
                pe.wait_ge(attn_loaded, i * 16 + 16)
                pe.wait_ge(sum_ready, i * group + group)
                for b in range(group):
                    for g in range(chunks):
                        ins = pe.matmul(ring[:, b, :], attn[:, b, g, :], wo[:, g, :], start=(g == 0),
                                        stop=(g == chunks - 1))
                    ins.then_inc(o_ready, 1)
                pe.wait_ge(xn_ready, i + 1)
                for b in range(group):
                    for k in range(chunks):
                        ins = pe.transpose(turned_ps[:, b, k * P:(k + 1) * P], xn[:, b, k * P:(k + 1) * P], ident[:])
                    ins.then_inc(turned, 1)
                pe.wait_ge(xn_t_ready, (i + 1) * group)
                for m in range(2 * pairs):
                    if m >= 4:
                        pe.wait_ge(in_taken, i * 2 * pairs + m - 3)
                    for half in range(2):
                        col = (2 * m + half) * P
                        for k in range(chunks):
                            ins = pe.matmul(ring[:, m % 4, half * T:(half + 1) * T], w_in[:, k, col:col + P],
                                            xn_t[:, k, :], start=(k == 0), stop=(k == chunks - 1))
                    ins.then_inc(in_ready, 1)
                for c in range(inner_chunks):
                    pe.wait_ge(u_ready, i * inner_chunks + c + 1 + 2)
                    ins = pe.matmul(turned_ps[0:ones_row, 0, 0:T], w_x[:, c, :], u[:, c, :], start=(c == 0),
                                    stop=(c == inner_chunks - 1))
                ins.then_inc(dbc_product, 1)
                pe.wait_ge(dbc_ready, i + 1)
                pe.wait_ge(in_taken, (i + 1) * 2 * pairs)
                for c in range(inner_chunks):
                    ins = pe.matmul(ring[:, c // 2, (c % 2) * T:(c % 2 + 1) * T], w_dt[:, c * P:(c + 1) * P],
                                    dbc[:], start=True, stop=True)
                ins.then_inc(dt_product, 1)
                pe.wait_ge(dt_ready, i + 1)
                for m in range(states):
                    if m >= 4:
                        pe.wait_ge(bc_ready, i * states + m - 3)
                    for half in range(2):
                        row = rank + 2 * m + half
                        ins = pe.matmul(ring[:, m % 4, half * T:(half + 1) * T],
                                        ident[0:ones_row, row:row + 1].to_broadcast([ones_row, P]),
                                        dbc[0:ones_row, :], start=True, stop=True)
                    ins.then_inc(bc_product, 1)
                for m in range(units):
                    c, g = m // groups, m % groups
                    if g == 0:
                        pe.wait_ge(y_ready, i * inner_chunks + c + 1)
                    pe.wait_ge(y_part, i * units + m + 1)
                    for s in range(SG):
                        ins = pe.matmul(y_ps[:, c % 2, 0:T], ident[:], drive[:, m % 3, s, :],
                                        start=(g == 0 and s == 0), stop=(g == groups - 1 and s == SG - 1))
                    ins.then_inc(summed, 1)
                pe.wait_ge(bc_ready, (i + 1) * states)
                pe.wait_ge(y_ready, (i + 1) * inner_chunks + 2)
                for b in range(group):
                    for c in range(inner_chunks):
                        ins = pe.matmul(ring[:, b, :], gate[:, c, b * P:(b + 1) * P], w_out[:, c, :],
                                        start=(c == 0), stop=(c == inner_chunks - 1))
                    ins.then_inc(out_ready, 1)


def feed_forward(nc, x1_dram, zm_dram, w1_t, b1, w2_t, b2, norm_w, w_gate, w_shared_t, w_expert_t, bias, out):
    batches, _, width = x1_dram.shape
    hidden = w2_t.shape[0]
    gates = w_gate.shape[1]
    chunks, hidden_chunks = width // P, hidden // P
    group = 4
    steps = batches // group
    T = group * P
    LOWEST = -3.4e38
    assert gates == 7

    with ExitStack() as ctx:
        def sb(name, shape, dt=F32):
            return ctx.enter_context(nc.sbuf_tensor(name, shape, dt))

        def psum(name, shape):
            return ctx.enter_context(nc.psum_tensor(name, shape, F32))

        def sem(name):
            return ctx.enter_context(nc.semaphore(name))

        w1 = sb("c_w1", [P, chunks, hidden])
        w2 = sb("c_w2", [P, hidden_chunks, width])
        w_s, w_e = sb("c_w_s", [P, chunks, width]), sb("c_w_e", [P, chunks, width])
        w_g = sb("c_w_g", [P, chunks, gates])
        b1_sb = sb("c_b1", [P, hidden_chunks])
        b2_sb, norm_sb, bias_sb = sb("c_b2", [P, width]), sb("c_norm", [P, width]), sb("c_bias", [P, width])
        ident = sb("c_ident", [P, P])
        eps_ln, eps_rms = sb("c_eps_ln", [P, 1]), sb("c_eps_rms", [P, 1])
        wait_taker = sb("c_wait_taker", [P, 1])

        zm = sb("c_zm", [P, group, width])
        x1 = sb("c_x1", [P, group, width])
        turned_sb = sb("c_turned_sb", [P, chunks, T])
        h_t = sb("c_h_t", [P, hidden_chunks, T])
        mix = sb("c_mix", [P, group, width])
        xf = sb("c_xf", [P, group, width])
        out_sb = sb("c_out_sb", [P, group, width])
        squares, mean_sq = sb("c_squares", [P, width]), sb("c_mean_sq", [P, group])
        std, rstd = sb("c_std", [P, group]), sb("c_rstd", [P, group])
        stats, moments = sb("c_stats", [P, group, 6]), sb("c_moments", [P, group, 2])
        logits, top = sb("c_logits", [P, group, 8]), sb("c_top", [P, group, 8])
        neg_top, exps, exp_sum = sb("c_neg_top", [P, group]), sb("c_exps", [P, group, 8]), sb("c_exp_sum", [P, group])
        two, two_sum, token_weight = sb("c_two", [P, group, 2]), sb("c_two_sum", [P, group]), sb("c_tw", [P, group])

        ring = psum("c_ring", [P, 4, 512])
        turned_ps = psum("c_turned_ps", [P, 2, 512])
        gate_ps = psum("c_gate_ps", [P, group, 8])

        loaded, ready = sem("c_loaded"), sem("c_ready")
        zm_loaded, x1_loaded = sem("c_zm_loaded"), sem("c_x1_loaded")
        turned, turned_taken = sem("c_turned"), sem("c_turned_taken")
        h_product, h_ready = sem("c_h_product"), sem("c_h_ready")
        mlp_ready, mix_ready, squared, rms_ready = sem("c_mlp"), sem("c_mix_ready"), sem("c_squared"), sem("c_rms")
        x2_ready = sem("c_x2_ready")
        moments_ready, std_ready, xf_ready = sem("c_moments_ready"), sem("c_std_ready"), sem("c_xf_ready")
        gate_ready, logits_ready, exp_ready = sem("c_gate_ready"), sem("c_logits_ready"), sem("c_exp_ready")
        ffn_ready, ffn_taken = sem("c_ffn_ready"), sem("c_ffn_taken")
        out_stored = sem("c_out_stored")
        dve_order = sem("c_dve_order")

        block = ctx.enter_context(nc.Block())
        x1_v, zm_v, out_v = (t.rearrange("(s b) t d -> s t b d", b=group) for t in (x1_dram, zm_dram, out))

        @block.sync
        def _(sp):
            sp.sem_inc(out_stored, 16)
            sp.dma_start(zm[:], zm_v[0]).then_inc(zm_loaded, 16)
            sp.dma_start(w1[:], w1_t.rearrange("(k p) o -> p k o", p=P)).then_inc(loaded, 16)
            sp.dma_start(b1_sb[:], b1).then_inc(loaded, 16)
            sp.dma_start(x1[:], x1_v[0]).then_inc(x1_loaded, 16)
            for dst, src in ((w2[:], w2_t.rearrange("(k p) o -> p k o", p=P)),
                             (w_s[:], w_shared_t.rearrange("(k p) o -> p k o", p=P)),
                             (w_e[:], w_expert_t.rearrange("(k p) o -> p k o", p=P)),
                             (w_g[:], w_gate.rearrange("(k p) o -> p k o", p=P)),
                             (b2_sb[:], b2.partition_broadcast(P)), (norm_sb[:], norm_w.partition_broadcast(P)),
                             (bias_sb[:], bias.partition_broadcast(P))):
                sp.dma_start(dst, src).then_inc(loaded, 16)

            def step(i, last):
                if not last:
                    sp.wait_ge(mix_ready, (i + 1) * group)
                    sp.dma_start(zm[:], zm_v[i + 1]).then_inc(zm_loaded, 16)
                    sp.wait_ge(x2_ready, i + 1)
                    sp.dma_start(x1[:], x1_v[i + 1]).then_inc(x1_loaded, 16)
                sp.wait_ge(ffn_taken, (i + 1) * group + group)
                sp.dma_start(out_v[i], out_sb[:]).then_inc(out_stored, 16)

            with sp.Fori(0, steps - 1) as i:
                step(i, False)
            step(steps - 1, True)
            sp.wait_ge(out_stored, 16 * (steps + 1))

        FIRST_LOADS, ALL_LOADS = 2 * 16, 9 * 16

        @block.gpsimd
        def _(pool):
            pool.memset(ident[:], 0.0).then_inc(ready, 1)
            pool.memset(eps_ln[:], LN_EPS).then_inc(ready, 1)
            pool.memset(eps_rms[:], RMS_EPS).then_inc(ready, 1)
            pool.memset(logits[:], LOWEST).then_inc(ready, 1)
            pool.wait_ge(ready, 4)
            pool.affine_select(out=ident[:], in_=ident[:], compare_op=ALU.not_equal, fill=1.0, base=0,
                               pattern=[[-1, P]], channel_multiplier=1).then_inc(ready, 1)

        @block.scalar
        def _(act):
            act.wait_ge(ready, 5)
            act.wait_ge(loaded, ALL_LOADS)

            def take_turned(i, half):
                for b in range(group):
                    n = half * group + b
                    act.wait_ge(turned, i * 2 * group + n + 1)
                    act.copy(turned_sb[:, :, b * P:(b + 1) * P],
                             turned_ps[:, b % 2, :].rearrange("p (k t) -> p k t", t=P)).then_inc(turned_taken, 1)

            with act.Fori(0, steps) as i:
                take_turned(i, 0)
                for m in range(hidden_chunks):
                    act.wait_ge(h_product, i * hidden_chunks + m + 1)
                    act.activation(h_t[:, m, :], ring[:, m % 4, :], ACT.Gelu,
                                   bias=b1_sb[:, m:m + 1]).then_inc(h_ready, 1)
                for b in range(group):
                    act.wait_ge(mix_ready, i * group + b + 1)
                    act.activation(squares[:], mix[:, b, :], ACT.Square, scale=float(width) ** -0.5,
                                   accum_out=mean_sq[:, b:b + 1]).then_inc(squared, 1)
                    act.wait_ge(squared, i * group + b + 1)
                act.activation(std[:], mean_sq[:], ACT.Sqrt, bias=eps_rms[:, 0:1]).then_inc(rms_ready, 1)
                act.wait_ge(moments_ready, i + 1)
                act.activation(std[:], moments[:, :, 1], ACT.Sqrt, bias=eps_ln[:, 0:1]).then_inc(std_ready, 1)
                take_turned(i, 1)
                act.wait_ge(logits_ready, i + 1)
                for b in range(group):
                    ins = act.activation(exps[:, b, :], top[:, b, :], ACT.Exp, bias=neg_top[:, b:b + 1],
                                         accum_out=exp_sum[:, b:b + 1])
                ins.then_inc(exp_ready, 1)

        @block.vector
        def _(dve):
            chain = Chain(dve, dve_order)
            dve.sem_inc(ffn_taken, group)
            dve.wait_ge(ready, 5)
            dve.wait_ge(loaded, ALL_LOADS)
            links = 2 * group + 13

            def wide(v):
                return v[:].unsqueeze(1).to_broadcast([P, group, width])

            with dve.Fori(0, steps) as i:
                chain.enter(i, links, 0)
                dve.wait_ge(zm_loaded, i * 16 + 16)
                for b in range(group):
                    dve.wait_ge(mlp_ready, i * group + b + 1)
                    chain(dve.tensor_tensor(mix[:, b, :], ring[:, b, :], zm[:, b, :], ALU.add))
                    dve.tensor_tensor(mix[:, b, :], mix[:, b, :], b2_sb[:], ALU.add).then_inc(mix_ready, 1)
                dve.wait_ge(rms_ready, i + 1)
                chain(dve.reciprocal(rstd[:], std[:]))
                for b in range(group):
                    ins = dve.scalar_tensor_tensor(mix[:, b, :], mix[:, b, :], rstd[:, b:b + 1], norm_sb[:],
                                                   ALU.mult, ALU.mult)
                chain(ins)
                dve.wait_ge(x1_loaded, i * 16 + 16)
                dve.tensor_tensor(mix[:], mix[:], x1[:], ALU.add).then_inc(x2_ready, 1)
                dve.wait_ge(x2_ready, i + 1)
                for b in range(group):
                    ins = dve.bn_stats(stats[:, b, :], mix[:, b, :])
                chain(ins)
                dve.memset(wait_taker[:], 0.0)
                for b in range(group):
                    ins = dve.bn_aggr(moments[:, b, :], stats[:, b, :])
                ins.then_inc(moments_ready, 1)
                dve.wait_ge(std_ready, i + 1)
                chain(dve.reciprocal(rstd[:], std[:]))
                for b in range(group):
                    ins = dve.tensor_scalar(xf[:, b, :], mix[:, b, :], moments[:, b, 0:1], rstd[:, b:b + 1],
                                            ALU.subtract, ALU.mult)
                ins.then_inc(xf_ready, 1)
                dve.wait_ge(xf_ready, i + 1)
                chain(dve.tensor_tensor(mix[:], mix[:], wide(bias_sb), ALU.add))
                dve.wait_ge(gate_ready, i + 1)
                chain(dve.tensor_copy(logits[:, :, 0:gates], gate_ps[:, :, 0:gates]))
                dve.memset(wait_taker[:], 0.0)
                for b in range(group):
                    ins = dve.max(out=top[:, b, :], in_=logits[:, b, :])
                chain(ins)
                dve.tensor_scalar(neg_top[:], top[:, :, 0], -1.0, None, ALU.mult).then_inc(logits_ready, 1)
                dve.wait_ge(exp_ready, i + 1)
                chain(dve.reciprocal(exp_sum[:], exp_sum[:]))
                chain(dve.tensor_tensor(two[:], exps[:, :, 0:2], exp_sum[:].unsqueeze(2).to_broadcast([P, group, 2]),
                                        ALU.mult))
                chain(dve.tensor_reduce(two_sum[:], two[:], AX.X, ALU.add))
                chain(dve.reciprocal(two_sum[:], two_sum[:]))
                chain(dve.tensor_tensor(two[:], two[:], two_sum[:].unsqueeze(2).to_broadcast([P, group, 2]), ALU.mult))
                chain(dve.tensor_reduce(token_weight[:], two[:], AX.X, ALU.add))
                dve.wait_ge(out_stored, i * 16 + 16)
                for b in range(group):
                    dve.wait_ge(ffn_ready, i * group + b + 1)
                    s, e = (2 * b) % 4, (2 * b + 1) % 4
                    chain(dve.scalar_tensor_tensor(out_sb[:, b, :], ring[:, e, :], token_weight[:, b:b + 1],
                                                   mix[:, b, :], ALU.mult, ALU.add))
                    ins = dve.tensor_tensor(out_sb[:, b, :], out_sb[:, b, :], ring[:, s, :], ALU.add)
                    ins.then_inc(ffn_taken, 1)
                dve.wait_ge(ffn_taken, (i + 1) * group + group)
            chain.leave(links, steps, 0)

        @block.tensor
        def _(pe):
            pe.sem_inc(turned_taken, 2)
            pe.wait_ge(ready, 5)
            pe.wait_ge(loaded, ALL_LOADS)

            def turn(i, half, src):
                for b in range(group):
                    pe.wait_ge(turned_taken, i * 2 * group + half * group + b + 1)
                    for k in range(chunks):
                        ins = pe.transpose(turned_ps[:, b % 2, k * P:(k + 1) * P], src[:, b, k * P:(k + 1) * P],
                                           ident[:])
                    ins.then_inc(turned, 1)
                pe.wait_ge(turned_taken, i * 2 * group + (half + 1) * group + 2)

            with pe.Fori(0, steps) as i:
                pe.wait_ge(zm_loaded, i * 16 + 16)
                turn(i, 0, zm)
                pe.wait_ge(ffn_taken, i * group + group)
                for m in range(hidden_chunks):
                    if m >= 4:
                        pe.wait_ge(h_ready, i * hidden_chunks + m - 3)
                    for k in range(chunks):
                        ins = pe.matmul(ring[:, m % 4, :], w1[:, k, m * P:(m + 1) * P], turned_sb[:, k, :],
                                        start=(k == 0), stop=(k == chunks - 1))
                    ins.then_inc(h_product, 1)
                pe.wait_ge(h_ready, (i + 1) * hidden_chunks)
                for b in range(group):
                    for m in range(hidden_chunks):
                        ins = pe.matmul(ring[:, b, :], h_t[:, m, b * P:(b + 1) * P], w2[:, m, :],
                                        start=(m == 0), stop=(m == hidden_chunks - 1))
                    ins.then_inc(mlp_ready, 1)
                pe.wait_ge(xf_ready, i + 1)
                turn(i, 1, xf)
                for b in range(group):
                    for k in range(chunks):
                        ins = pe.matmul(gate_ps[:, b, 0:gates], turned_sb[:, k, b * P:(b + 1) * P], w_g[:, k, :],
                                        start=(k == 0), stop=(k == chunks - 1))
                ins.then_inc(gate_ready, 1)
                for b in range(group):
                    if b >= 2:
                        pe.wait_ge(ffn_taken, i * group + b - 1 + group)
                    for bank, w in (((2 * b) % 4, w_s), ((2 * b + 1) % 4, w_e)):
                        for k in range(chunks):
                            ins = pe.matmul(ring[:, bank, :], turned_sb[:, k, b * P:(b + 1) * P], w[:, k, :],
                                            start=(k == 0), stop=(k == chunks - 1))
                    ins.then_inc(ffn_ready, 1)


def perceiver_layer(nc, i, out):
    batches, seq, width = i["x"].shape
    heads_shape = (batches, P, width // P, seq)
    q_dram = nc.dram_tensor("q_scratch", heads_shape, F32).ap()
    attn_dram = nc.dram_tensor("attn_scratch", heads_shape, F32).ap()
    x1_dram = nc.dram_tensor("x1_scratch", (batches, seq, width), F32).ap()
    zm_dram = nc.dram_tensor("zm_scratch", (batches, seq, width), F32).ap()
    project_queries(nc, i["x"], i["xattn_wq"], i["xattn_bq"], q_dram)
    cross_attention(nc, i["ctx"], i["xattn_wk"], i["xattn_wv"], i["xattn_bk"], i["xattn_bv"], q_dram, attn_dram,
                    heads=16)
    mamba(nc, i["x"], attn_dram, i["xattn_wo"], i["xattn_bo"], i["in_proj_w"], i["conv_w"], i["conv_b"],
          i["x_proj_w"], i["dt_proj_w"], i["dt_proj_b"], i["A_log"], i["D"], i["out_proj_w"], i["norm1_w"],
          x1_dram, zm_dram)
    feed_forward(nc, x1_dram, zm_dram, i["mlp_w1"], i["mlp_b1"], i["mlp_w2"], i["mlp_b2"], i["norm1_w"],
                 i["W_gate"], i["W_shared"], i["W_expert"], i["bias"], out)


def kernel(**inputs):
    import concourse.bacc as bacc
    from concourse.bass_utils import run_bass_kernel_spmd

    a = {name.removeprefix("L0_").removeprefix("attn_").removeprefix("ffn_"): np.asarray(v)
         for name, v in inputs.items()}

    def by_channel(v):
        return v.reshape((-1, P) + v.shape[1:]).swapaxes(0, 1)

    laid_out = {
        "x": a["x"],
        "ctx": a["ctx_1024"].transpose(0, 2, 1),
        "xattn_wq": a["xattn_wq"].T, "xattn_wk": a["xattn_wk"].T, "xattn_wv": a["xattn_wv"].T,
        "xattn_wo": a["xattn_wo"].T,
        "xattn_bq": by_channel(a["xattn_bq"]), "xattn_bk": by_channel(a["xattn_bk"]),
        "xattn_bv": by_channel(a["xattn_bv"]), "xattn_bo": a["xattn_bo"],
        "in_proj_w": a["in_proj_w"].T, "conv_w": by_channel(a["conv_w"]), "conv_b": by_channel(a["conv_b"]),
        "x_proj_w": a["x_proj_w"].T, "dt_proj_w": a["dt_proj_w"].T, "dt_proj_b": a["dt_proj_b"][None, :],
        "A_log": by_channel(a["A_log"]), "D": by_channel(a["D"]), "out_proj_w": a["out_proj_w"].T,
        "norm1_w": a["norm1_w"], "mlp_w1": a["mlp_w1"].T, "mlp_b1": by_channel(a["mlp_b1"]),
        "mlp_w2": a["mlp_w2"].T, "mlp_b2": a["mlp_b2"],
        "W_gate": a["W_gate"], "W_shared": a["W_shared"].T, "W_expert": a["W_expert"].T, "bias": a["bias"],
    }
    nc = bacc.Bacc("TRN2", target_bir_lowering=False, num_devices=1)
    arrays, aps = {}, {}
    for name, v in laid_out.items():
        arrays[f"in_{name}"] = np.ascontiguousarray(v)
        aps[name] = nc.dram_tensor(f"in_{name}", v.shape, mybir.dt.from_np(v.dtype), kind="ExternalInput").ap()
    out = nc.dram_tensor("out", a["x"].shape, F32, kind="ExternalOutput").ap()
    perceiver_layer(nc, aps, out)
    r = run_bass_kernel_spmd(nc, [arrays], core_ids=[0])
    return r.results[0]["out"]
```

```python
from contextlib import ExitStack

import numpy as np

import concourse.bass as bass
from concourse import mybir

F32 = mybir.dt.float32
F32R = mybir.dt.float32r
ALU = mybir.AluOpType
ACT = mybir.ActivationFunctionType
AX = mybir.AxisListType

P = 128
LN_EPS = 1e-5
RMS_EPS = 1e-6


class Chain:

    def __init__(self, eng, sem):
        self.eng, self.sem, self.base, self.n = eng, sem, 0, 0

    def __call__(self, ins):
        self.n += 1
        ins.then_inc(self.sem, 1)
        self.eng.wait_ge(self.sem, self.base + self.n)

    def enter(self, i, per_iteration, before):
        self.base, self.n = i * per_iteration + before, 0

    def leave(self, per_iteration, iterations, before):
        assert self.n == per_iteration, (self.n, per_iteration)
        self.base, self.n = 0, before + per_iteration * iterations


def project_queries(nc, x, wq_t, bq, q_dram):
    batches, _, width = x.shape
    chunks = width // P
    group = 4
    steps = batches // group
    T = group * P

    with ExitStack() as ctx:
        def sb(name, shape, dt=F32):
            return ctx.enter_context(nc.sbuf_tensor(name, shape, dt))

        def sem(name):
            return ctx.enter_context(nc.semaphore(name))

        wq = sb("wq_sb", [P, chunks, width])
        bq_sb = sb("bq_sb", [P, chunks])
        ident = sb("q_ident", [P, P])
        eps = sb("q_eps", [P, 1])
        wait_taker = sb("q_wait_taker", [P, 1])
        x_sb = sb("q_x", [P, group, width])
        xn = sb("q_xn", [P, group, width])
        xn_t = sb("q_xn_t", [P, chunks, T])
        q_sb = sb("q_out", [P, group, chunks, P])
        stats = sb("q_stats", [P, group, 6])
        moments = sb("q_moments", [P, group, 2])
        std = sb("q_std", [P, group])
        rstd = sb("q_rstd", [P, group])
        turned_ps = ctx.enter_context(nc.psum_tensor("q_turned_ps", [P, 2, T], F32))
        q_ps = ctx.enter_context(nc.psum_tensor("q_ps", [P, 2, T], F32))

        weights_loaded, x_loaded = sem("q_weights_loaded"), sem("q_x_loaded")
        ident_ready, moments_ready, std_ready = sem("q_ident_ready"), sem("q_moments_ready"), sem("q_std_ready")
        xn_ready, turned, xn_t_ready = sem("q_xn_ready"), sem("q_turned"), sem("q_xn_t_ready")
        product_ready, q_ready = sem("q_product_ready"), sem("q_ready")
        q_stored = sem("q_stored")
        dve_order = sem("q_dve_order")

        block = ctx.enter_context(nc.Block())
        x_v = x.rearrange("(s b) t d -> s t b d", b=group)
        q_v = q_dram.rearrange("(s b) p g t -> s p b g t", b=group)

        @block.sync
        def _(sp):
            sp.sem_inc(q_stored, 16)
            sp.dma_start(x_sb[:], x_v[0]).then_inc(x_loaded, 16)
            sp.dma_start(wq[:], wq_t.rearrange("(k p) o -> p k o", p=P)).then_inc(weights_loaded, 16)
            sp.dma_start(bq_sb[:], bq).then_inc(weights_loaded, 16)

            def step(i, last):
                if not last:
                    sp.wait_ge(xn_ready, i + 1)
                    sp.dma_start(x_sb[:], x_v[i + 1]).then_inc(x_loaded, 16)
                sp.wait_ge(q_ready, (i + 1) * chunks)
                sp.dma_start(q_v[i], q_sb[:]).then_inc(q_stored, 16)

            with sp.Fori(0, steps - 1) as i:
                step(i, False)
            step(steps - 1, True)
            sp.wait_ge(q_stored, 16 * (steps + 1))

        @block.gpsimd
        def _(pool):
            pool.memset(ident[:], 0.0).then_inc(ident_ready, 1)
            pool.memset(eps[:], LN_EPS).then_inc(ident_ready, 1)
            pool.wait_ge(ident_ready, 2)
            pool.affine_select(out=ident[:], in_=ident[:], compare_op=ALU.not_equal, fill=1.0, base=0,
                               pattern=[[-1, P]], channel_multiplier=1).then_inc(ident_ready, 1)

        @block.vector
        def _(dve):
            chain = Chain(dve, dve_order)

            with dve.Fori(0, steps) as i:
                chain.enter(i, 2, 0)
                dve.wait_ge(x_loaded, i * 16 + 16)
                for b in range(group):
                    ins = dve.bn_stats(stats[:, b, :], x_sb[:, b, :])
                chain(ins)
                dve.memset(wait_taker[:], 0.0)
                for b in range(group):
                    ins = dve.bn_aggr(moments[:, b, :], stats[:, b, :])
                ins.then_inc(moments_ready, 1)
                dve.wait_ge(std_ready, i + 1)
                chain(dve.reciprocal(rstd[:], std[:]))
                for b in range(group):
                    ins = dve.tensor_scalar(xn[:, b, :], x_sb[:, b, :], moments[:, b, 0:1], rstd[:, b:b + 1],
                                            ALU.subtract, ALU.mult)
                ins.then_inc(xn_ready, 1)
            chain.leave(2, steps, 0)

        @block.scalar
        def _(act):
            act.wait_ge(ident_ready, 3)
            act.wait_ge(weights_loaded, 32)
            with act.Fori(0, steps) as i:
                act.wait_ge(moments_ready, i + 1)
                act.activation(std[:], moments[:, :, 1], ACT.Sqrt, bias=eps[:, 0:1]).then_inc(std_ready, 1)
                for b in range(group):
                    act.wait_ge(turned, i * group + b + 1)
                    act.copy(xn_t[:, :, b * P:(b + 1) * P],
                             turned_ps[:, b % 2, :].rearrange("p (k t) -> p k t", t=P)).then_inc(xn_t_ready, 1)
                act.wait_ge(q_stored, i * 16 + 16)
                for g in range(chunks):
                    act.wait_ge(product_ready, i * chunks + g + 1)
                    act.activation(q_sb[:, :, g, :], q_ps[:, g % 2, :].rearrange("p (b t) -> p b t", t=P),
                                   ACT.Identity, bias=bq_sb[:, g:g + 1]).then_inc(q_ready, 1)

        @block.tensor
        def _(pe):
            pe.wait_ge(ident_ready, 3)
            pe.wait_ge(weights_loaded, 32)
            pe.sem_inc(xn_t_ready, 2)
            with pe.Fori(0, steps) as i:
                pe.wait_ge(xn_ready, i + 1)
                for b in range(group):
                    pe.wait_ge(xn_t_ready, i * group + b + 1)
                    for k in range(chunks):
                        ins = pe.transpose(turned_ps[:, b % 2, k * P:(k + 1) * P],
                                           xn[:, b, k * P:(k + 1) * P], ident[:])
                    ins.then_inc(turned, 1)
                pe.wait_ge(xn_t_ready, (i + 1) * group + 2)
                for g in range(chunks):
                    if g >= 2:
                        pe.wait_ge(q_ready, i * chunks + g - 1)
                    for k in range(chunks):
                        ins = pe.matmul(q_ps[:, g % 2, :], wq[:, k, g * P:(g + 1) * P], xn_t[:, k, :],
                                        start=(k == 0), stop=(k == chunks - 1))
                    ins.then_inc(product_ready, 1)


def cross_attention(nc, ctx_t, wk_t, wv_t, bk, bv, q_dram, attn_dram, heads):
    batches, width, keys = ctx_t.shape
    chunks = width // P
    block_keys = 512
    blocks = keys // block_keys
    per_block = block_keys // P
    tiles = keys // P
    hd = width // heads
    row_tiles = P // hd
    scale = float(hd) ** -0.5
    queries = P
    assert heads == chunks * row_tiles and per_block == chunks and row_tiles == 4
    QW = chunks * queries

    k_per_batch = blocks * chunks
    max_units = blocks * chunks * 2
    exp_units = tiles * 2

    with ExitStack() as ctx:
        def sb(name, shape, dt=F32):
            return ctx.enter_context(nc.sbuf_tensor(name, shape, dt))

        def sem(name):
            return ctx.enter_context(nc.semaphore(name))

        wk_hi, wk_lo = sb("wk_hi", [P, chunks, width], F32R), sb("wk_lo", [P, chunks, width], F32R)
        wv_hi, wv_lo = sb("wv_hi", [P, chunks, width], F32R), sb("wv_lo", [P, chunks, width], F32R)
        c_hi = sb("c_hi", [P, 2, chunks, block_keys], F32R)
        c_lo = sb("c_lo", [P, 2, chunks, block_keys], F32R)
        k_hi, k_lo = sb("k_hi", [P, chunks, keys], F32R), sb("k_lo", [P, chunks, keys], F32R)
        v_sb = sb("v_sb", [P, tiles, width])
        probs = sb("probs", [P, 4, 2, QW])
        prob_sums = sb("prob_sums", [P, chunks, QW])
        q_hi, q_lo = sb("q_hi", [P, chunks, QW], F32R), sb("q_lo", [P, chunks, QW], F32R)
        max_parts = sb("max_parts", [P, row_tiles, chunks, blocks])
        neg_max_pad = sb("neg_max_pad", [P, chunks * row_tiles, hd])
        neg_max = sb("neg_max", [P, QW], F32R)
        c_raw = prob_sums
        neg_max_all = c_hi[:, 1]
        out_sb = sb("attn_out_sb", [P, chunks, queries])
        q_raw = out_sb
        ident = sb("a_ident", [P, P])
        ident_r = sb("ident_r", [P, P], F32R)
        ones_f = sb("ones_f", [P, hd])
        bk_sb, bv_sb = sb("bk_sb", [P, chunks]), sb("bv_sb", [P, chunks])

        scores = ctx.enter_context(nc.psum_tensor("scores", [P, chunks, QW], F32))
        proj = ctx.enter_context(nc.psum_tensor("proj", [P, 2, 512], F32))
        o_acc = ctx.enter_context(nc.psum_tensor("o_acc", [P, QW], F32))
        misc = ctx.enter_context(nc.psum_tensor("misc", [P, QW], F32))

        weights_loaded, bias_loaded = sem("a_weights_loaded"), sem("a_bias_loaded")
        weights_split, ident_ready = sem("a_weights_split"), sem("a_ident_ready")
        ctx_loaded = sem("ctx_loaded")
        q_loaded, q_split = sem("q_loaded"), sem("q_split")
        c_hi_ready, c_lo_ready = sem("c_hi_ready"), sem("c_lo_ready")
        proj_ready = sem("proj_ready")
        k_hi_ready, k_lo_ready = sem("k_hi_ready"), sem("k_lo_ready")
        v_ready = sem("v_ready")
        max_scores = sem("max_scores")
        max_taken = sem("max_taken")
        pad_ready, pad_turned, neg_max_ready = sem("pad_ready"), sem("pad_turned"), sem("neg_max_ready")
        scores_ready = sem("scores_ready")
        shifted = sem("shifted")
        exp_done = sem("exp_done")
        pv_done = sem("pv_done")
        even_summed, odd_summed = sem("even_summed"), sem("odd_summed")
        neg_max_spread, neg_max_taken = sem("neg_max_spread"), sem("neg_max_taken")
        den_ready, attn_ready = sem("den_ready"), sem("attn_ready")
        attn_stored = sem("attn_stored")
        dve_order = sem("a_dve_order")

        block = ctx.enter_context(nc.Block())
        ctx_v = ctx_t.rearrange("b (k p) s -> b p k s", p=P)

        @block.sync
        def _(sp):
            sp.sem_inc(attn_stored, 16)
            for n, w in enumerate((wk_t, wv_t)):
                sp.dma_start(v_sb[:, n * chunks:(n + 1) * chunks, :],
                             w.rearrange("(k p) o -> p k o", p=P)).then_inc(weights_loaded, 16)
            sp.dma_start(q_raw[:], q_dram[0]).then_inc(q_loaded, 16)
            sp.dma_start(bk_sb[:], bk).then_inc(bias_loaded, 16)
            sp.dma_start(bv_sb[:], bv).then_inc(bias_loaded, 16)

            def load(b, s):
                sp.dma_start(c_raw[:], ctx_v[b, :, :, s * block_keys:(s + 1) * block_keys]
                             ).then_inc(ctx_loaded, 16)

            load(0, 0)

            def batch(i, first, last):
                for s in range(blocks):
                    if s < blocks - 1 or not last:
                        if s == 0 and not first:
                            sp.wait_ge(den_ready, i + 1)
                        sp.wait_ge(c_lo_ready, i * blocks + s + 1)
                        load(*((i, s + 1) if s < blocks - 1 else (i + 1, 0)))
                    if s == 0 and not first:
                        sp.wait_ge(attn_ready, i + 1)
                        sp.dma_start(attn_dram[i - 1], out_sb[:]).then_inc(attn_stored, 16)
                    if s == 1 and not last:
                        if first:
                            sp.wait_ge(q_split, 2)
                        sp.wait_ge(attn_stored, (i + 1) * 16)
                        sp.dma_start(q_raw[:], q_dram[i + 1]).then_inc(q_loaded, 16)

            batch(0, True, False)
            with sp.Fori(1, batches - 1) as i:
                batch(i, False, False)
            batch(batches - 1, False, True)
            sp.wait_ge(attn_ready, batches + 1)
            sp.dma_start(attn_dram[batches - 1], out_sb[:]).then_inc(attn_stored, 16)
            sp.wait_ge(attn_stored, 16 * (batches + 1))

        def add_up(eng, done, i, t, pair, last):
            part, new = prob_sums[:, 2 * pair:2 * pair + 2, :], probs[:, (2 * t + pair) % 4]
            eng.wait_ge(exp_done, i * exp_units + 2 * t + pair + 1)
            if t == 0:
                eng.wait_ge(c_lo_ready, (i + 1) * blocks + (0 if last else 1))
                ones = ones_f[:, 0:1].unsqueeze(2).to_broadcast([P, 2, QW])
                eng.tensor_tensor(part, new, ones, ALU.mult).then_inc(done, 1)
            else:
                eng.wait_ge(done, i * tiles + t + 2)
                eng.tensor_tensor(part, part, new, ALU.add).then_inc(done, 1)

        @block.gpsimd
        def _(pool):
            pool.memset(ident[:], 0.0).then_inc(ident_ready, 1)
            pool.wait_ge(ident_ready, 1)
            pool.affine_select(out=ident[:], in_=ident[:], compare_op=ALU.not_equal, fill=1.0, base=0,
                               pattern=[[-1, P]], channel_multiplier=1).then_inc(ident_ready, 1)
            pool.memset(neg_max_pad[:], 0.0).then_inc(ident_ready, 1)
            pool.memset(ones_f[:], 1.0).then_inc(ident_ready, 1)

            pool.sem_inc(odd_summed, 2)

            def low_part(n, s):
                pool.wait_ge(c_hi_ready, n + 1)
                pool.tensor_tensor(c_lo[:, s % 2], c_raw[:], c_hi[:, s % 2].bitcast(F32),
                                   ALU.subtract).then_inc(c_lo_ready, 1)

            low_part(0, 0)

            def batch(i, last):
                for s in range(blocks if not last else blocks - 1):
                    low_part(i * blocks + s + 1, s + 1)
                for t in range(tiles):
                    add_up(pool, odd_summed, i, t, 1, last)

            with pool.Fori(0, batches - 1) as i:
                batch(i, False)
            batch(batches - 1, True)

        @block.scalar
        def _(act):
            act.sem_inc(v_ready, chunks)
            act.wait_ge(bias_loaded, 32)

            def batch(i):
                for s in range(blocks):
                    n = i * blocks + s
                    for g in range(chunks):
                        act.wait_ge(proj_ready, n * 2 * chunks + g + 1)
                        act.activation(k_hi[:, g, s * block_keys:(s + 1) * block_keys], proj[:, g % 2, :],
                                       ACT.Identity, bias=bk_sb[:, g:g + 1]).then_inc(k_hi_ready, 1)
                    for r in range(per_block):
                        act.wait_ge(proj_ready, n * 2 * chunks + chunks + r + 1)
                        act.copy(v_sb[:, s * per_block + r, :], proj[:, r % 2, :]).then_inc(v_ready, 1)
                for g in range(chunks):
                    act.wait_ge(neg_max_spread, i * chunks + g + 1)
                    act.copy(neg_max_all[:, g, :], proj[:, g % 2, :]).then_inc(neg_max_taken, 1)
                for u in range(exp_units):
                    act.wait_ge(shifted, i * exp_units + u + 1 + 2)
                    act.activation(probs[:, u % 4], probs[:, u % 4], ACT.Exp, scale=scale).then_inc(exp_done, 1)

            with act.Fori(0, batches) as i:
                batch(i)

        @block.vector
        def _(dve):
            chain = Chain(dve, dve_order)
            dve.sem_inc(max_taken, 2)
            dve.sem_inc(shifted, 2)
            dve.sem_inc(even_summed, 2)
            dve.sem_inc(attn_ready, 1)
            dve.wait_ge(ident_ready, 4)
            dve.tensor_copy(ident_r[:], ident[:])
            dve.memset(q_hi[:].bitcast(mybir.dt.uint32), 0)
            dve.memset(q_lo[:].bitcast(mybir.dt.uint32), 0).then_inc(weights_split, 1)
            dve.wait_ge(weights_loaded, 32)
            for n, (hi, lo) in enumerate(((wk_hi, wk_lo), (wv_hi, wv_lo))):
                raw = v_sb[:, n * chunks:(n + 1) * chunks, :]
                chain(dve.tensor_copy(hi[:], raw))
                dve.tensor_tensor(lo[:], raw, hi[:].bitcast(F32), ALU.subtract).then_inc(weights_split, 1)

            def high_part(n, s):
                dve.wait_ge(ctx_loaded, (n + 1) * 16)
                dve.tensor_copy(c_hi[:, s % 2], c_raw[:]).then_inc(c_hi_ready, 1)

            high_part(0, 0)

            def split_queries(i):
                dve.wait_ge(q_loaded, i * 16 + 16)
                diagonal = [(slice(j * hd, (j + 1) * hd), slice(j * queries, (j + 1) * queries))
                            for j in range(row_tiles)]
                for js, qs in diagonal:
                    ins = dve.tensor_copy(q_hi[js, :, qs], q_raw[js])
                ins.then_inc(q_split, 1)
                dve.wait_ge(q_split, i * 2 + 1)
                for js, qs in diagonal:
                    ins = dve.tensor_tensor(q_lo[js, :, qs], q_raw[js], q_hi[js, :, qs].bitcast(F32),
                                            ALU.subtract)
                ins.then_inc(q_split, 1)

            def k_low(n, s, g):
                cols = slice(s * block_keys, (s + 1) * block_keys)
                dve.wait_ge(k_hi_ready, n * chunks + g + 1)
                dve.scalar_tensor_tensor(k_lo[:, g, cols], proj[:, g % 2, :], bk_sb[:, g:g + 1],
                                         k_hi[:, g, cols].bitcast(F32), ALU.add,
                                         ALU.subtract).then_inc(k_lo_ready, 1)

            def reduce_max(i, s, g):
                for pair in range(2):
                    u = (s * chunks + g) * 2 + pair
                    dve.wait_ge(max_scores, i * max_units + u + 1)
                    dve.tensor_reduce(max_parts[:, 2 * pair:2 * pair + 2, g, s],
                                      scores[:, 2 * pair:2 * pair + 2, :], AX.X,
                                      ALU.max).then_inc(max_taken, 1)

            def divide(i):
                dve.wait_ge(den_ready, i + 2)
                dve.wait_ge(attn_stored, (i + 1) * 16)
                chain(dve.reciprocal(out_sb[:], misc[:].rearrange("p (g q) -> p g q", q=queries)))
                chain(dve.tensor_tensor(out_sb[:], o_acc[:].rearrange("p (g q) -> p g q", q=queries),
                                        out_sb[:], ALU.mult))
                dve.tensor_tensor(out_sb[:], out_sb[:], bv_sb[:].unsqueeze(2).to_broadcast([P, chunks, queries]),
                                  ALU.add).then_inc(attn_ready, 1)

            def batch(i, first, last):
                split_queries(i)
                for s in range(blocks):
                    n = i * blocks + s
                    k_low(n, s, 0)
                    for g in range(chunks):
                        if g + 1 < chunks:
                            k_low(n, s, g + 1)
                        else:
                            if s < blocks - 1 or not last:
                                if s > 0 or not first:
                                    dve.wait_ge(proj_ready, n * 2 * chunks)
                                high_part(n + 1, s + 1)
                        reduce_max(i, s, g)
                    if s == 0 and not first:
                        divide(i - 1)
                dve.wait_ge(max_taken, (i + 1) * max_units + 2)
                dve.tensor_reduce(neg_max_pad[:, :, 0], max_parts[:].rearrange("p j g s -> p (j g) s"),
                                  AX.X, ALU.max, negate=True).then_inc(pad_ready, 1)
                dve.wait_ge(pad_turned, i + 1)
                dve.tensor_copy(neg_max[:], misc[:]).then_inc(neg_max_ready, 1)
                for u in range(exp_units):
                    t, pair = u // 2, u % 2
                    if t == 0:
                        dve.wait_ge(neg_max_taken, i * chunks + 2 * pair + 2)
                    dve.wait_ge(scores_ready, i * exp_units + u + 1)
                    dve.wait_ge(pv_done, i * exp_units + u + 1)
                    dve.wait_ge(odd_summed if pair else even_summed, i * tiles + t + 1)
                    dve.tensor_tensor(probs[:, u % 4], scores[:, 2 * pair:2 * pair + 2, :],
                                      neg_max_all[:, 2 * pair:2 * pair + 2, :].bitcast(F32), ALU.add).then_inc(shifted, 1)
                    if pair == 1 and t > 0:
                        add_up(dve, even_summed, i, t - 1, 0, last)
                add_up(dve, even_summed, i, tiles - 1, 0, last)

            batch(0, True, False)
            before = chain.n
            with dve.Fori(1, batches - 1) as i:
                chain.enter(i - 1, 2, before)
                batch(i, False, False)
            chain.leave(2, batches - 2, before)
            batch(batches - 1, False, True)
            divide(batches - 1)

        @block.tensor
        def _(pe):
            pe.sem_inc(pv_done, 4)
            pe.sem_inc(den_ready, 1)
            pe.wait_ge(ident_ready, 4)
            pe.wait_ge(weights_split, 3)

            def project(out, products):
                steps = [(lhs(k), rhs(k)) for lhs, rhs in products for k in range(chunks)]
                for m, (lhs, rhs) in enumerate(steps):
                    ins = pe.matmul(out, lhs, rhs, start=(m == 0), stop=(m == len(steps) - 1))
                ins.then_inc(proj_ready, 1)

            def project_k(i, s, g):
                n, slot = i * blocks + s, s % 2
                if g == 0:
                    pe.wait_ge(c_hi_ready, n + 1)
                    pe.wait_ge(c_lo_ready, n + 1)
                if g < 2:
                    pe.wait_ge(v_ready, n * chunks + g + 3)
                else:
                    pe.wait_ge(k_lo_ready, n * chunks + g - 1)
                gs = slice(g * P, (g + 1) * P)
                project(proj[:, g % 2, :], [
                    (lambda k: wk_hi[:, k, gs], lambda k: c_hi[:, slot, k, :]),
                    (lambda k: wk_lo[:, k, gs], lambda k: c_hi[:, slot, k, :]),
                    (lambda k: wk_hi[:, k, gs], lambda k: c_lo[:, slot, k, :])])

            def project_v(i, s, r):
                n, slot = i * blocks + s, s % 2
                if r < 2:
                    pe.wait_ge(k_lo_ready, n * chunks + r + 3)
                else:
                    pe.wait_ge(v_ready, n * chunks + r - 1 + chunks)
                rs = slice(r * P, (r + 1) * P)
                project(proj[:, r % 2, :], [
                    (lambda k: c_hi[:, slot, k, rs], lambda k: wv_hi[:, k, :]),
                    (lambda k: c_hi[:, slot, k, rs], lambda k: wv_lo[:, k, :]),
                    (lambda k: c_lo[:, slot, k, rs], lambda k: wv_hi[:, k, :])])

            def score_for_max(i, s, g):
                if s == 0 and g == 0:
                    pe.wait_ge(q_split, i * 2 + 2)
                    pe.wait_ge(shifted, i * exp_units + 2)
                pe.wait_ge(k_hi_ready, (i * blocks + s) * chunks + g + 1)
                for pair in range(2):
                    u = (s * chunks + g) * 2 + pair
                    pe.wait_ge(max_taken, i * max_units + u + 1)
                    for j in (2 * pair, 2 * pair + 1):
                        ins = pe.matmul(scores[:, j, :], q_hi[:, g, j * queries:(j + 1) * queries],
                                        k_hi[:, g, s * block_keys:(s + 1) * block_keys],
                                        start=True, stop=True)
                    ins.then_inc(max_scores, 1)

            def turn_neg_max(i):
                pe.wait_ge(pad_ready, i + 1)
                for j in range(row_tiles):
                    ins = pe.transpose(misc[:, j * P:(j + 1) * P],
                                       neg_max_pad[:, j * chunks:(j + 1) * chunks, :].rearrange(
                                           "p g d -> p (g d)"), ident[:])
                ins.then_inc(pad_turned, 1)

            def spread_neg_max(i, g):
                if g == 0:
                    pe.wait_ge(neg_max_ready, i + 1)
                if g < 2:
                    pe.wait_ge(v_ready, (i + 1) * k_per_batch + g + chunks - 1)
                else:
                    pe.wait_ge(neg_max_taken, i * chunks + g - 1)
                pe.matmul(proj[:, g % 2, :], ident_r[:, g * hd:g * hd + 1].to_broadcast([P, P]), neg_max[:],
                          start=True, stop=True).then_inc(neg_max_spread, 1)

            def score_unit(i, u):
                t, pair = u // 2, u % 2
                ts = slice(t * P, (t + 1) * P)
                if u == 0:
                    pe.wait_ge(max_taken, (i + 1) * max_units + 2)
                pe.wait_ge(shifted, i * exp_units + u + 1)
                for g in (2 * pair, 2 * pair + 1):
                    for step, (lhs, rhs) in enumerate(((k_hi, q_hi), (k_lo, q_hi), (k_hi, q_lo))):
                        ins = pe.matmul(scores[:, g, :], lhs[:, g, ts], rhs[:, g, :], start=(step == 0),
                                        stop=(step == 2))
                ins.then_inc(scores_ready, 1)

            def values(i, u):
                t, pair = u // 2, u % 2
                if u == 0:
                    pe.wait_ge(attn_ready, i + 1)
                    pe.wait_ge(v_ready, (i + 1) * k_per_batch + chunks)
                pe.wait_ge(exp_done, i * exp_units + u + 1)
                for g in (2 * pair, 2 * pair + 1):
                    for j in range(row_tiles):
                        h = g * row_tiles + j
                        ins = pe.matmul(o_acc[j * hd:(j + 1) * hd, g * queries:(g + 1) * queries],
                                        v_sb[:, t, h * hd:(h + 1) * hd],
                                        probs[:, u % 4, g % 2, j * queries:(j + 1) * queries],
                                        start=(u == 0 and g == 0), stop=(t == tiles - 1),
                                        skip_group_check=True, tile_position=(0, j * hd))
                ins.then_inc(pv_done, 1)

            def sum_over_keys(i):
                pe.wait_ge(even_summed, (i + 1) * tiles + 2)
                pe.wait_ge(odd_summed, (i + 1) * tiles + 2)
                for j in range(row_tiles):
                    ins = pe.matmul(misc[j * hd:(j + 1) * hd, :], ones_f[:],
                                    prob_sums[:, :, j * queries:(j + 1) * queries],
                                    start=True, stop=True, tile_position=(0, j * hd))
                ins.then_inc(den_ready, 1)

            def batch(i, first):
                for s in range(blocks):
                    project_k(i, s, 0)
                    if s == 0 and not first:
                        for u in range(exp_units - LAG, exp_units):
                            values(i - 1, u)
                    project_k(i, s, 1)
                    if s == 0 and not first:
                        sum_over_keys(i - 1)
                    score_for_max(i, s, 0)
                    for g in range(2, chunks):
                        project_k(i, s, g)
                        score_for_max(i, s, g - 1)
                    project_v(i, s, 0)
                    score_for_max(i, s, chunks - 1)
                    project_v(i, s, 1)
                    project_v(i, s, 2)
                    if s == blocks - 1:
                        turn_neg_max(i)
                    project_v(i, s, 3)
                for u in range(exp_units):
                    score_unit(i, u)
                    if u < 2:
                        for g in (2 * u, 2 * u + 1):
                            spread_neg_max(i, g)
                    if u >= LAG:
                        values(i, u - LAG)

            LAG = 2
            batch(0, True)
            with pe.Fori(1, batches) as i:
                batch(i, False)
            for u in range(exp_units - LAG, exp_units):
                values(batches - 1, u)
            sum_over_keys(batches - 1)


def mamba(nc, x, attn_dram, wo_t, bo, w_in_t, conv_w, conv_b, w_x_t, w_dt_t, dt_b, a_log, d_skip,
          w_out_t, norm_w, x1_dram, zm_dram):
    batches, seq, width = x.shape
    inner = w_out_t.shape[0]
    taps = conv_w.shape[2]
    rank = w_dt_t.shape[0]
    states = a_log.shape[2]
    chunks, inner_chunks = width // P, inner // P
    group = 2
    steps = batches // group
    T = group * seq
    pairs = inner_chunks // 2
    in_pairs = 2 * pairs
    SG = 2
    groups = states // SG
    units = groups * pairs
    rows = rank + 2 * states
    bc_slots = 4
    half = inner_chunks // 2
    assert seq == P and inner_chunks == 2 * chunks == 8 and 2 * rows == P and pairs == 4
    assert steps % 2 == 0 and rank % 32 == 0

    PE_OUT_LAST, PE_HEADS, PE_TURN, PE_IN, PE_X, PE_DT, PE_OUT = (0, 1), (3, 4), 6, 8, 19, (21, 23), (30, 31)
    ACT_SQUARES, ACT_RSTD, ACT_XN_T, ACT_IN, ACT_U, ACT_DBC, ACT_EXP, ACT_LOG = 5, 7, 8, 11, (14, 18), 21, (25, 27), (28, 30)
    DVE_SUM, DVE_X1, DVE_ZM, DVE_CONV, DVE_LOW = 2, 5, 6, 10, 20
    DVE_T, DVE_ONE_PLUS, DVE_DT, DVE_DT_U = (22, 24), (25, 27), (27, 29), 28

    with ExitStack() as ctx:
        def sb(name, shape, dt=F32):
            return ctx.enter_context(nc.sbuf_tensor(name, shape, dt))

        def psum(name, shape):
            return ctx.enter_context(nc.psum_tensor(name, shape, F32))

        def sem(name):
            return ctx.enter_context(nc.semaphore(name))

        wo = sb("b_wo", [P, chunks, width])
        w_in = sb("b_w_in", [P, chunks, 2 * inner])
        w_x = sb("b_w_x", [P, inner_chunks, 2, rows])
        w_dt = sb("b_w_dt", [rank + 1, inner])
        w_out = sb("b_w_out", [P, inner_chunks, width])
        bo_sb, norm_sb = sb("b_bo", [P, width]), sb("b_norm", [P, width])
        conv_w_sb, conv_b_sb = sb("b_conv_w", [P, inner_chunks, taps]), sb("b_conv_b", [P, inner_chunks])
        a_neg, d_sb = sb("b_a", [P, inner_chunks, states]), sb("b_d", [P, inner_chunks])
        ident = sb("b_ident", [P, P])
        selector = sb("b_selector", [P, rows], F32R)

        attn = sb("b_attn", [P, group, chunks, P])
        x1 = sb("b_x1", [P, group, width])
        xn = sb("b_xn", [P, 2, group, width])
        xn_t = sb("b_xn_t", [P, chunks, T])
        padded = sb("b_padded", [P, 2, 2 * group, taps - 1 + seq])
        u = sb("b_u", [P, 2, inner_chunks, T])
        gate = sb("b_gate", [P, 2, inner_chunks, T])
        dbc = sb("b_dbc", [P, 2, T], F32R)
        dt_low = sb("b_dt_low", [rank + 1, T])
        dt = sb("b_dt", [P, 2, inner_chunks, T])
        dt_u = sb("b_dt_u", [P, inner_chunks, T])
        bc = sb("b_bc", [P, bc_slots, 2, SG, T])
        mix = sb("b_mix", [P, group, width])
        exp_neg = (xn_t[:].rearrange("p c (b t) -> p (c b) t", t=seq), mix[:].rearrange("p b (c t) -> p (b c) t", t=seq))
        one_plus = padded[:].rearrange("p n r t -> p (n r) t")[:, :, taps - 1:]
        squares = padded[:, 0, :, taps - 1:]
        decay = sb("b_decay", [P, 2, SG, 2, group, seq])
        drive = sb("b_drive", [P, 4, SG, 2, T])
        state = sb("b_state", [P, 2, SG, 2, T])
        stats, moments = sb("b_stats", [P, group, 6]), sb("b_moments", [P, group, 2])
        eps_ln, eps_rms = sb("b_eps_ln", [P, 1]), sb("b_eps_rms", [P, 1])
        wait_taker = sb("b_wait_taker", [P, 1])
        rstd, out_rstd, mean_sq = sb("b_rstd", [P, group]), sb("b_out_rstd", [P, group]), sb("b_mean_sq", [P, group])

        y_ps = psum("b_y", [P, pairs, 512])
        work = psum("b_work", [P, 2, 512])
        bc_ps = psum("b_bc_ps", [P, 2, 512])

        ready = sem("b_ready")
        heads_loaded, loaded = sem("b_heads_loaded"), sem("b_loaded")
        x_half_loaded, z_half_loaded = sem("b_x_half_loaded"), sem("b_z_half_loaded")
        attn_loaded, x_loaded = sem("b_attn_loaded"), sem("b_x_loaded")
        o_ready, x1_ready, x1_stored = sem("b_o_ready"), sem("b_x1_ready"), sem("b_x1_stored")
        xn_ready, turned, xn_t_ready = sem("b_xn_ready"), sem("b_turned_ready"), sem("b_xn_t_ready")
        in_ready, in_taken = sem("b_in_ready"), sem("b_in_taken")
        conv_ready, u_ready = sem("b_conv_ready"), sem("b_u_ready")
        gate_ready = sem("b_gate_ready")
        dbc_product, dbc_ready, low_ready = sem("b_dbc_product"), sem("b_dbc_ready"), sem("b_low_ready")
        dt_product, t_taken = sem("b_dt_product"), sem("b_t_taken")
        exp_ready, one_plus_ready, log_ready = sem("b_exp_ready"), sem("b_one_plus"), sem("b_log_ready")
        dt_ready, dt_u_ready = sem("b_dt_ready"), sem("b_dt_u_ready")
        bc_product, bc_ready = sem("b_bc_product"), sem("b_bc_ready")
        decay_ready = sem("b_decay_ready")
        drive_ready = sem("b_drive_ready")
        scanned = sem("b_scanned")
        y_part = sem("b_y_part")
        summed = sem("b_summed")
        y_ready = sem("b_y_ready")
        out_ready, sum_ready = sem("b_out_ready"), sem("b_sum_ready")
        squared, zm_ready, zm_stored = sem("b_squared"), sem("b_zm_ready"), sem("b_zm_stored")
        moments_ready, rstd_ready, out_rstd_ready = sem("b_moments_ready"), sem("b_rstd_ready"), sem("b_out_rstd")
        dve_order = sem("b_dve_order")

        block = ctx.enter_context(nc.Block())
        attn_v = attn_dram.rearrange("(s b) p g t -> s p b g t", b=group)
        x_v, x1_v, zm_v = (t.rearrange("(s b) t d -> s t b d", b=group) for t in (x, x1_dram, zm_dram))

        def by_row(tokens):
            return tokens.rearrange("p c (b t) -> p (c b) t", t=seq)

        def run_steps(eng, front, body, finish):
            front(0, 0)
            body(0, 0, True, False)
            with eng.Fori(0, (steps - 2) // 2) as k:
                body(k * 2 + 1, 1, False, False)
                body(k * 2 + 2, 0, False, False)
            body(steps - 1, 1, False, True)
            finish()

        @block.sync
        def _(sp):
            sp.sem_inc(zm_stored, 32)
            sp.dma_start(attn[:], attn_v[0]).then_inc(attn_loaded, 16)
            sp.dma_start(wo[:], wo_t.rearrange("(k p) o -> p k o", p=P)).then_inc(heads_loaded, 16)
            sp.dma_start(x1[:], x_v[0]).then_inc(x_loaded, 16)
            sp.dma_start(bo_sb[:], bo.partition_broadcast(P)).then_inc(heads_loaded, 16)
            w_in_v = w_in_t.rearrange("(k p) o -> p k o", p=P)
            for part in range(2):
                cols = slice(part * inner, (part + 1) * inner)
                sp.dma_start(w_in[:, :, cols], w_in_v[:, :, cols]).then_inc((x_half_loaded, z_half_loaded)[part], 16)
                if part == 0:
                    sp.dma_start(conv_w_sb[:], conv_w).then_inc(x_half_loaded, 16)
                    sp.dma_start(conv_b_sb[:], conv_b).then_inc(x_half_loaded, 16)
            w_x_v = w_x_t.rearrange("(k p) o -> p k o", p=P)
            for dst, src in ((w_x[:, :, 0, :], w_x_v), (w_x[:, :, 1, :], w_x_v),
                             (w_dt[0:rank, :], w_dt_t), (w_dt[rank:rank + 1, :], dt_b),
                             (a_neg[:], a_log), (d_sb[:], d_skip),
                             (norm_sb[:], norm_w.partition_broadcast(P)),
                             (w_out[:], w_out_t.rearrange("(k p) o -> p k o", p=P))):
                sp.dma_start(dst, src).then_inc(loaded, 16)

            def step(j, first, last):
                if not last:
                    sp.wait_ge(o_ready, (j + 1) * group)
                    sp.dma_start(attn[:], attn_v[j + 1]).then_inc(attn_loaded, 16)
                sp.wait_ge(xn_ready, j + 1)
                sp.dma_start(x1_v[j], x1[:]).then_inc(x1_stored, 16)
                if not first:
                    sp.wait_ge(zm_ready, j - 1)
                    sp.dma_start(zm_v[j - 2], mix[:]).then_inc(zm_stored, 16)
                if not last:
                    sp.wait_ge(x1_stored, (j + 1) * 16)
                    sp.dma_start(x1[:], x_v[j + 1]).then_inc(x_loaded, 16)

            step(0, True, False)
            step(1, True, False)
            with sp.Fori(2, steps - 1) as j:
                step(j, False, False)
            step(steps - 1, False, True)
            for t in (steps - 2, steps - 1):
                sp.wait_ge(zm_ready, t + 1)
                sp.dma_start(zm_v[t], mix[:]).then_inc(zm_stored, 16)
            sp.wait_ge(x1_stored, 16 * steps)
            sp.wait_ge(zm_stored, 16 * (steps + 2))

        HEADS_LOADED, X_HALF_LOADED, Z_HALF_LOADED, LOADED = 2 * 16, 3 * 16, 16, 8 * 16

        @block.gpsimd
        def _(pool):
            pool.memset(ident[:], 0.0).then_inc(ready, 1)
            pool.wait_ge(ready, 1)
            pool.affine_select(out=ident[:], in_=ident[:], compare_op=ALU.not_equal, fill=1.0, base=0,
                               pattern=[[-1, P]], channel_multiplier=1).then_inc(ready, 1)
            pool.memset(eps_ln[:], LN_EPS).then_inc(ready, 1)
            pool.memset(eps_rms[:], RMS_EPS).then_inc(ready, 1)
            pool.memset(padded[:], 0.0).then_inc(ready, 1)
            pool.memset(decay[:], 0.0).then_inc(ready, 1)
            pool.wait_ge(ready, 6)
            pool.memset(dt_low[rank:rank + 1, :], 1.0).then_inc(ready, 1)
            pool.wait_ge(ready, 7)

            def body(i, par, first, last):
                for m in range(units):
                    g, p = m // pairs, m % pairs
                    if g == 0:
                        pool.wait_ge(dt_u_ready, i * pairs + p + 1)
                    if p == 0:
                        pool.wait_ge(bc_ready, i * 2 * groups + 2 * g + 1 + 2)
                    pool.wait_ge(summed, i * units + m + 1)
                    pool.tensor_tensor(
                        drive[:, m % 4], dt_u[:, 2 * p:2 * p + 2, :].unsqueeze(1).to_broadcast([P, SG, 2, T]),
                        bc[:, g % bc_slots, 0].unsqueeze(2).to_broadcast([P, SG, 2, T]), ALU.mult
                    ).then_inc(drive_ready, 1)

            run_steps(pool, lambda j, par: None, body, lambda: None)

        @block.scalar
        def _(act):
            act.wait_ge(ready, 7)

            def take_squares(t):
                for b in range(group):
                    act.wait_ge(sum_ready, t * group + b + 1 + 2 * group)
                    act.activation(squares, mix[:, b, :].rearrange("p (c t) -> p c t", t=seq), ACT.Square, scale=float(width) ** -0.5,
                                   accum_out=mean_sq[:, b:b + 1]).then_inc(squared, 1)
                    act.wait_ge(squared, t * 3 + b + 1)
                act.activation(out_rstd[:], mean_sq[:], ACT.Ln, bias=eps_rms[:, 0:1]).then_inc(squared, 1)
                act.wait_ge(squared, (t + 1) * 3)
                act.activation(out_rstd[:], out_rstd[:], ACT.Exp, scale=-0.5).then_inc(out_rstd_ready, 1)

            def take_variance(j):
                act.wait_ge(moments_ready, j * 2 + 1)
                act.activation(rstd[:], moments[:, :, 1], ACT.Ln, bias=eps_ln[:, 0:1]).then_inc(moments_ready, 1)
                act.wait_ge(moments_ready, j * 2 + 2)
                act.activation(rstd[:], rstd[:], ACT.Exp, scale=-0.5).then_inc(rstd_ready, 1)

            def take_turned(j):
                for b in range(group):
                    act.wait_ge(turned, j * group + b + 1)
                    act.copy(xn_t[:, :, b * P:(b + 1) * P],
                             work[:, b, :].rearrange("p (k t) -> p k t", t=P)).then_inc(xn_t_ready, 1)

            def take_in(j, par, n):
                act.wait_ge(in_ready, j * in_pairs + n + 1)
                if n < pairs:
                    act.wait_ge(conv_ready, j * pairs + n + 1)
                    act.copy(padded[:, n % 2, :, taps - 1:],
                             work[:, n % 2, :].rearrange("p (r t) -> p r t", t=seq)).then_inc(in_taken, 1)
                else:
                    if n == pairs:
                        act.wait_ge(sum_ready, (j + 1) * group)
                    c = 2 * (n - pairs)
                    act.copy(gate[:, par, c:c + 2, :],
                             work[:, n % 2, :].rearrange("p (c t) -> p c t", t=T)).then_inc(in_taken, 1)

            def silu_u(j, par, h):
                act.wait_ge(conv_ready, j * pairs + (h + 1) * pairs // 2 + 2)
                for c in range(h * half, (h + 1) * half):
                    ins = act.activation(u[:, par, c, :], u[:, par, c, :], ACT.Silu, bias=conv_b_sb[:, c:c + 1])
                ins.then_inc(u_ready, 1)

            def silu_gate(j, par):
                act.wait_ge(in_taken, (j + 1) * in_pairs)
                act.activation(gate[:, par], gate[:, par], ACT.Silu).then_inc(gate_ready, 1)

            def take_dbc(j, par):
                act.wait_ge(dbc_product, j + 1)
                act.copy(dt_low[0:rank, :], work[0:rank, 0, 0:T])
                act.copy(dbc[:, par, :], work[:, 0, 0:T]).then_inc(dbc_ready, 1)

            def exp_of_abs(j, par, h):
                act.wait_ge(t_taken, j * 2 + h + 1)
                if h == 1:
                    act.wait_ge(zm_stored, (j + 1) * 16)
                act.activation(exp_neg[h], by_row(dt[:, par, h * half:(h + 1) * half, :]), ACT.Abs).then_inc(exp_ready, 1)
                act.wait_ge(exp_ready, j * 4 + 2 * h + 1)
                act.activation(exp_neg[h], exp_neg[h], ACT.Exp, scale=-1.0).then_inc(exp_ready, 1)

            def log(j, h):
                act.wait_ge(one_plus_ready, j * 4 + 2 * h + 2)
                act.activation(one_plus, one_plus, ACT.Ln).then_inc(log_ready, 1)

            def take_bc(i, g, which):
                act.wait_ge(bc_product, i * 2 * groups + 2 * g + which + 1)
                act.copy(bc[:, g % bc_slots, which], bc_ps[:, which, :].rearrange("p (s t) -> p s t", t=T)
                         ).then_inc(bc_ready, 1)

            def front(j, par):
                take_variance(j)
                take_turned(j)
                for n in range(in_pairs):
                    take_in(j, par, n)
                    if n == pairs:
                        act.wait_ge(x_half_loaded, X_HALF_LOADED)
                        for h in range(2):
                            silu_u(j, par, h)
                silu_gate(j, par)
                take_dbc(j, par)
                for h in range(2):
                    exp_of_abs(j, par, h)
                    log(j, h)
                for which in range(2):
                    take_bc(j, 0, which)
                act.wait_ge(loaded, LOADED)
                act.activation(a_neg[:], a_neg[:], ACT.Exp, bias=0.0).then_inc(ready, 1)
                act.wait_ge(ready, 10)

            def body(i, par, first, last):
                j = i + 1
                for m in range(units):
                    g, p = m // pairs, m % pairs
                    act.wait_ge(scanned, i * units + m + 1)
                    if g == 0:
                        act.wait_ge(dt_ready, i * 2 + p // 2 + 1)
                    for s in range(SG):
                        for cc in range(2):
                            c = 2 * p + cc
                            ins = act.activation(
                                decay[:, m % 2, s, cc, :, 1:],
                                dt[:, par, c, :].rearrange("p (b t) -> p b t", t=seq)[:, :, 1:], ACT.Exp,
                                scale=a_neg[:, c, g * SG + s:g * SG + s + 1])
                    ins.then_inc(decay_ready, 1)
                    if m % pairs < 2 and not (last and g == groups - 1):
                        if not first or g > 2:
                            act.wait_ge(y_part, i * units + (g - 2) * pairs)
                        if g < groups - 1:
                            take_bc(i, g + 1, m % pairs)
                        else:
                            take_bc(j, 0, m % pairs)
                    if not first and m == ACT_SQUARES:
                        take_squares(i - 1)
                    if last:
                        continue
                    if m == ACT_RSTD:
                        take_variance(j)
                    if m == ACT_XN_T:
                        take_turned(j)
                    if ACT_IN <= m < ACT_IN + in_pairs:
                        take_in(j, 1 - par, m - ACT_IN)
                    if m in ACT_U:
                        silu_u(j, 1 - par, ACT_U.index(m))
                    if m == ACT_U[1]:
                        silu_gate(j, 1 - par)
                    if m == ACT_DBC:
                        take_dbc(j, 1 - par)
                    if m in ACT_EXP:
                        exp_of_abs(j, 1 - par, ACT_EXP.index(m))
                    if m in ACT_LOG:
                        log(j, ACT_LOG.index(m))

            act.sem_inc(bc_ready, 2)
            run_steps(act, front, body, lambda: take_squares(steps - 1))

        TAIL_LINKS, FRONT_LINKS, END_LINKS = 0, group + 1 + pairs * 2 * (taps - 1) + 2, pairs

        @block.vector
        def _(dve):
            chain = Chain(dve, dve_order)
            dve.sem_inc(scanned, 2)
            dve.sem_inc(conv_ready, 2)
            dve.sem_inc(y_ready, pairs)
            dve.sem_inc(sum_ready, 2 * group)
            dve.wait_ge(ready, 7)
            dve.tensor_tensor(selector[:], ident[:, 0:rows], ident[:, rows:2 * rows], ALU.add).then_inc(ready, 1)
            dve.wait_ge(heads_loaded, HEADS_LOADED)

            def add_heads(j, par):
                dve.wait_ge(x_loaded, j * 16 + 16)
                for b in range(group):
                    dve.wait_ge(o_ready, j * group + b + 1)
                    chain(dve.tensor_tensor(x1[:, b, :], work[:, b, :], x1[:, b, :], ALU.add))
                dve.tensor_tensor(x1[:], x1[:], bo_sb[:].unsqueeze(1).to_broadcast([P, group, width]),
                                  ALU.add).then_inc(x1_ready, 1)
                dve.wait_ge(x1_ready, j + 1)
                for b in range(group):
                    ins = dve.bn_stats(stats[:, b, :], x1[:, b, :])
                chain(ins)
                dve.memset(wait_taker[:], 0.0)
                for b in range(group):
                    ins = dve.bn_aggr(moments[:, b, :], stats[:, b, :])
                ins.then_inc(moments_ready, 1)
                dve.wait_ge(rstd_ready, j + 1)
                for b in range(group):
                    ins = dve.tensor_scalar(xn[:, par, b, :], x1[:, b, :], moments[:, b, 0:1], rstd[:, b:b + 1],
                                            ALU.subtract, ALU.mult)
                ins.then_inc(xn_ready, 1)

            def convolve(j, par, p):
                dve.wait_ge(in_taken, j * in_pairs + p + 1)
                for c in (2 * p, 2 * p + 1):
                    r = (c % 2) * group
                    out = u[:, par, c, :].rearrange("p (b t) -> p b t", t=seq)
                    for k in range(taps):
                        src = padded[:, p % 2, r:r + group, k:k + seq]
                        tap = conv_w_sb[:, c, k:k + 1]
                        if k == 0:
                            ins = dve.tensor_scalar(out, src, tap, None, ALU.mult)
                        else:
                            ins = dve.scalar_tensor_tensor(out, src, tap, out, ALU.mult, ALU.add)
                        if k < taps - 1:
                            chain(ins)
                ins.then_inc(conv_ready, 1)

            def take_low(j, par):
                dve.wait_ge(dbc_ready, j + 1)
                dve.tensor_tensor(dbc[rows:2 * rows, par, :], work[rows:2 * rows, 0, 0:T],
                                  dbc[rows:2 * rows, par, :].bitcast(F32), ALU.subtract).then_inc(low_ready, 1)

            def take_t(j, par, h):
                dve.wait_ge(dt_product, j * 2 + h + 1)
                dve.tensor_copy(dt[:, par, h * half:(h + 1) * half, :],
                                work[:].rearrange("p r (c t) -> p (r c) t", t=T)).then_inc(t_taken, 1)

            def add_one(j, h):
                dve.wait_ge(exp_ready, j * 4 + 2 * h + 2)
                if h == 1:
                    dve.wait_ge(dt_ready, j * 2 + 1)
                dve.tensor_scalar(one_plus, exp_neg[h], 1.0, None, ALU.add).then_inc(one_plus_ready, 1)
                dve.wait_ge(one_plus_ready, j * 4 + 2 * h + 1)
                dve.scalar_tensor_tensor(exp_neg[h], one_plus, -1.0, exp_neg[h], ALU.add,
                                         ALU.subtract).then_inc(one_plus_ready, 1)

            def make_dt(j, par, h):
                dve.wait_ge(log_ready, j * 2 + h + 1)
                part = by_row(dt[:, par, h * half:(h + 1) * half, :])
                chain(dve.scalar_tensor_tensor(part, part, 0.0, one_plus, ALU.max, ALU.add))
                dve.tensor_tensor(part, part, exp_neg[h], ALU.subtract).then_inc(dt_ready, 1)

            def make_dt_u(j, par, p):
                dve.wait_ge(dt_ready, j * 2 + p // 2 + 1)
                pair = slice(2 * p, 2 * p + 2)
                dve.tensor_tensor(dt_u[:, pair, :], dt[:, par, pair, :], u[:, par, pair, :],
                                  ALU.mult).then_inc(dt_u_ready, 1)

            def end_pair(i, par, p):
                dve.wait_ge(summed, i * units + (groups - 1) * pairs + p + 1 + 4)
                dve.wait_ge(gate_ready, i + 1)
                for cc in range(2):
                    c = 2 * p + cc
                    ins = dve.scalar_tensor_tensor(u[:, par, c, :], u[:, par, c, :], d_sb[:, c:c + 1],
                                                   y_ps[:, p, cc * T:(cc + 1) * T], ALU.mult, ALU.add)
                chain(ins)
                pair = slice(2 * p, 2 * p + 2)
                dve.tensor_tensor(gate[:, par, pair, :], u[:, par, pair, :], gate[:, par, pair, :],
                                  ALU.mult).then_inc(y_ready, 1)

            def add_input(t, par):
                dve.wait_ge(zm_stored, t * 16 + 32)
                for b in range(group):
                    dve.wait_ge(out_ready, t * group + b + 1)
                    dve.tensor_tensor(mix[:, b, :], work[:, b, :], xn[:, par, b, :], ALU.add).then_inc(sum_ready, 1)

            def normalise(t):
                dve.wait_ge(out_rstd_ready, t + 1)
                for b in range(group):
                    ins = dve.scalar_tensor_tensor(mix[:, b, :], mix[:, b, :], out_rstd[:, b:b + 1], norm_sb[:],
                                                   ALU.mult, ALU.mult)
                ins.then_inc(zm_ready, 1)

            def front(j, par):
                chain.base, chain.n = 0, 0
                add_heads(j, par)
                dve.wait_ge(x_half_loaded, X_HALF_LOADED)
                for p in range(pairs):
                    convolve(j, par, p)
                take_low(j, par)
                for h in range(2):
                    take_t(j, par, h)
                for h in range(2):
                    add_one(j, h)
                    make_dt(j, par, h)
                for p in range(pairs):
                    make_dt_u(j, par, p)
                dve.wait_ge(loaded, LOADED)
                dve.wait_ge(ready, 9)
                dve.tensor_scalar(a_neg[:], a_neg[:], -1.0, None, ALU.mult).then_inc(ready, 1)
                assert chain.n == FRONT_LINKS

            def body(i, par, first, last):
                j = i + 1
                done = FRONT_LINKS + (FRONT_LINKS + END_LINKS - 1)
                per_step = TAIL_LINKS + FRONT_LINKS + END_LINKS
                chain.base, chain.n = (FRONT_LINKS if first else (i - 1) * per_step + done), 0
                for m in range(units):
                    g, p = m // pairs, m % pairs
                    dve.wait_ge(decay_ready, i * units + m + 1)
                    dve.wait_ge(drive_ready, i * units + m + 1)
                    if not first or m > 1:
                        dve.wait_ge(y_part, i * units + m - 1)
                    dve.tensor_tensor_scan(state[:, m % 2].rearrange("p n c t -> p (n c t)"),
                                           decay[:, m % 2].rearrange("p n c b t -> p (n c b t)"),
                                           drive[:, m % 4].rearrange("p n c t -> p (n c t)"),
                                           0.0, ALU.mult, ALU.add).then_inc(scanned, 1)
                    dve.wait_ge(scanned, i * units + m + 1 + 2)
                    if p == 0:
                        dve.wait_ge(bc_ready, i * 2 * groups + 2 * g + 2 + 2)
                    dve.tensor_tensor(drive[:, m % 4], state[:, m % 2],
                                      bc[:, g % bc_slots, 1].unsqueeze(2).to_broadcast([P, SG, 2, T]),
                                      ALU.mult).then_inc(y_part, 1)
                    if m == 0 and not first:
                        end_pair(i - 1, 1 - par, pairs - 1)
                    if not first and m == DVE_SUM:
                        add_input(i - 1, 1 - par)
                    if not last and m == DVE_X1:
                        dve.wait_ge(sum_ready, (j + 1) * group)
                        add_heads(j, 1 - par)
                    if not first and m == DVE_ZM:
                        normalise(i - 1)
                    if not last:
                        if DVE_CONV <= m < DVE_CONV + pairs:
                            convolve(j, 1 - par, m - DVE_CONV)
                        if m == DVE_LOW:
                            take_low(j, 1 - par)
                        if m in DVE_T:
                            take_t(j, 1 - par, DVE_T.index(m))
                        if m in DVE_DT:
                            make_dt(j, 1 - par, DVE_DT.index(m))
                        if m in DVE_ONE_PLUS:
                            add_one(j, DVE_ONE_PLUS.index(m))
                        if m >= DVE_DT_U:
                            make_dt_u(j, 1 - par, m - DVE_DT_U)
                    if g == groups - 1 and p > 0:
                        end_pair(i, par, p - 1)
                if not last:
                    links = END_LINKS + FRONT_LINKS + TAIL_LINKS - (TAIL_LINKS + 1 if first else 0)
                    assert chain.n == links, (chain.n, links)

            def finish():
                end_pair(steps - 1, 1, pairs - 1)
                add_input(steps - 1, 1)
                normalise(steps - 1)

            run_steps(dve, front, body, finish)

        @block.tensor
        def _(pe):
            pe.sem_inc(summed, 4)
            pe.wait_ge(ready, 8)
            pe.wait_ge(heads_loaded, HEADS_LOADED)

            def project_heads(j, b):
                if b == 0:
                    pe.wait_ge(attn_loaded, j * 16 + 16)
                    pe.wait_ge(sum_ready, (j + 1) * group)
                for g in range(chunks):
                    ins = pe.matmul(work[:, b, :], attn[:, b, g, :], wo[:, g, :], start=(g == 0),
                                    stop=(g == chunks - 1))
                ins.then_inc(o_ready, 1)

            def turn(j, par):
                pe.wait_ge(xn_ready, j + 1)
                for b in range(group):
                    for k in range(chunks):
                        ins = pe.transpose(work[:, b, k * P:(k + 1) * P], xn[:, par, b, k * P:(k + 1) * P], ident[:])
                    ins.then_inc(turned, 1)

            def project_in(j, n):
                if n < 2:
                    pe.wait_ge(xn_t_ready, (j + 1) * group)
                else:
                    pe.wait_ge(in_taken, j * in_pairs + n - 1)
                for cc in range(2):
                    col = (2 * n + cc) * P
                    for k in range(chunks):
                        ins = pe.matmul(work[:, n % 2, cc * T:(cc + 1) * T], w_in[:, k, col:col + P],
                                        xn_t[:, k, :], start=(k == 0), stop=(k == chunks - 1))
                ins.then_inc(in_ready, 1)

            def project_x(j, par):
                pe.wait_ge(in_taken, (j + 1) * in_pairs)
                for c in range(inner_chunks):
                    if c % half == 0:
                        pe.wait_ge(u_ready, j * 2 + c // half + 1)
                    ins = pe.matmul(work[:, 0, 0:T], w_x[:, c].rearrange("p w r -> p (w r)"), u[:, par, c, :],
                                    start=(c == 0), stop=(c == inner_chunks - 1))
                ins.then_inc(dbc_product, 1)

            def project_dt(j, h):
                if h == 0:
                    pe.wait_ge(dbc_ready, j + 1)
                    pe.wait_ge(low_ready, j + 1)
                else:
                    pe.wait_ge(t_taken, j * 2 + 1)
                for c in range(half):
                    col = (h * half + c) * P
                    ins = pe.matmul(work[:, c // 2, (c % 2) * T:(c % 2 + 1) * T], w_dt[:, col:col + P],
                                    dt_low[:], start=True, stop=True)
                ins.then_inc(dt_product, 1)

            def spread_bc(i, par, g, which):
                if g == 0:
                    pe.wait_ge(low_ready, i + 1)
                pe.wait_ge(bc_ready, i * 2 * groups + 2 * g + which + 1)
                for s in range(SG):
                    row = rank + which * states + g * SG + s
                    ins = pe.matmul(bc_ps[:, which, s * T:(s + 1) * T],
                                    selector[:, row:row + 1].to_broadcast([P, P]), dbc[:, par, :],
                                    start=True, stop=True)
                ins.then_inc(bc_product, 1)

            def project_out(i, par, p, last):
                pe.wait_ge(y_ready, (i + 1) * pairs + p + 1)
                if p == 0:
                    pe.wait_ge(t_taken, (i + (1 if last else 2)) * 2)
                for b in range(group):
                    for c in (2 * p, 2 * p + 1):
                        ins = pe.matmul(work[:, b, :], gate[:, par, c, b * P:(b + 1) * P], w_out[:, c, :],
                                        start=(c == 0), stop=(c == inner_chunks - 1))
                    if p == pairs - 1:
                        ins.then_inc(out_ready, 1)

            def front(j, par):
                for b in range(group):
                    project_heads(j, b)
                turn(j, par)
                for n in range(in_pairs):
                    if n == 0:
                        pe.wait_ge(x_half_loaded, X_HALF_LOADED)
                    if n == pairs:
                        pe.wait_ge(z_half_loaded, Z_HALF_LOADED)
                    project_in(j, n)
                pe.wait_ge(loaded, LOADED)
                project_x(j, par)
                for h in range(2):
                    project_dt(j, h)
                for g in range(2):
                    for which in range(2):
                        spread_bc(j, par, g, which)

            def body(i, par, first, last):
                j = i + 1
                for m in range(units):
                    g, p = m // pairs, m % pairs
                    if g == 0:
                        pe.wait_ge(y_ready, i * pairs + p + 1)
                    pe.wait_ge(y_part, i * units + m + 1)
                    for s in range(SG):
                        ins = pe.matmul(y_ps[:, p, :], ident[:], drive[:, m % 4, s].rearrange("p c t -> p (c t)"),
                                        start=(g == 0 and s == 0), stop=(g == groups - 1 and s == SG - 1))
                    ins.then_inc(summed, 1)
                    if p in (1, 2) and g + 2 < groups:
                        spread_bc(i, par, g + 2, p - 1)
                    if not first and m in PE_OUT_LAST:
                        project_out(i - 1, 1 - par, 2 + PE_OUT_LAST.index(m), False)
                    if not last:
                        if m in PE_HEADS:
                            project_heads(j, PE_HEADS.index(m))
                        if m == PE_TURN:
                            turn(j, 1 - par)
                        if PE_IN <= m < PE_IN + in_pairs:
                            project_in(j, m - PE_IN)
                        if m == PE_X:
                            project_x(j, 1 - par)
                        if m in PE_DT:
                            project_dt(j, PE_DT.index(m))
                        if p in (1, 2) and g + 2 >= groups:
                            spread_bc(j, 1 - par, g + 2 - groups, p - 1)
                    if m in PE_OUT:
                        project_out(i, par, PE_OUT.index(m), last)

            def finish():
                for p in (2, 3):
                    project_out(steps - 1, 1, p, True)

            run_steps(pe, front, body, finish)


def feed_forward(nc, x1_dram, zm_dram, w1_t, b1, w2_t, b2, norm_w, w_gate, w_shared_t, w_expert_t, bias, out):
    batches, _, width = x1_dram.shape
    hidden = w2_t.shape[0]
    gates = w_gate.shape[1]
    chunks, hidden_chunks = width // P, hidden // P
    group = 4
    steps = batches // group
    T = group * P
    LOWEST = -3.4e38
    assert gates == 7

    with ExitStack() as ctx:
        def sb(name, shape, dt=F32):
            return ctx.enter_context(nc.sbuf_tensor(name, shape, dt))

        def psum(name, shape):
            return ctx.enter_context(nc.psum_tensor(name, shape, F32))

        def sem(name):
            return ctx.enter_context(nc.semaphore(name))

        w1 = sb("c_w1", [P, chunks, hidden])
        w2 = sb("c_w2", [P, hidden_chunks, width])
        w_s, w_e = sb("c_w_s", [P, chunks, width]), sb("c_w_e", [P, chunks, width])
        w_g = sb("c_w_g", [P, chunks, gates])
        b1_sb = sb("c_b1", [P, hidden_chunks])
        b2_sb, norm_sb, bias_sb = sb("c_b2", [P, width]), sb("c_norm", [P, width]), sb("c_bias", [P, width])
        ident = sb("c_ident", [P, P])
        eps_ln, eps_rms = sb("c_eps_ln", [P, 1]), sb("c_eps_rms", [P, 1])
        wait_taker = sb("c_wait_taker", [P, 1])

        zm = sb("c_zm", [P, group, width])
        x1 = sb("c_x1", [P, group, width])
        turned_sb = sb("c_turned_sb", [P, chunks, T])
        h_t = sb("c_h_t", [P, hidden_chunks, T])
        mix = sb("c_mix", [P, group, width])
        xf = sb("c_xf", [P, group, width])
        out_sb = sb("c_out_sb", [P, group, width])
        squares, mean_sq = sb("c_squares", [P, width]), sb("c_mean_sq", [P, group])
        std, rstd = sb("c_std", [P, group]), sb("c_rstd", [P, group])
        stats, moments = sb("c_stats", [P, group, 6]), sb("c_moments", [P, group, 2])
        logits, top = sb("c_logits", [P, group, 8]), sb("c_top", [P, group, 8])
        neg_top, exps, exp_sum = sb("c_neg_top", [P, group]), sb("c_exps", [P, group, 8]), sb("c_exp_sum", [P, group])
        two, two_sum, token_weight = sb("c_two", [P, group, 2]), sb("c_two_sum", [P, group]), sb("c_tw", [P, group])

        ring = psum("c_ring", [P, 4, 512])
        turned_ps = psum("c_turned_ps", [P, 2, 512])
        gate_ps = psum("c_gate_ps", [P, group, 8])

        loaded, ready = sem("c_loaded"), sem("c_ready")
        zm_loaded, x1_loaded = sem("c_zm_loaded"), sem("c_x1_loaded")
        turned, turned_taken = sem("c_turned"), sem("c_turned_taken")
        h_product, h_ready = sem("c_h_product"), sem("c_h_ready")
        mlp_ready, mix_ready, squared, rms_ready = sem("c_mlp"), sem("c_mix_ready"), sem("c_squared"), sem("c_rms")
        x2_ready = sem("c_x2_ready")
        moments_ready, std_ready, xf_ready = sem("c_moments_ready"), sem("c_std_ready"), sem("c_xf_ready")
        gate_ready, logits_ready, exp_ready = sem("c_gate_ready"), sem("c_logits_ready"), sem("c_exp_ready")
        ffn_ready, ffn_taken = sem("c_ffn_ready"), sem("c_ffn_taken")
        out_stored = sem("c_out_stored")
        dve_order = sem("c_dve_order")

        block = ctx.enter_context(nc.Block())
        x1_v, zm_v, out_v = (t.rearrange("(s b) t d -> s t b d", b=group) for t in (x1_dram, zm_dram, out))

        @block.sync
        def _(sp):
            sp.sem_inc(out_stored, 16)
            sp.dma_start(zm[:], zm_v[0]).then_inc(zm_loaded, 16)
            sp.dma_start(w1[:], w1_t.rearrange("(k p) o -> p k o", p=P)).then_inc(loaded, 16)
            sp.dma_start(b1_sb[:], b1).then_inc(loaded, 16)
            sp.dma_start(x1[:], x1_v[0]).then_inc(x1_loaded, 16)
            for dst, src in ((w2[:], w2_t.rearrange("(k p) o -> p k o", p=P)),
                             (w_s[:], w_shared_t.rearrange("(k p) o -> p k o", p=P)),
                             (w_e[:], w_expert_t.rearrange("(k p) o -> p k o", p=P)),
                             (w_g[:], w_gate.rearrange("(k p) o -> p k o", p=P)),
                             (b2_sb[:], b2.partition_broadcast(P)), (norm_sb[:], norm_w.partition_broadcast(P)),
                             (bias_sb[:], bias.partition_broadcast(P))):
                sp.dma_start(dst, src).then_inc(loaded, 16)

            def step(i, last):
                if not last:
                    sp.wait_ge(mix_ready, (i + 1) * group)
                    sp.dma_start(zm[:], zm_v[i + 1]).then_inc(zm_loaded, 16)
                    sp.wait_ge(x2_ready, i + 1)
                    sp.dma_start(x1[:], x1_v[i + 1]).then_inc(x1_loaded, 16)
                sp.wait_ge(ffn_taken, (i + 1) * group + group)
                sp.dma_start(out_v[i], out_sb[:]).then_inc(out_stored, 16)

            with sp.Fori(0, steps - 1) as i:
                step(i, False)
            step(steps - 1, True)
            sp.wait_ge(out_stored, 16 * (steps + 1))

        FIRST_LOADS, ALL_LOADS = 2 * 16, 9 * 16

        @block.gpsimd
        def _(pool):
            pool.memset(ident[:], 0.0).then_inc(ready, 1)
            pool.memset(eps_ln[:], LN_EPS).then_inc(ready, 1)
            pool.memset(eps_rms[:], RMS_EPS).then_inc(ready, 1)
            pool.memset(logits[:], LOWEST).then_inc(ready, 1)
            pool.wait_ge(ready, 4)
            pool.affine_select(out=ident[:], in_=ident[:], compare_op=ALU.not_equal, fill=1.0, base=0,
                               pattern=[[-1, P]], channel_multiplier=1).then_inc(ready, 1)

        @block.scalar
        def _(act):
            act.wait_ge(ready, 5)
            act.wait_ge(loaded, ALL_LOADS)

            def take_turned(i, half):
                for b in range(group):
                    n = half * group + b
                    act.wait_ge(turned, i * 2 * group + n + 1)
                    act.copy(turned_sb[:, :, b * P:(b + 1) * P],
                             turned_ps[:, b % 2, :].rearrange("p (k t) -> p k t", t=P)).then_inc(turned_taken, 1)

            with act.Fori(0, steps) as i:
                take_turned(i, 0)
                for m in range(hidden_chunks):
                    act.wait_ge(h_product, i * hidden_chunks + m + 1)
                    act.activation(h_t[:, m, :], ring[:, m % 4, :], ACT.Gelu,
                                   bias=b1_sb[:, m:m + 1]).then_inc(h_ready, 1)
                for b in range(group):
                    act.wait_ge(mix_ready, i * group + b + 1)
                    act.activation(squares[:], mix[:, b, :], ACT.Square, scale=float(width) ** -0.5,
                                   accum_out=mean_sq[:, b:b + 1]).then_inc(squared, 1)
                    act.wait_ge(squared, i * group + b + 1)
                act.activation(std[:], mean_sq[:], ACT.Sqrt, bias=eps_rms[:, 0:1]).then_inc(rms_ready, 1)
                act.wait_ge(moments_ready, i + 1)
                act.activation(std[:], moments[:, :, 1], ACT.Sqrt, bias=eps_ln[:, 0:1]).then_inc(std_ready, 1)
                take_turned(i, 1)
                act.wait_ge(logits_ready, i + 1)
                for b in range(group):
                    ins = act.activation(exps[:, b, :], top[:, b, :], ACT.Exp, bias=neg_top[:, b:b + 1],
                                         accum_out=exp_sum[:, b:b + 1])
                ins.then_inc(exp_ready, 1)

        @block.vector
        def _(dve):
            chain = Chain(dve, dve_order)
            dve.sem_inc(ffn_taken, group)
            dve.wait_ge(ready, 5)
            dve.wait_ge(loaded, ALL_LOADS)
            links = 2 * group + 13

            def wide(v):
                return v[:].unsqueeze(1).to_broadcast([P, group, width])

            with dve.Fori(0, steps) as i:
                chain.enter(i, links, 0)
                dve.wait_ge(zm_loaded, i * 16 + 16)
                for b in range(group):
                    dve.wait_ge(mlp_ready, i * group + b + 1)
                    chain(dve.tensor_tensor(mix[:, b, :], ring[:, b, :], zm[:, b, :], ALU.add))
                    dve.tensor_tensor(mix[:, b, :], mix[:, b, :], b2_sb[:], ALU.add).then_inc(mix_ready, 1)
                dve.wait_ge(rms_ready, i + 1)
                chain(dve.reciprocal(rstd[:], std[:]))
                for b in range(group):
                    ins = dve.scalar_tensor_tensor(mix[:, b, :], mix[:, b, :], rstd[:, b:b + 1], norm_sb[:],
                                                   ALU.mult, ALU.mult)
                chain(ins)
                dve.wait_ge(x1_loaded, i * 16 + 16)
                dve.tensor_tensor(mix[:], mix[:], x1[:], ALU.add).then_inc(x2_ready, 1)
                dve.wait_ge(x2_ready, i + 1)
                for b in range(group):
                    ins = dve.bn_stats(stats[:, b, :], mix[:, b, :])
                chain(ins)
                dve.memset(wait_taker[:], 0.0)
                for b in range(group):
                    ins = dve.bn_aggr(moments[:, b, :], stats[:, b, :])
                ins.then_inc(moments_ready, 1)
                dve.wait_ge(std_ready, i + 1)
                chain(dve.reciprocal(rstd[:], std[:]))
                for b in range(group):
                    ins = dve.tensor_scalar(xf[:, b, :], mix[:, b, :], moments[:, b, 0:1], rstd[:, b:b + 1],
                                            ALU.subtract, ALU.mult)
                ins.then_inc(xf_ready, 1)
                dve.wait_ge(xf_ready, i + 1)
                chain(dve.tensor_tensor(mix[:], mix[:], wide(bias_sb), ALU.add))
                dve.wait_ge(gate_ready, i + 1)
                chain(dve.tensor_copy(logits[:, :, 0:gates], gate_ps[:, :, 0:gates]))
                dve.memset(wait_taker[:], 0.0)
                for b in range(group):
                    ins = dve.max(out=top[:, b, :], in_=logits[:, b, :])
                chain(ins)
                dve.tensor_scalar(neg_top[:], top[:, :, 0], -1.0, None, ALU.mult).then_inc(logits_ready, 1)
                dve.wait_ge(exp_ready, i + 1)
                chain(dve.reciprocal(exp_sum[:], exp_sum[:]))
                chain(dve.tensor_tensor(two[:], exps[:, :, 0:2], exp_sum[:].unsqueeze(2).to_broadcast([P, group, 2]),
                                        ALU.mult))
                chain(dve.tensor_reduce(two_sum[:], two[:], AX.X, ALU.add))
                chain(dve.reciprocal(two_sum[:], two_sum[:]))
                chain(dve.tensor_tensor(two[:], two[:], two_sum[:].unsqueeze(2).to_broadcast([P, group, 2]), ALU.mult))
                chain(dve.tensor_reduce(token_weight[:], two[:], AX.X, ALU.add))
                dve.wait_ge(out_stored, i * 16 + 16)
                for b in range(group):
                    dve.wait_ge(ffn_ready, i * group + b + 1)
                    s, e = (2 * b) % 4, (2 * b + 1) % 4
                    chain(dve.scalar_tensor_tensor(out_sb[:, b, :], ring[:, e, :], token_weight[:, b:b + 1],
                                                   mix[:, b, :], ALU.mult, ALU.add))
                    ins = dve.tensor_tensor(out_sb[:, b, :], out_sb[:, b, :], ring[:, s, :], ALU.add)
                    ins.then_inc(ffn_taken, 1)
                dve.wait_ge(ffn_taken, (i + 1) * group + group)
            chain.leave(links, steps, 0)

        @block.tensor
        def _(pe):
            pe.sem_inc(turned_taken, 2)
            pe.wait_ge(ready, 5)
            pe.wait_ge(loaded, ALL_LOADS)

            def turn(i, half, src):
                for b in range(group):
                    pe.wait_ge(turned_taken, i * 2 * group + half * group + b + 1)
                    for k in range(chunks):
                        ins = pe.transpose(turned_ps[:, b % 2, k * P:(k + 1) * P], src[:, b, k * P:(k + 1) * P],
                                           ident[:])
                    ins.then_inc(turned, 1)
                pe.wait_ge(turned_taken, i * 2 * group + (half + 1) * group + 2)

            with pe.Fori(0, steps) as i:
                pe.wait_ge(zm_loaded, i * 16 + 16)
                turn(i, 0, zm)
                pe.wait_ge(ffn_taken, i * group + group)
                for m in range(hidden_chunks):
                    if m >= 4:
                        pe.wait_ge(h_ready, i * hidden_chunks + m - 3)
                    for k in range(chunks):
                        ins = pe.matmul(ring[:, m % 4, :], w1[:, k, m * P:(m + 1) * P], turned_sb[:, k, :],
                                        start=(k == 0), stop=(k == chunks - 1))
                    ins.then_inc(h_product, 1)
                pe.wait_ge(h_ready, (i + 1) * hidden_chunks)
                for b in range(group):
                    for m in range(hidden_chunks):
                        ins = pe.matmul(ring[:, b, :], h_t[:, m, b * P:(b + 1) * P], w2[:, m, :],
                                        start=(m == 0), stop=(m == hidden_chunks - 1))
                    ins.then_inc(mlp_ready, 1)
                pe.wait_ge(xf_ready, i + 1)
                turn(i, 1, xf)
                for b in range(group):
                    for k in range(chunks):
                        ins = pe.matmul(gate_ps[:, b, 0:gates], turned_sb[:, k, b * P:(b + 1) * P], w_g[:, k, :],
                                        start=(k == 0), stop=(k == chunks - 1))
                ins.then_inc(gate_ready, 1)
                for b in range(group):
                    if b >= 2:
                        pe.wait_ge(ffn_taken, i * group + b - 1 + group)
                    for bank, w in (((2 * b) % 4, w_s), ((2 * b + 1) % 4, w_e)):
                        for k in range(chunks):
                            ins = pe.matmul(ring[:, bank, :], turned_sb[:, k, b * P:(b + 1) * P], w[:, k, :],
                                            start=(k == 0), stop=(k == chunks - 1))
                    ins.then_inc(ffn_ready, 1)


def perceiver_layer(nc, i, out):
    batches, seq, width = i["x"].shape
    heads_shape = (batches, P, width // P, seq)
    q_dram = nc.dram_tensor("q_scratch", heads_shape, F32).ap()
    attn_dram = nc.dram_tensor("attn_scratch", heads_shape, F32).ap()
    x1_dram = nc.dram_tensor("x1_scratch", (batches, seq, width), F32).ap()
    zm_dram = nc.dram_tensor("zm_scratch", (batches, seq, width), F32).ap()
    project_queries(nc, i["x"], i["xattn_wq"], i["xattn_bq"], q_dram)
    cross_attention(nc, i["ctx"], i["xattn_wk"], i["xattn_wv"], i["xattn_bk"], i["xattn_bv"], q_dram, attn_dram,
                    heads=16)
    mamba(nc, i["x"], attn_dram, i["xattn_wo"], i["xattn_bo"], i["in_proj_w"], i["conv_w"], i["conv_b"],
          i["x_proj_w"], i["dt_proj_w"], i["dt_proj_b"], i["A_log"], i["D"], i["out_proj_w"], i["norm1_w"],
          x1_dram, zm_dram)
    feed_forward(nc, x1_dram, zm_dram, i["mlp_w1"], i["mlp_b1"], i["mlp_w2"], i["mlp_b2"], i["norm1_w"],
                 i["W_gate"], i["W_shared"], i["W_expert"], i["bias"], out)


def kernel(**inputs):
    import concourse.bacc as bacc
    from concourse.bass_utils import run_bass_kernel_spmd

    a = {name.removeprefix("L0_").removeprefix("attn_").removeprefix("ffn_"): np.asarray(v)
         for name, v in inputs.items()}

    def by_channel(v):
        return v.reshape((-1, P) + v.shape[1:]).swapaxes(0, 1)

    laid_out = {
        "x": a["x"],
        "ctx": a["ctx_1024"].transpose(0, 2, 1),
        "xattn_wq": a["xattn_wq"].T, "xattn_wk": a["xattn_wk"].T, "xattn_wv": a["xattn_wv"].T,
        "xattn_wo": a["xattn_wo"].T,
        "xattn_bq": by_channel(a["xattn_bq"]), "xattn_bk": by_channel(a["xattn_bk"]),
        "xattn_bv": by_channel(a["xattn_bv"]), "xattn_bo": a["xattn_bo"],
        "in_proj_w": a["in_proj_w"].T, "conv_w": by_channel(a["conv_w"]), "conv_b": by_channel(a["conv_b"]),
        "x_proj_w": a["x_proj_w"].T, "dt_proj_w": a["dt_proj_w"].T, "dt_proj_b": a["dt_proj_b"][None, :],
        "A_log": by_channel(a["A_log"]), "D": by_channel(a["D"]), "out_proj_w": a["out_proj_w"].T,
        "norm1_w": a["norm1_w"], "mlp_w1": a["mlp_w1"].T, "mlp_b1": by_channel(a["mlp_b1"]),
        "mlp_w2": a["mlp_w2"].T, "mlp_b2": a["mlp_b2"],
        "W_gate": a["W_gate"], "W_shared": a["W_shared"].T, "W_expert": a["W_expert"].T, "bias": a["bias"],
    }
    nc = bacc.Bacc("TRN2", target_bir_lowering=False, num_devices=1)
    arrays, aps = {}, {}
    for name, v in laid_out.items():
        arrays[f"in_{name}"] = np.ascontiguousarray(v)
        aps[name] = nc.dram_tensor(f"in_{name}", v.shape, mybir.dt.from_np(v.dtype), kind="ExternalInput").ap()
    out = nc.dram_tensor("out", a["x"].shape, F32, kind="ExternalOutput").ap()
    perceiver_layer(nc, aps, out)
    r = run_bass_kernel_spmd(nc, [arrays], core_ids=[0])
    return r.results[0]["out"]
```

```python
from contextlib import ExitStack

import numpy as np

import concourse.bass as bass
from concourse import mybir

F32 = mybir.dt.float32
F32R = mybir.dt.float32r
ALU = mybir.AluOpType
ACT = mybir.ActivationFunctionType
AX = mybir.AxisListType

P = 128
LN_EPS = 1e-5
RMS_EPS = 1e-6


class Chain:

    def __init__(self, eng, sem):
        self.eng, self.sem, self.base, self.n = eng, sem, 0, 0

    def __call__(self, ins):
        self.n += 1
        ins.then_inc(self.sem, 1)
        self.eng.wait_ge(self.sem, self.base + self.n)

    def enter(self, i, per_iteration, before):
        self.base, self.n = i * per_iteration + before, 0

    def leave(self, per_iteration, iterations, before):
        assert self.n == per_iteration, (self.n, per_iteration)
        self.base, self.n = 0, before + per_iteration * iterations


def project_queries(nc, x, wq_t, bq, q_dram):
    batches, _, width = x.shape
    chunks = width // P
    group = 4
    steps = batches // group
    T = group * P

    with ExitStack() as ctx:
        def sb(name, shape, dt=F32):
            return ctx.enter_context(nc.sbuf_tensor(name, shape, dt))

        def sem(name):
            return ctx.enter_context(nc.semaphore(name))

        wq = sb("wq_sb", [P, chunks, width])
        wq_hi, wq_lo = sb("wq_hi", [P, chunks, width], F32R), sb("wq_lo", [P, chunks, width], F32R)
        bq_sb = sb("bq_sb", [P, chunks])
        ident = sb("q_ident", [P, P])
        eps, minus_half = sb("q_eps", [P, group]), sb("q_minus_half", [P, group])
        wait_taker = sb("q_wait_taker", [P, 1])
        x_sb = sb("q_x", [P, group, width])
        xn = sb("q_xn", [P, 2, group, width])
        xn_hi, xn_lo = sb("q_xn_hi", [P, chunks, T], F32R), sb("q_xn_lo", [P, chunks, T], F32R)
        q_sb = sb("q_out", [P, group, chunks, P])
        stats = sb("q_stats", [P, group, 6])
        moments = sb("q_moments", [P, group, 2])
        rstd = sb("q_rstd", [P, group])
        turned_ps = ctx.enter_context(nc.psum_tensor("q_turned_ps", [P, 2, T], F32))
        q_ps = ctx.enter_context(nc.psum_tensor("q_ps", [P, 2, T], F32))

        weights_loaded, x_loaded = sem("q_weights_loaded"), sem("q_x_loaded")
        ident_ready, weights_split = sem("q_ident_ready"), sem("q_weights_split")
        moments_ready, rstd_ready = sem("q_moments_ready"), sem("q_rstd_ready")
        xn_ready, turned = sem("q_xn_ready"), sem("q_turned")
        xn_hi_ready, xn_lo_ready = sem("q_xn_hi_ready"), sem("q_xn_lo_ready")
        product_ready, q_ready = sem("q_product_ready"), sem("q_ready")
        q_stored = sem("q_stored")
        dve_order = sem("q_dve_order")

        block = ctx.enter_context(nc.Block())

        def run_steps(eng, body):
            with eng.Fori(0, steps // 2) as k:
                for par in range(2):
                    body(k * 2 + par, par)

        x_v = x.rearrange("(s b) t d -> s t b d", b=group)
        q_v = q_dram.rearrange("(s b) p g t -> s p b g t", b=group)

        @block.sync
        def _(sp):
            sp.sem_inc(q_stored, 16)
            sp.dma_start(x_sb[:], x_v[0]).then_inc(x_loaded, 16)
            sp.dma_start(wq[:], wq_t.rearrange("(k p) o -> p k o", p=P)).then_inc(weights_loaded, 16)
            sp.dma_start(bq_sb[:], bq).then_inc(weights_loaded, 16)

            def step(i, last):
                if not last:
                    sp.wait_ge(xn_ready, i + 1)
                    sp.dma_start(x_sb[:], x_v[i + 1]).then_inc(x_loaded, 16)
                sp.wait_ge(q_ready, (i + 1) * chunks)
                sp.dma_start(q_v[i], q_sb[:]).then_inc(q_stored, 16)

            with sp.Fori(0, steps - 1) as i:
                step(i, False)
            step(steps - 1, True)
            sp.wait_ge(q_stored, 16 * (steps + 1))

        @block.gpsimd
        def _(pool):
            pool.memset(ident[:], 0.0).then_inc(ident_ready, 1)
            pool.memset(eps[:], LN_EPS).then_inc(ident_ready, 1)
            pool.memset(minus_half[:], -0.5).then_inc(ident_ready, 1)
            pool.wait_ge(ident_ready, 3)
            pool.affine_select(out=ident[:], in_=ident[:], compare_op=ALU.not_equal, fill=1.0, base=0,
                               pattern=[[-1, P]], channel_multiplier=1).then_inc(ident_ready, 1)
            with pool.Fori(0, steps) as i:
                pool.wait_ge(moments_ready, i + 1)
                pool.tensor_tensor(rstd[:], moments[:, :, 1], eps[:], ALU.add).then_inc(rstd_ready, 1)
                pool.wait_ge(rstd_ready, i * 2 + 1)
                pool.tensor_tensor(rstd[:], rstd[:], minus_half[:], ALU.pow).then_inc(rstd_ready, 1)

        @block.vector
        def _(dve):
            chain = Chain(dve, dve_order)
            dve.sem_inc(xn_lo_ready, 2)
            LINKS = 1

            def layernorm(i, par):
                dve.wait_ge(x_loaded, i * 16 + 16)
                for b in range(group):
                    ins = dve.bn_stats(stats[:, b, :], x_sb[:, b, :])
                chain(ins)
                dve.memset(wait_taker[:], 0.0)
                for b in range(group):
                    ins = dve.bn_aggr(moments[:, b, :], stats[:, b, :])
                ins.then_inc(moments_ready, 1)
                dve.wait_ge(rstd_ready, i * 2 + 2)
                for b in range(group):
                    ins = dve.tensor_scalar(xn[:, par, b, :], x_sb[:, b, :], moments[:, b, 0:1], rstd[:, b:b + 1],
                                            ALU.subtract, ALU.mult)
                ins.then_inc(xn_ready, 1)

            def low_parts(i):
                for b in range(group):
                    cols = slice(b * P, (b + 1) * P)
                    dve.wait_ge(xn_hi_ready, i * group + b + 1)
                    dve.tensor_tensor(xn_lo[:, :, cols], turned_ps[:, b % 2, :].rearrange("p (k t) -> p k t", t=P),
                                      xn_hi[:, :, cols].bitcast(F32), ALU.subtract).then_inc(xn_lo_ready, 1)

            layernorm(0, 0)
            dve.wait_ge(weights_loaded, 32)
            dve.tensor_copy(wq_hi[:], wq[:]).then_inc(weights_split, 1)
            dve.wait_ge(weights_split, 1)
            dve.tensor_tensor(wq_lo[:], wq[:], wq_hi[:].bitcast(F32), ALU.subtract).then_inc(weights_split, 1)
            before = chain.n

            def body(i, par):
                chain.base, chain.n = i * LINKS + before, 0
                low_parts(i)
                layernorm(i + 1, 1 - par)
                assert chain.n == LINKS

            for i in range(steps - 1):
                body(i, i % 2)
            low_parts(steps - 1)

        @block.scalar
        def _(act):
            act.wait_ge(weights_loaded, 32)
            with act.Fori(0, steps) as i:
                for b in range(group):
                    act.wait_ge(turned, i * group + b + 1)
                    act.copy(xn_hi[:, :, b * P:(b + 1) * P],
                             turned_ps[:, b % 2, :].rearrange("p (k t) -> p k t", t=P)).then_inc(xn_hi_ready, 1)
                act.wait_ge(q_stored, i * 16 + 16)
                for g in range(chunks):
                    act.wait_ge(product_ready, i * chunks + g + 1)
                    act.activation(q_sb[:, :, g, :], q_ps[:, g % 2, :].rearrange("p (b t) -> p b t", t=P),
                                   ACT.Identity, bias=bq_sb[:, g:g + 1]).then_inc(q_ready, 1)

        @block.tensor
        def _(pe):
            pe.wait_ge(ident_ready, 4)

            def body(i, par):
                pe.wait_ge(xn_ready, i + 1)
                for b in range(group):
                    pe.wait_ge(xn_lo_ready, i * group + b + 1)
                    for k in range(chunks):
                        ins = pe.transpose(turned_ps[:, b % 2, k * P:(k + 1) * P],
                                           xn[:, par, b, k * P:(k + 1) * P], ident[:])
                    ins.then_inc(turned, 1)
                pe.wait_ge(xn_lo_ready, (i + 1) * group + 2)
                pe.wait_ge(weights_split, 2)
                for g in range(chunks):
                    if g >= 2:
                        pe.wait_ge(q_ready, i * chunks + g - 1)
                    cols = slice(g * P, (g + 1) * P)
                    for n, (w, a) in enumerate(((wq_hi, xn_hi), (wq_lo, xn_hi), (wq_hi, xn_lo))):
                        for k in range(chunks):
                            ins = pe.matmul(q_ps[:, g % 2, :], w[:, k, cols], a[:, k, :],
                                            start=(n == 0 and k == 0), stop=(n == 2 and k == chunks - 1))
                    ins.then_inc(product_ready, 1)

            run_steps(pe, body)


def cross_attention(nc, ctx_t, wk_t, wv_t, bk, bv, q_dram, attn_dram, heads):
    batches, width, keys = ctx_t.shape
    chunks = width // P
    block_keys = 512
    blocks = keys // block_keys
    per_block = block_keys // P
    tiles = keys // P
    hd = width // heads
    row_tiles = P // hd
    scale = float(hd) ** -0.5
    queries = P
    assert heads == chunks * row_tiles and per_block == chunks and row_tiles == 4
    QW = chunks * queries

    k_per_batch = blocks * chunks
    max_units = blocks * chunks * 2
    exp_units = tiles * 2

    with ExitStack() as ctx:
        def sb(name, shape, dt=F32):
            return ctx.enter_context(nc.sbuf_tensor(name, shape, dt))

        def sem(name):
            return ctx.enter_context(nc.semaphore(name))

        wk_hi, wk_lo = sb("wk_hi", [P, chunks, width], F32R), sb("wk_lo", [P, chunks, width], F32R)
        wv_hi, wv_lo = sb("wv_hi", [P, chunks, width], F32R), sb("wv_lo", [P, chunks, width], F32R)
        c_hi = sb("c_hi", [P, 2, chunks, block_keys], F32R)
        c_lo = sb("c_lo", [P, 2, chunks, block_keys], F32R)
        k_parts = sb("k_parts", [P, 2, chunks, keys], F32R)
        v_sb = sb("v_sb", [P, tiles, width])
        probs = sb("probs", [P, 4, 2, QW])
        prob_sums = sb("prob_sums", [P, chunks, QW])
        q_hi, q_lo = (sb(name, [P, chunks, 2, 2 * queries], F32R) for name in ("q_hi", "q_lo"))
        k_full = probs[:, 0]
        own = (slice(0, P // 2), slice(P // 2, P))
        max_parts = sb("max_parts", [P, row_tiles, chunks, blocks])
        neg_max_pad = sb("neg_max_pad", [P, chunks * row_tiles, hd])
        neg_max = sb("neg_max", [P, QW], F32R)
        c_raw = prob_sums
        neg_max_all = c_hi[:, 1]
        out_sb = sb("attn_out_sb", [P, chunks, queries])
        q_raw = out_sb
        ident = sb("a_ident", [P, P])
        ident_r = sb("ident_r", [P, P], F32R)
        ones_f = sb("ones_f", [P, hd])
        bk_sb, bv_sb = sb("bk_sb", [P, chunks]), sb("bv_sb", [P, chunks])

        scores = ctx.enter_context(nc.psum_tensor("scores", [P, chunks, QW], F32))
        proj = ctx.enter_context(nc.psum_tensor("proj", [P, 2, 512], F32))
        o_acc = ctx.enter_context(nc.psum_tensor("o_acc", [P, QW], F32))
        misc = ctx.enter_context(nc.psum_tensor("misc", [P, QW], F32))

        wk_loaded, wv_loaded, bias_loaded = sem("a_wk_loaded"), sem("a_wv_loaded"), sem("a_bias_loaded")
        q_zeroed = sem("a_q_zeroed")
        weights_split, ident_ready = sem("a_weights_split"), sem("a_ident_ready")
        ctx_loaded = sem("ctx_loaded")
        q_loaded, q_split = sem("q_loaded"), sem("q_split")
        c_hi_ready, c_lo_ready = sem("c_hi_ready"), sem("c_lo_ready")
        proj_ready = sem("proj_ready")
        k_hi_ready = sem("k_hi_ready")
        k_lo_ready = (sem("k_lo_even_ready"), sem("k_lo_odd_ready"))
        v_ready = sem("v_ready")
        max_scores = sem("max_scores")
        max_taken = sem("max_taken")
        pad_ready, pad_turned, neg_max_ready = sem("pad_ready"), sem("pad_turned"), sem("neg_max_ready")
        scores_ready = sem("scores_ready")
        shifted = sem("shifted")
        exp_done = sem("exp_done")
        pv_done = sem("pv_done")
        even_summed, odd_summed = sem("even_summed"), sem("odd_summed")
        neg_max_spread, neg_max_taken = sem("neg_max_spread"), sem("neg_max_taken")
        den_ready, attn_ready = sem("den_ready"), sem("attn_ready")
        attn_stored = sem("attn_stored")
        dve_order = sem("a_dve_order")

        block = ctx.enter_context(nc.Block())
        ctx_v = ctx_t.rearrange("b (k p) s -> b p k s", p=P)

        @block.sync
        def _(sp):
            sp.sem_inc(attn_stored, 16)
            def load(b, s):
                sp.dma_start(c_raw[:], ctx_v[b, :, :, s * block_keys:(s + 1) * block_keys]
                             ).then_inc(ctx_loaded, 16)

            load(0, 0)
            sp.dma_start(v_sb[:, 0:chunks, :], wk_t.rearrange("(k p) o -> p k o", p=P)).then_inc(wk_loaded, 16)
            sp.dma_start(bk_sb[:], bk).then_inc(bias_loaded, 16)
            sp.dma_start(bv_sb[:], bv).then_inc(bias_loaded, 16)
            sp.dma_start(v_sb[:, chunks:2 * chunks, :], wv_t.rearrange("(k p) o -> p k o", p=P)
                         ).then_inc(wv_loaded, 16)
            sp.dma_start(q_raw[:], q_dram[0]).then_inc(q_loaded, 16)

            def batch(i, first, last):
                for s in range(blocks):
                    if s < blocks - 1 or not last:
                        if s == 0 and not first:
                            sp.wait_ge(den_ready, i + 1)
                        sp.wait_ge(c_lo_ready, i * blocks + s + 1)
                        load(*((i, s + 1) if s < blocks - 1 else (i + 1, 0)))
                    if s == 0 and not first:
                        sp.wait_ge(attn_ready, i + 1)
                        sp.dma_start(attn_dram[i - 1], out_sb[:]).then_inc(attn_stored, 16)
                    if s == 1 and not last:
                        if first:
                            sp.wait_ge(q_split, 2)
                        sp.wait_ge(attn_stored, (i + 1) * 16)
                        sp.dma_start(q_raw[:], q_dram[i + 1]).then_inc(q_loaded, 16)

            batch(0, True, False)
            with sp.Fori(1, batches - 1) as i:
                batch(i, False, False)
            batch(batches - 1, False, True)
            sp.wait_ge(attn_ready, batches + 1)
            sp.dma_start(attn_dram[batches - 1], out_sb[:]).then_inc(attn_stored, 16)
            sp.wait_ge(attn_stored, 16 * (batches + 1))

        def k_low(eng, e, n, s, g):
            cols, rows = slice(s * block_keys, (s + 1) * block_keys), own[e]
            eng.wait_ge(k_hi_ready, n * chunks + g + 1)
            eng.tensor_tensor(k_parts[own[1 - e], e, g, cols], k_full[rows, g % 2, :],
                              k_parts[rows, e, g, cols].bitcast(F32), ALU.subtract).then_inc(k_lo_ready[e], 1)

        def head_cols(j):
            return slice((j % 2) * queries, (j % 2 + 1) * queries)

        def by_tensor(u):
            return u % 8 == 3

        def shifts_before(u):
            return sum(not by_tensor(v) for v in range(u))

        shifts = shifts_before(exp_units)
        assert not by_tensor(exp_units - 1) and not by_tensor(exp_units - 2)

        def add_up(eng, done, i, t, pair, last, gs=(0, 1)):
            part = prob_sums[:, 2 * pair + gs[0]:2 * pair + gs[-1] + 1, :]
            new = probs[:, (2 * t + pair) % 4, gs[0]:gs[-1] + 1, :]
            eng.wait_ge(exp_done, i * exp_units + 2 * t + pair + 1)
            if t == 0:
                eng.wait_ge(c_lo_ready, (i + 1) * blocks + (0 if last else 1))
                ones = ones_f[:, 0:1].unsqueeze(2).to_broadcast([P, len(gs), QW])
                ins = eng.tensor_tensor(part, new, ones, ALU.mult)
            else:
                eng.wait_ge(done, i * tiles + t + 2)
                ins = eng.tensor_tensor(part, part, new, ALU.add)
            if gs[-1] == 1:
                ins.then_inc(done, 1)

        @block.gpsimd
        def _(pool):
            pool.memset(ident[:], 0.0).then_inc(ident_ready, 1)
            pool.wait_ge(ident_ready, 1)
            pool.affine_select(out=ident[:], in_=ident[:], compare_op=ALU.not_equal, fill=1.0, base=0,
                               pattern=[[-1, P]], channel_multiplier=1).then_inc(ident_ready, 1)
            pool.memset(neg_max_pad[:], 0.0).then_inc(ident_ready, 1)
            pool.memset(ones_f[:], 1.0).then_inc(ident_ready, 1)
            pool.memset(q_hi[:].bitcast(mybir.dt.uint32), 0).then_inc(q_zeroed, 1)
            pool.memset(q_lo[:].bitcast(mybir.dt.uint32), 0).then_inc(q_zeroed, 1)

            pool.sem_inc(odd_summed, 2)
            pool.sem_inc(k_lo_ready[1], 2)

            def low_part(n, s):
                pool.wait_ge(c_hi_ready, n + 1)
                pool.tensor_tensor(c_lo[:, s % 2], c_raw[:], c_hi[:, s % 2].bitcast(F32),
                                   ALU.subtract).then_inc(c_lo_ready, 1)

            low_part(0, 0)

            def batch(i, last):
                for s in range(blocks):
                    pool.wait_ge(c_lo_ready, i * blocks + s + 1)
                    if s == 0:
                        pool.wait_ge(odd_summed, i * tiles + 2)
                    for g in range(chunks):
                        k_low(pool, 1, i * blocks + s, s, g)
                    pool.wait_ge(k_lo_ready[1], (i * blocks + s + 1) * chunks + 2)
                    if s < blocks - 1 or not last:
                        low_part(i * blocks + s + 1, s + 1)
                for t in range(tiles):
                    if t % 4 == 2:
                        add_up(pool, even_summed, i, t, 0, last)
                    add_up(pool, odd_summed, i, t, 1, last)

            with pool.Fori(0, batches - 1) as i:
                batch(i, False)
            batch(batches - 1, True)

        @block.scalar
        def _(act):
            act.sem_inc(v_ready, chunks)
            act.wait_ge(bias_loaded, 32)

            def batch(i):
                for s in range(blocks):
                    n = i * blocks + s
                    for g in range(chunks):
                        act.wait_ge(proj_ready, n * 2 * chunks + g + 1)
                        for e, rows in enumerate(own):
                            act.activation(k_parts[rows, e, g, s * block_keys:(s + 1) * block_keys],
                                           proj[rows, g % 2, :], ACT.Identity, bias=bk_sb[rows, g:g + 1])
                        if s == 0 and g == 0:
                            act.wait_ge(even_summed, i * tiles + 1)
                            act.wait_ge(pv_done, i * exp_units + 1)
                        for e in range(2):
                            act.wait_ge(k_lo_ready[e], n * chunks + g + 1)
                        act.activation(k_full[:, g % 2, :], proj[:, g % 2, :], ACT.Identity, bias=bk_sb[:, g:g + 1]
                                       ).then_inc(k_hi_ready, 1)
                    for r in range(per_block):
                        act.wait_ge(proj_ready, n * 2 * chunks + chunks + r + 1)
                        act.copy(v_sb[:, s * per_block + r, :], proj[:, r % 2, :]).then_inc(v_ready, 1)
                for g in range(chunks):
                    act.wait_ge(neg_max_spread, i * chunks + g + 1)
                    act.copy(neg_max_all[:, g, :], proj[:, g % 2, :]).then_inc(neg_max_taken, 1)
                for u in range(exp_units):
                    t, pair = u // 2, u % 2
                    if by_tensor(u):
                        act.wait_ge(scores_ready, i * exp_units + u + 1)
                        act.wait_ge(pv_done, i * exp_units + u + 1)
                        act.wait_ge(odd_summed if pair else even_summed, i * tiles + t + 1)
                        source = scores[:, 2 * pair:2 * pair + 2, :]
                    else:
                        act.wait_ge(shifted, i * shifts + shifts_before(u) + 1 + 2)
                        source = probs[:, u % 4]
                    act.activation(probs[:, u % 4], source, ACT.Exp, scale=scale).then_inc(exp_done, 1)

            with act.Fori(0, batches) as i:
                batch(i)

        @block.vector
        def _(dve):
            chain = Chain(dve, dve_order)
            dve.sem_inc(max_taken, 2)
            dve.sem_inc(shifted, 2)
            dve.sem_inc(even_summed, 2)
            dve.sem_inc(attn_ready, 1)
            dve.sem_inc(k_lo_ready[0], 2)
            dve.wait_ge(ident_ready, 4)
            dve.tensor_copy(ident_r[:], ident[:])

            def split_weights(n, loaded, hi, lo):
                dve.wait_ge(loaded, 16)
                raw = v_sb[:, n * chunks:(n + 1) * chunks, :]
                chain(dve.tensor_copy(hi[:], raw))
                dve.tensor_tensor(lo[:], raw, hi[:].bitcast(F32), ALU.subtract).then_inc(weights_split, 1)

            def high_part(n, s):
                dve.wait_ge(ctx_loaded, (n + 1) * 16)
                dve.tensor_copy(c_hi[:, s % 2], c_raw[:]).then_inc(c_hi_ready, 1)

            high_part(0, 0)
            split_weights(0, wk_loaded, wk_hi, wk_lo)
            split_weights(1, wv_loaded, wv_hi, wv_lo)
            dve.wait_ge(q_zeroed, 2)

            def split_queries(i):
                dve.wait_ge(q_loaded, i * 16 + 16)
                for shift in (0, 2):
                    for j in range(row_tiles):
                        to = (j + shift) % row_tiles * hd
                        ins = dve.tensor_copy(q_hi[to:to + hd, :, j // 2, head_cols(j)], q_raw[j * hd:(j + 1) * hd])
                ins.then_inc(q_split, 1)
                dve.wait_ge(q_split, i * 2 + 1)
                for j in range(row_tiles):
                    js = slice(j * hd, (j + 1) * hd)
                    ins = dve.tensor_tensor(q_lo[js, :, j // 2, head_cols(j)], q_raw[js],
                                            q_hi[js, :, j // 2, head_cols(j)].bitcast(F32), ALU.subtract)
                ins.then_inc(q_split, 1)

            def reduce_max(i, s, g):
                for pair in range(2):
                    u = (s * chunks + g) * 2 + pair
                    dve.wait_ge(max_scores, i * max_units + u + 1)
                    dve.tensor_reduce(max_parts[:, 2 * pair:2 * pair + 2, g, s],
                                      scores[:, 2 * pair:2 * pair + 2, :], AX.X,
                                      ALU.max).then_inc(max_taken, 1)

            def divide(i):
                dve.wait_ge(den_ready, i + 2)
                dve.wait_ge(attn_stored, (i + 1) * 16)
                chain(dve.reciprocal(out_sb[:], misc[:].rearrange("p (g q) -> p g q", q=queries)))
                chain(dve.tensor_tensor(out_sb[:], o_acc[:].rearrange("p (g q) -> p g q", q=queries),
                                        out_sb[:], ALU.mult))
                dve.tensor_tensor(out_sb[:], out_sb[:], bv_sb[:].unsqueeze(2).to_broadcast([P, chunks, queries]),
                                  ALU.add).then_inc(attn_ready, 1)

            def batch(i, first, last):
                split_queries(i)
                for s in range(blocks):
                    n = i * blocks + s
                    for g in range(2):
                        k_low(dve, 0, n, s, g)
                    for g in range(chunks):
                        reduce_max(i, s, g)
                        if g + 2 < chunks:
                            k_low(dve, 0, n, s, g + 2)
                        elif g + 2 == chunks and (s < blocks - 1 or not last):
                            if s > 0 or not first:
                                dve.wait_ge(proj_ready, n * 2 * chunks)
                            high_part(n + 1, s + 1)
                    if s == 0 and not first:
                        divide(i - 1)
                dve.wait_ge(max_taken, (i + 1) * max_units + 2)
                dve.tensor_reduce(neg_max_pad[:, :, 0], max_parts[:].rearrange("p j g s -> p (j g) s"),
                                  AX.X, ALU.max, negate=True).then_inc(pad_ready, 1)
                dve.wait_ge(pad_turned, i + 1)
                dve.tensor_copy(neg_max[:], misc[:]).then_inc(neg_max_ready, 1)
                for u in range(exp_units):
                    t, pair = u // 2, u % 2
                    if t == 0:
                        dve.wait_ge(neg_max_taken, i * chunks + 2 * pair + 2)
                    if not by_tensor(u):
                        dve.wait_ge(scores_ready, i * exp_units + u + 1)
                        dve.wait_ge(pv_done, i * exp_units + u + 1)
                        dve.wait_ge(odd_summed if pair else even_summed, i * tiles + t + 1)
                        dve.tensor_tensor(probs[:, u % 4], scores[:, 2 * pair:2 * pair + 2, :],
                                          neg_max_all[:, 2 * pair:2 * pair + 2, :].bitcast(F32),
                                          ALU.add).then_inc(shifted, 1)
                    if t > 0 and (t - 1) % 4 != 2:
                        add_up(dve, even_summed, i, t - 1, 0, last, gs=(pair,))
                add_up(dve, even_summed, i, tiles - 1, 0, last)

            batch(0, True, False)
            before = chain.n
            with dve.Fori(1, batches - 1) as i:
                chain.enter(i - 1, 2, before)
                batch(i, False, False)
            chain.leave(2, batches - 2, before)
            batch(batches - 1, False, True)
            divide(batches - 1)

        @block.tensor
        def _(pe):
            pe.sem_inc(pv_done, 4)
            pe.sem_inc(den_ready, 1)
            pe.wait_ge(ident_ready, 4)
            pe.wait_ge(weights_split, 1)

            def project(out, products):
                steps = [(lhs(k), rhs(k)) for lhs, rhs in products for k in range(chunks)]
                for m, (lhs, rhs) in enumerate(steps):
                    ins = pe.matmul(out, lhs, rhs, start=(m == 0), stop=(m == len(steps) - 1))
                ins.then_inc(proj_ready, 1)

            def project_k(i, s, g):
                n, slot = i * blocks + s, s % 2
                if g == 0:
                    pe.wait_ge(c_hi_ready, n + 1)
                    pe.wait_ge(c_lo_ready, n + 1)
                if g < 2:
                    pe.wait_ge(v_ready, n * chunks + g + 3)
                else:
                    pe.wait_ge(k_hi_ready, n * chunks + g - 1)
                gs = slice(g * P, (g + 1) * P)
                project(proj[:, g % 2, :], [
                    (lambda k: wk_hi[:, k, gs], lambda k: c_hi[:, slot, k, :]),
                    (lambda k: wk_lo[:, k, gs], lambda k: c_hi[:, slot, k, :]),
                    (lambda k: wk_hi[:, k, gs], lambda k: c_lo[:, slot, k, :])])

            def project_v(i, s, r):
                n, slot = i * blocks + s, s % 2
                pe.wait_ge(weights_split, 2)
                if r < 2:
                    pe.wait_ge(k_hi_ready, n * chunks + r + 3)
                else:
                    pe.wait_ge(v_ready, n * chunks + r - 1 + chunks)
                rs = slice(r * P, (r + 1) * P)
                project(proj[:, r % 2, :], [
                    (lambda k: c_hi[:, slot, k, rs], lambda k: wv_hi[:, k, :]),
                    (lambda k: c_hi[:, slot, k, rs], lambda k: wv_lo[:, k, :]),
                    (lambda k: c_lo[:, slot, k, rs], lambda k: wv_hi[:, k, :])])

            def score_for_max(i, s, g):
                if s == 0 and g == 0:
                    pe.wait_ge(q_split, i * 2 + 2)
                    pe.wait_ge(shifted, i * shifts + 2)
                for e in range(2):
                    pe.wait_ge(k_lo_ready[e], (i * blocks + s) * chunks + g + 1 + 2)
                for pair in range(2):
                    u = (s * chunks + g) * 2 + pair
                    pe.wait_ge(max_taken, i * max_units + u + 1)
                    for j in (2 * pair, 2 * pair + 1):
                        ins = pe.matmul(scores[:, j, :], q_hi[:, g, j // 2, head_cols(j)],
                                        k_parts[:, j // 2, g, s * block_keys:(s + 1) * block_keys],
                                        start=True, stop=True)
                    ins.then_inc(max_scores, 1)

            def turn_neg_max(i):
                pe.wait_ge(pad_ready, i + 1)
                for j in range(row_tiles):
                    ins = pe.transpose(misc[:, j * P:(j + 1) * P],
                                       neg_max_pad[:, j * chunks:(j + 1) * chunks, :].rearrange(
                                           "p g d -> p (g d)"), ident[:])
                ins.then_inc(pad_turned, 1)

            def spread_neg_max(i, g):
                if g == 0:
                    pe.wait_ge(neg_max_ready, i + 1)
                if g < 2:
                    pe.wait_ge(v_ready, (i + 1) * k_per_batch + g + chunks - 1)
                else:
                    pe.wait_ge(neg_max_taken, i * chunks + g - 1)
                pe.matmul(proj[:, g % 2, :], ident_r[:, g * hd:g * hd + 1].to_broadcast([P, P]), neg_max[:],
                          start=True, stop=True).then_inc(neg_max_spread, 1)

            def score_unit(i, u):
                t, pair = u // 2, u % 2
                ts = slice(t * P, (t + 1) * P)
                if u == 0:
                    pe.wait_ge(max_taken, (i + 1) * max_units + 2)
                elif u >= 2 and by_tensor(u - 2):
                    pe.wait_ge(exp_done, i * exp_units + u - 1)
                elif u >= 2:
                    pe.wait_ge(shifted, i * shifts + shifts_before(u - 2) + 1 + 2)
                for g in (2 * pair, 2 * pair + 1):
                    if by_tensor(u):
                        pe.matmul(scores[:, g, :], ident_r[:, g * hd:g * hd + 1].to_broadcast([P, P]), neg_max[:],
                                  start=True, stop=False)
                    for e in range(2):
                        for step, q_part in enumerate((q_hi, q_lo)):
                            ins = pe.matmul(scores[:, g, e * 2 * queries:(e + 1) * 2 * queries],
                                            k_parts[:, e, g, ts], q_part[:, g, e, :], start=(step == 0 and not by_tensor(u)),
                                            stop=(step == 1 and (e == 1 or not by_tensor(u))))
                ins.then_inc(scores_ready, 1)

            def values(i, u):
                t, pair = u // 2, u % 2
                if u == 0:
                    pe.wait_ge(attn_ready, i + 1)
                    pe.wait_ge(v_ready, (i + 1) * k_per_batch + chunks)
                pe.wait_ge(exp_done, i * exp_units + u + 1)
                for g in (2 * pair, 2 * pair + 1):
                    for j in range(row_tiles):
                        h = g * row_tiles + j
                        ins = pe.matmul(o_acc[j * hd:(j + 1) * hd, g * queries:(g + 1) * queries],
                                        v_sb[:, t, h * hd:(h + 1) * hd],
                                        probs[:, u % 4, g % 2, j * queries:(j + 1) * queries],
                                        start=(u == 0 and g == 0), stop=(t == tiles - 1),
                                        skip_group_check=True, tile_position=(0, j * hd))
                ins.then_inc(pv_done, 1)

            def sum_over_keys(i):
                pe.wait_ge(even_summed, (i + 1) * tiles + 2)
                pe.wait_ge(odd_summed, (i + 1) * tiles + 2)
                for j in range(row_tiles):
                    ins = pe.matmul(misc[j * hd:(j + 1) * hd, :], ones_f[:],
                                    prob_sums[:, :, j * queries:(j + 1) * queries],
                                    start=True, stop=True, tile_position=(0, j * hd))
                ins.then_inc(den_ready, 1)

            def batch(i, first):
                for s in range(blocks):
                    project_k(i, s, 0)
                    if s == 0 and not first:
                        for u in range(exp_units - LAG, exp_units):
                            values(i - 1, u)
                    project_k(i, s, 1)
                    if s == 0 and not first:
                        sum_over_keys(i - 1)
                    for g in range(2, chunks):
                        project_k(i, s, g)
                        score_for_max(i, s, g - 2)
                    for r in range(2):
                        project_v(i, s, r)
                        score_for_max(i, s, r + 2)
                    project_v(i, s, 2)
                    if s == blocks - 1:
                        turn_neg_max(i)
                    project_v(i, s, 3)
                for u in range(exp_units):
                    score_unit(i, u)
                    if u < 2:
                        for g in (2 * u, 2 * u + 1):
                            spread_neg_max(i, g)
                    if u >= LAG:
                        values(i, u - LAG)

            LAG = 2
            batch(0, True)
            with pe.Fori(1, batches) as i:
                batch(i, False)
            for u in range(exp_units - LAG, exp_units):
                values(batches - 1, u)
            sum_over_keys(batches - 1)


def mamba(nc, x, attn_dram, wo_t, bo, w_in_t, conv_w, conv_b, w_x_t, w_dt_t, dt_b, a_log, d_skip,
          w_out_t, norm_w, x1_dram, zm_dram):
    batches, seq, width = x.shape
    inner = w_out_t.shape[0]
    taps = conv_w.shape[2]
    rank = w_dt_t.shape[0]
    states = a_log.shape[2]
    chunks, inner_chunks = width // P, inner // P
    group = 2
    steps = batches // group
    T = group * seq
    pairs = inner_chunks // 2
    in_pairs = 2 * pairs
    SG = 2
    groups = states // SG
    units = groups * pairs
    rows = rank + 2 * states
    bc_slots = 4
    half = inner_chunks // 2
    assert seq == P and inner_chunks == 2 * chunks == 8 and 2 * rows == P and pairs == 4
    assert steps % 2 == 0 and rank % 32 == 0

    PE_OUT_LAST, PE_HEADS, PE_TURN, PE_IN, PE_X, PE_DT, PE_OUT = (0, 1), (1, 3), 7, 7, 18, (20, 23), (29, 30)
    POOL_OUT_RSTD, POOL_RSTD = 8, 7
    ACT_SQUARES, ACT_XN_T, ACT_IN, ACT_U, ACT_GATE, ACT_DBC, ACT_EXP, ACT_LOG = 6, 9, 11, 15, 19, 21, (26, 27), (27, 29)
    DVE_SUM, DVE_X1, DVE_XN, DVE_ZM, DVE_CONV, DVE_LOW = 4, (4, 6), 7, 8, 11, 21
    DVE_T, DVE_ONE_PLUS, DVE_DT, DVE_DT_U = (23, 25), (25, 27), (27, 29), 28

    with ExitStack() as ctx:
        def sb(name, shape, dt=F32):
            return ctx.enter_context(nc.sbuf_tensor(name, shape, dt))

        def psum(name, shape):
            return ctx.enter_context(nc.psum_tensor(name, shape, F32))

        def sem(name):
            return ctx.enter_context(nc.semaphore(name))

        wo = sb("b_wo", [P, chunks, width])
        w_in = sb("b_w_in", [P, chunks, 2 * inner])
        w_x = sb("b_w_x", [P, inner_chunks, 2, rows])
        w_dt = sb("b_w_dt", [rank + 1, inner])
        w_out = sb("b_w_out", [P, inner_chunks, width])
        bo_sb, norm_sb = sb("b_bo", [P, width]), sb("b_norm", [P, width])
        conv_w_sb, conv_b_sb = sb("b_conv_w", [P, inner_chunks, taps]), sb("b_conv_b", [P, inner_chunks])
        a_neg, d_sb = sb("b_a", [P, inner_chunks, states]), sb("b_d", [P, inner_chunks])
        ident = sb("b_ident", [P, P])
        selector = sb("b_selector", [P, rows], F32R)

        attn = sb("b_attn", [P, group, chunks, P])
        x1 = sb("b_x1", [P, group, width])
        xn = sb("b_xn", [P, 2, group, width])
        xn_t = sb("b_xn_t", [P, chunks, T])
        padded = sb("b_padded", [P, 2, 2 * group, taps - 1 + seq])
        u = sb("b_u", [P, 2, inner_chunks, T])
        gate = sb("b_gate", [P, 2, inner_chunks, T])
        dbc = sb("b_dbc", [P, 2, T], F32R)
        dt_low = sb("b_dt_low", [rank + 1, T])
        dt = sb("b_dt", [P, 2, inner_chunks, T])
        dt_u = sb("b_dt_u", [P, inner_chunks, T])
        bc = sb("b_bc", [P, bc_slots, 2, SG, T])
        mix = sb("b_mix", [P, group, width])
        exp_neg = (xn_t[:].rearrange("p c (b t) -> p (c b) t", t=seq), mix[:].rearrange("p b (c t) -> p (b c) t", t=seq))
        one_plus = padded[:].rearrange("p n r t -> p (n r) t")[:, :, taps - 1:]
        squares = padded[:, 0, :, taps - 1:]
        decay = sb("b_decay", [P, 2, SG, 2, group, seq])
        drive = sb("b_drive", [P, 4, SG, 2, T])
        state = sb("b_state", [P, 2, SG, 2, T])
        stats, moments = sb("b_stats", [P, group, 6]), sb("b_moments", [P, group, 2])
        eps_ln, eps_rms = sb("b_eps_ln", [P, group]), sb("b_eps_rms", [P, group])
        minus_half = sb("b_minus_half", [P, group])
        wait_taker = sb("b_wait_taker", [P, 1])
        rstd, out_rstd, mean_sq = sb("b_rstd", [P, group]), sb("b_out_rstd", [P, group]), sb("b_mean_sq", [P, group])

        y_ps = psum("b_y", [P, pairs, 512])
        work = psum("b_work", [P, 2, 512])
        bc_ps = psum("b_bc_ps", [P, 2, 512])

        ready = sem("b_ready")
        wo_loaded, bo_loaded, loaded = sem("b_wo_loaded"), sem("b_bo_loaded"), sem("b_loaded")
        x_half_loaded, z_half_loaded = sem("b_x_half_loaded"), sem("b_z_half_loaded")
        attn_loaded, x_loaded = sem("b_attn_loaded"), sem("b_x_loaded")
        o_ready, x1_ready, x1_stored = sem("b_o_ready"), sem("b_x1_ready"), sem("b_x1_stored")
        xn_ready, turned, xn_t_ready = sem("b_xn_ready"), sem("b_turned_ready"), sem("b_xn_t_ready")
        in_ready, in_taken = sem("b_in_ready"), sem("b_in_taken")
        conv_ready, u_ready = sem("b_conv_ready"), sem("b_u_ready")
        gate_ready = sem("b_gate_ready")
        dbc_product, dbc_ready, low_ready = sem("b_dbc_product"), sem("b_dbc_ready"), sem("b_low_ready")
        dt_product, t_taken = sem("b_dt_product"), sem("b_t_taken")
        exp_ready, one_plus_ready, log_ready = sem("b_exp_ready"), sem("b_one_plus"), sem("b_log_ready")
        dt_ready, dt_u_ready = sem("b_dt_ready"), sem("b_dt_u_ready")
        bc_product, bc_ready = sem("b_bc_product"), sem("b_bc_ready")
        decay_ready = sem("b_decay_ready")
        drive_ready = sem("b_drive_ready")
        scanned = sem("b_scanned")
        y_part = sem("b_y_part")
        summed = sem("b_summed")
        y_ready = sem("b_y_ready")
        out_ready, sum_ready = sem("b_out_ready"), sem("b_sum_ready")
        squared, zm_ready, zm_stored = sem("b_squared"), sem("b_zm_ready"), sem("b_zm_stored")
        moments_ready, rstd_ready, out_rstd_ready = sem("b_moments_ready"), sem("b_rstd_ready"), sem("b_out_rstd")
        dve_order = sem("b_dve_order")

        block = ctx.enter_context(nc.Block())
        attn_v = attn_dram.rearrange("(s b) p g t -> s p b g t", b=group)
        x_v, x1_v, zm_v = (t.rearrange("(s b) t d -> s t b d", b=group) for t in (x, x1_dram, zm_dram))

        def by_row(tokens):
            return tokens.rearrange("p c (b t) -> p (c b) t", t=seq)

        def run_steps(eng, front, body, finish):
            front(0, 0)
            body(0, 0, True, False)
            with eng.Fori(0, (steps - 2) // 2) as k:
                body(k * 2 + 1, 1, False, False)
                body(k * 2 + 2, 0, False, False)
            body(steps - 1, 1, False, True)
            finish()

        @block.sync
        def _(sp):
            sp.sem_inc(zm_stored, 32)
            sp.dma_start(attn[:], attn_v[0]).then_inc(attn_loaded, 16)
            sp.dma_start(wo[:], wo_t.rearrange("(k p) o -> p k o", p=P)).then_inc(wo_loaded, 16)
            sp.dma_start(x1[:], x_v[0]).then_inc(x_loaded, 16)
            sp.dma_start(bo_sb[:], bo.partition_broadcast(P)).then_inc(bo_loaded, 16)
            w_in_v = w_in_t.rearrange("(k p) o -> p k o", p=P)
            for part in range(2):
                cols = slice(part * inner, (part + 1) * inner)
                sp.dma_start(w_in[:, :, cols], w_in_v[:, :, cols]).then_inc((x_half_loaded, z_half_loaded)[part], 16)
                if part == 0:
                    sp.dma_start(conv_w_sb[:], conv_w).then_inc(x_half_loaded, 16)
                    sp.dma_start(conv_b_sb[:], conv_b).then_inc(x_half_loaded, 16)
            w_x_v = w_x_t.rearrange("(k p) o -> p k o", p=P)
            for dst, src in ((w_x[:, :, 0, :], w_x_v), (w_x[:, :, 1, :], w_x_v),
                             (w_dt[0:rank, :], w_dt_t), (w_dt[rank:rank + 1, :], dt_b),
                             (a_neg[:], a_log), (d_sb[:], d_skip),
                             (norm_sb[:], norm_w.partition_broadcast(P)),
                             (w_out[:], w_out_t.rearrange("(k p) o -> p k o", p=P))):
                sp.dma_start(dst, src).then_inc(loaded, 16)

            def step(j, first, last):
                if not last:
                    sp.wait_ge(o_ready, (j + 1) * group)
                    sp.dma_start(attn[:], attn_v[j + 1]).then_inc(attn_loaded, 16)
                sp.wait_ge(xn_ready, j + 1)
                sp.dma_start(x1_v[j], x1[:]).then_inc(x1_stored, 16)
                if not first:
                    sp.wait_ge(zm_ready, j - 1)
                    sp.dma_start(zm_v[j - 2], mix[:]).then_inc(zm_stored, 16)
                if not last:
                    sp.wait_ge(x1_stored, (j + 1) * 16)
                    sp.dma_start(x1[:], x_v[j + 1]).then_inc(x_loaded, 16)

            step(0, True, False)
            step(1, True, False)
            with sp.Fori(2, steps - 1) as j:
                step(j, False, False)
            step(steps - 1, False, True)
            for t in (steps - 2, steps - 1):
                sp.wait_ge(zm_ready, t + 1)
                sp.dma_start(zm_v[t], mix[:]).then_inc(zm_stored, 16)
            sp.wait_ge(x1_stored, 16 * steps)
            sp.wait_ge(zm_stored, 16 * (steps + 2))

        X_HALF_LOADED, Z_HALF_LOADED, LOADED = 3 * 16, 16, 8 * 16

        @block.gpsimd
        def _(pool):
            pool.memset(ident[:], 0.0).then_inc(ready, 1)
            pool.wait_ge(ready, 1)
            pool.affine_select(out=ident[:], in_=ident[:], compare_op=ALU.not_equal, fill=1.0, base=0,
                               pattern=[[-1, P]], channel_multiplier=1).then_inc(ready, 1)
            pool.memset(eps_ln[:], LN_EPS).then_inc(ready, 1)
            pool.memset(eps_rms[:], RMS_EPS).then_inc(ready, 1)
            pool.memset(padded[:], 0.0).then_inc(ready, 1)
            pool.memset(decay[:], 0.0).then_inc(ready, 1)
            pool.memset(minus_half[:], -0.5).then_inc(ready, 1)
            pool.wait_ge(ready, 7)
            pool.memset(dt_low[rank:rank + 1, :], 1.0).then_inc(ready, 1)
            pool.wait_ge(ready, 8)

            def make_rstd(n, out, variance, eps, done):
                pool.tensor_tensor(out[:], variance, eps[:], ALU.add).then_inc(done, 1)
                pool.wait_ge(done, n * 2 + 1)
                pool.tensor_tensor(out[:], out[:], minus_half[:], ALU.pow).then_inc(done, 1)

            def norm_rstd(j):
                pool.wait_ge(moments_ready, (j + 1) * group)
                make_rstd(j, rstd, moments[:, :, 1], eps_ln, rstd_ready)

            def out_norm_rstd(t):
                pool.wait_ge(squared, (t + 1) * group)
                make_rstd(t, out_rstd, mean_sq[:], eps_rms, out_rstd_ready)

            def body(i, par, first, last):
                for m in range(units):
                    g, p = m // pairs, m % pairs
                    if g == 0:
                        pool.wait_ge(dt_u_ready, i * pairs + p + 1)
                    if p == 0:
                        pool.wait_ge(bc_ready, i * 2 * groups + 2 * g + 1 + 2)
                    pool.wait_ge(summed, i * units + m + 1)
                    pool.tensor_tensor(
                        drive[:, m % 4], dt_u[:, 2 * p:2 * p + 2, :].unsqueeze(1).to_broadcast([P, SG, 2, T]),
                        bc[:, g % bc_slots, 0].unsqueeze(2).to_broadcast([P, SG, 2, T]), ALU.mult
                    ).then_inc(drive_ready, 1)
                    if not first and m == POOL_OUT_RSTD:
                        out_norm_rstd(i - 1)
                    if not last and m == POOL_RSTD:
                        norm_rstd(i + 1)

            run_steps(pool, lambda j, par: norm_rstd(j), body, lambda: out_norm_rstd(steps - 1))

        @block.scalar
        def _(act):
            act.wait_ge(ready, 8)

            def take_squares(t):
                for b in range(group):
                    act.wait_ge(sum_ready, t * group + b + 1 + 2 * group)
                    act.activation(squares, mix[:, b, :].rearrange("p (c t) -> p c t", t=seq), ACT.Square, scale=float(width) ** -0.5,
                                   accum_out=mean_sq[:, b:b + 1]).then_inc(squared, 1)
                    act.wait_ge(squared, t * group + b + 1)

            def take_turned(j):
                for b in range(group):
                    act.wait_ge(turned, j * group + b + 1)
                    act.copy(xn_t[:, :, b * P:(b + 1) * P],
                             work[:, b, :].rearrange("p (k t) -> p k t", t=P)).then_inc(xn_t_ready, 1)

            def take_in(j, par, n):
                act.wait_ge(in_ready, j * in_pairs + n + 1)
                if n < pairs:
                    act.wait_ge(conv_ready, j * pairs + n + 1)
                    act.copy(padded[:, n % 2, :, taps - 1:],
                             work[:, n % 2, :].rearrange("p (r t) -> p r t", t=seq)).then_inc(in_taken, 1)
                else:
                    if n == pairs:
                        act.wait_ge(sum_ready, (j + 1) * group)
                    c = 2 * (n - pairs)
                    act.copy(gate[:, par, c:c + 2, :],
                             work[:, n % 2, :].rearrange("p (c t) -> p c t", t=T)).then_inc(in_taken, 1)

            def silu_u(j, par, h):
                act.wait_ge(conv_ready, j * pairs + (h + 1) * pairs // 2 + 2)
                for c in range(h * half, (h + 1) * half):
                    ins = act.activation(u[:, par, c, :], u[:, par, c, :], ACT.Silu, bias=conv_b_sb[:, c:c + 1])
                ins.then_inc(u_ready, 1)

            def silu_gate(j, par):
                act.wait_ge(in_taken, (j + 1) * in_pairs)
                act.activation(gate[:, par], gate[:, par], ACT.Silu).then_inc(gate_ready, 1)

            def take_dbc(j, par):
                act.wait_ge(dbc_product, j + 1)
                act.copy(dt_low[0:rank, :], work[0:rank, 0, 0:T])
                act.copy(dbc[:, par, :], work[:, 0, 0:T]).then_inc(dbc_ready, 1)

            def exp_of_abs(j, par, h):
                act.wait_ge(t_taken, j * 2 + h + 1)
                if h == 1:
                    act.wait_ge(zm_stored, (j + 1) * 16)
                act.activation(exp_neg[h], by_row(dt[:, par, h * half:(h + 1) * half, :]), ACT.Abs).then_inc(exp_ready, 1)
                act.wait_ge(exp_ready, j * 4 + 2 * h + 1)
                act.activation(exp_neg[h], exp_neg[h], ACT.Exp, scale=-1.0).then_inc(exp_ready, 1)

            def log(j, h):
                act.wait_ge(one_plus_ready, j * 4 + 2 * h + 2)
                act.activation(one_plus, one_plus, ACT.Ln).then_inc(log_ready, 1)

            def take_bc(i, g, which):
                act.wait_ge(bc_product, i * 2 * groups + 2 * g + which + 1)
                act.copy(bc[:, g % bc_slots, which], bc_ps[:, which, :].rearrange("p (s t) -> p s t", t=T)
                         ).then_inc(bc_ready, 1)

            def front(j, par):
                take_turned(j)
                for n in range(in_pairs):
                    take_in(j, par, n)
                    if n == pairs:
                        act.wait_ge(x_half_loaded, X_HALF_LOADED)
                        for h in range(2):
                            silu_u(j, par, h)
                silu_gate(j, par)
                take_dbc(j, par)
                for h in range(2):
                    exp_of_abs(j, par, h)
                    log(j, h)
                for which in range(2):
                    take_bc(j, 0, which)
                act.wait_ge(loaded, LOADED)
                act.activation(a_neg[:], a_neg[:], ACT.Exp, bias=0.0).then_inc(ready, 1)
                act.wait_ge(ready, 11)

            def body(i, par, first, last):
                j = i + 1
                for m in range(units):
                    g, p = m // pairs, m % pairs
                    act.wait_ge(scanned, i * units + m + 1)
                    if g == 0:
                        act.wait_ge(dt_ready, i * 2 + p // 2 + 1)
                    for s in range(SG):
                        for cc in range(2):
                            c = 2 * p + cc
                            ins = act.activation(
                                decay[:, m % 2, s, cc, :, 1:],
                                dt[:, par, c, :].rearrange("p (b t) -> p b t", t=seq)[:, :, 1:], ACT.Exp,
                                scale=a_neg[:, c, g * SG + s:g * SG + s + 1])
                    ins.then_inc(decay_ready, 1)
                    if m % pairs < 2 and not (last and g == groups - 1):
                        if not first or g > 2:
                            act.wait_ge(y_part, i * units + (g - 2) * pairs)
                        if g < groups - 1:
                            take_bc(i, g + 1, m % pairs)
                        else:
                            take_bc(j, 0, m % pairs)
                    if not first and m == ACT_SQUARES:
                        take_squares(i - 1)
                    if last:
                        continue
                    if m == ACT_XN_T:
                        take_turned(j)
                    if ACT_IN <= m < ACT_IN + in_pairs:
                        take_in(j, 1 - par, m - ACT_IN)
                    if m == ACT_U:
                        for h in range(2):
                            silu_u(j, 1 - par, h)
                    if m == ACT_GATE:
                        silu_gate(j, 1 - par)
                    if m == ACT_DBC:
                        take_dbc(j, 1 - par)
                    if m in ACT_EXP:
                        exp_of_abs(j, 1 - par, ACT_EXP.index(m))
                    if m in ACT_LOG:
                        log(j, ACT_LOG.index(m))

            act.sem_inc(bc_ready, 2)
            run_steps(act, front, body, lambda: take_squares(steps - 1))

        TAIL_LINKS, FRONT_LINKS, END_LINKS = 0, 2 * group + pairs * 2 * (taps - 1) + 2, pairs

        @block.vector
        def _(dve):
            chain = Chain(dve, dve_order)
            dve.sem_inc(scanned, 2)
            dve.sem_inc(conv_ready, 2)
            dve.sem_inc(y_ready, pairs)
            dve.sem_inc(sum_ready, 2 * group)
            dve.wait_ge(ready, 8)
            dve.tensor_tensor(selector[:], ident[:, 0:rows], ident[:, rows:2 * rows], ALU.add).then_inc(ready, 1)
            dve.wait_ge(bo_loaded, 16)

            def add_heads(j, b):
                if b == 0:
                    dve.wait_ge(x_loaded, j * 16 + 16)
                dve.wait_ge(o_ready, j * group + b + 1)
                chain(dve.tensor_tensor(x1[:, b, :], work[:, b, :], x1[:, b, :], ALU.add))
                dve.tensor_tensor(x1[:, b, :], x1[:, b, :], bo_sb[:], ALU.add).then_inc(x1_ready, 1)
                dve.wait_ge(x1_ready, j * group + b + 1)
                chain(dve.bn_stats(stats[:, b, :], x1[:, b, :]))
                dve.memset(wait_taker[:], 0.0)
                dve.bn_aggr(moments[:, b, :], stats[:, b, :]).then_inc(moments_ready, 1)

            def layernorm(j, par):
                dve.wait_ge(rstd_ready, j * 2 + 2)
                for b in range(group):
                    ins = dve.tensor_scalar(xn[:, par, b, :], x1[:, b, :], moments[:, b, 0:1], rstd[:, b:b + 1],
                                            ALU.subtract, ALU.mult)
                ins.then_inc(xn_ready, 1)

            def convolve(j, par, p):
                dve.wait_ge(in_taken, j * in_pairs + p + 1)
                for c in (2 * p, 2 * p + 1):
                    r = (c % 2) * group
                    out = u[:, par, c, :].rearrange("p (b t) -> p b t", t=seq)
                    for k in range(taps):
                        src = padded[:, p % 2, r:r + group, k:k + seq]
                        tap = conv_w_sb[:, c, k:k + 1]
                        if k == 0:
                            ins = dve.tensor_scalar(out, src, tap, None, ALU.mult)
                        else:
                            ins = dve.scalar_tensor_tensor(out, src, tap, out, ALU.mult, ALU.add)
                        if k < taps - 1:
                            chain(ins)
                ins.then_inc(conv_ready, 1)

            def take_low(j, par):
                dve.wait_ge(dbc_ready, j + 1)
                dve.tensor_tensor(dbc[rows:2 * rows, par, :], work[rows:2 * rows, 0, 0:T],
                                  dbc[rows:2 * rows, par, :].bitcast(F32), ALU.subtract).then_inc(low_ready, 1)

            def take_t(j, par, h):
                dve.wait_ge(dt_product, j * 2 + h + 1)
                dve.tensor_copy(dt[:, par, h * half:(h + 1) * half, :],
                                work[:].rearrange("p r (c t) -> p (r c) t", t=T)).then_inc(t_taken, 1)

            def add_one(j, h):
                dve.wait_ge(exp_ready, j * 4 + 2 * h + 2)
                if h == 1:
                    dve.wait_ge(dt_ready, j * 2 + 1)
                dve.tensor_scalar(one_plus, exp_neg[h], 1.0, None, ALU.add).then_inc(one_plus_ready, 1)
                dve.wait_ge(one_plus_ready, j * 4 + 2 * h + 1)
                dve.scalar_tensor_tensor(exp_neg[h], one_plus, -1.0, exp_neg[h], ALU.add,
                                         ALU.subtract).then_inc(one_plus_ready, 1)

            def make_dt(j, par, h):
                dve.wait_ge(log_ready, j * 2 + h + 1)
                part = by_row(dt[:, par, h * half:(h + 1) * half, :])
                chain(dve.scalar_tensor_tensor(part, part, 0.0, one_plus, ALU.max, ALU.add))
                dve.tensor_tensor(part, part, exp_neg[h], ALU.subtract).then_inc(dt_ready, 1)

            def make_dt_u(j, par, p):
                dve.wait_ge(dt_ready, j * 2 + p // 2 + 1)
                pair = slice(2 * p, 2 * p + 2)
                dve.tensor_tensor(dt_u[:, pair, :], dt[:, par, pair, :], u[:, par, pair, :],
                                  ALU.mult).then_inc(dt_u_ready, 1)

            def end_pair(i, par, p):
                dve.wait_ge(summed, i * units + (groups - 1) * pairs + p + 1 + 4)
                dve.wait_ge(gate_ready, i + 1)
                for cc in range(2):
                    c = 2 * p + cc
                    ins = dve.scalar_tensor_tensor(u[:, par, c, :], u[:, par, c, :], d_sb[:, c:c + 1],
                                                   y_ps[:, p, cc * T:(cc + 1) * T], ALU.mult, ALU.add)
                chain(ins)
                pair = slice(2 * p, 2 * p + 2)
                dve.tensor_tensor(gate[:, par, pair, :], u[:, par, pair, :], gate[:, par, pair, :],
                                  ALU.mult).then_inc(y_ready, 1)

            def add_input(t, par):
                dve.wait_ge(zm_stored, t * 16 + 32)
                for b in range(group):
                    dve.wait_ge(out_ready, t * group + b + 1)
                    dve.tensor_tensor(mix[:, b, :], work[:, b, :], xn[:, par, b, :], ALU.add).then_inc(sum_ready, 1)

            def normalise(t):
                dve.wait_ge(out_rstd_ready, t * 2 + 2)
                for b in range(group):
                    ins = dve.scalar_tensor_tensor(mix[:, b, :], mix[:, b, :], out_rstd[:, b:b + 1], norm_sb[:],
                                                   ALU.mult, ALU.mult)
                ins.then_inc(zm_ready, 1)

            def front(j, par):
                chain.base, chain.n = 0, 0
                for b in range(group):
                    add_heads(j, b)
                layernorm(j, par)
                dve.wait_ge(x_half_loaded, X_HALF_LOADED)
                for p in range(pairs):
                    convolve(j, par, p)
                take_low(j, par)
                for h in range(2):
                    take_t(j, par, h)
                for h in range(2):
                    add_one(j, h)
                    make_dt(j, par, h)
                for p in range(pairs):
                    make_dt_u(j, par, p)
                dve.wait_ge(loaded, LOADED)
                dve.wait_ge(ready, 10)
                dve.tensor_scalar(a_neg[:], a_neg[:], -1.0, None, ALU.mult).then_inc(ready, 1)
                assert chain.n == FRONT_LINKS

            def body(i, par, first, last):
                j = i + 1
                done = FRONT_LINKS + (FRONT_LINKS + END_LINKS - 1)
                per_step = TAIL_LINKS + FRONT_LINKS + END_LINKS
                chain.base, chain.n = (FRONT_LINKS if first else (i - 1) * per_step + done), 0
                for m in range(units):
                    g, p = m // pairs, m % pairs
                    dve.wait_ge(decay_ready, i * units + m + 1)
                    dve.wait_ge(drive_ready, i * units + m + 1)
                    if not first or m > 1:
                        dve.wait_ge(y_part, i * units + m - 1)
                    dve.tensor_tensor_scan(state[:, m % 2].rearrange("p n c t -> p (n c t)"),
                                           decay[:, m % 2].rearrange("p n c b t -> p (n c b t)"),
                                           drive[:, m % 4].rearrange("p n c t -> p (n c t)"),
                                           0.0, ALU.mult, ALU.add).then_inc(scanned, 1)
                    dve.wait_ge(scanned, i * units + m + 1 + 2)
                    if p == 0:
                        dve.wait_ge(bc_ready, i * 2 * groups + 2 * g + 2 + 2)
                    dve.tensor_tensor(drive[:, m % 4], state[:, m % 2],
                                      bc[:, g % bc_slots, 1].unsqueeze(2).to_broadcast([P, SG, 2, T]),
                                      ALU.mult).then_inc(y_part, 1)
                    if m == 0 and not first:
                        end_pair(i - 1, 1 - par, pairs - 1)
                    if not first and m == DVE_SUM:
                        add_input(i - 1, 1 - par)
                    if not last and m in DVE_X1:
                        add_heads(j, DVE_X1.index(m))
                    if not last and m == DVE_XN:
                        dve.wait_ge(sum_ready, (j + 1) * group)
                        layernorm(j, 1 - par)
                    if not first and m == DVE_ZM:
                        normalise(i - 1)
                    if not last:
                        if DVE_CONV <= m < DVE_CONV + pairs:
                            convolve(j, 1 - par, m - DVE_CONV)
                        if m == DVE_LOW:
                            take_low(j, 1 - par)
                        if m in DVE_T:
                            take_t(j, 1 - par, DVE_T.index(m))
                        if m in DVE_DT:
                            make_dt(j, 1 - par, DVE_DT.index(m))
                        if m in DVE_ONE_PLUS:
                            add_one(j, DVE_ONE_PLUS.index(m))
                        if m >= DVE_DT_U:
                            make_dt_u(j, 1 - par, m - DVE_DT_U)
                    if g == groups - 1 and p > 0:
                        end_pair(i, par, p - 1)
                if not last:
                    links = END_LINKS + FRONT_LINKS + TAIL_LINKS - (TAIL_LINKS + 1 if first else 0)
                    assert chain.n == links, (chain.n, links)

            def finish():
                end_pair(steps - 1, 1, pairs - 1)
                add_input(steps - 1, 1)
                normalise(steps - 1)

            run_steps(dve, front, body, finish)

        @block.tensor
        def _(pe):
            pe.sem_inc(summed, 4)
            pe.wait_ge(ready, 9)
            pe.wait_ge(wo_loaded, 16)

            def project_heads(j, b):
                if b == 0:
                    pe.wait_ge(attn_loaded, j * 16 + 16)
                    pe.wait_ge(sum_ready, (j + 1) * group)
                for g in range(chunks):
                    ins = pe.matmul(work[:, b, :], attn[:, b, g, :], wo[:, g, :], start=(g == 0),
                                    stop=(g == chunks - 1))
                ins.then_inc(o_ready, 1)

            def turn(j, par):
                pe.wait_ge(xn_ready, j + 1)
                for b in range(group):
                    for k in range(chunks):
                        ins = pe.transpose(work[:, b, k * P:(k + 1) * P], xn[:, par, b, k * P:(k + 1) * P], ident[:])
                    ins.then_inc(turned, 1)

            def project_in(j, n):
                if n < 2:
                    pe.wait_ge(xn_t_ready, (j + 1) * group)
                else:
                    pe.wait_ge(in_taken, j * in_pairs + n - 1)
                for cc in range(2):
                    col = (2 * n + cc) * P
                    for k in range(chunks):
                        ins = pe.matmul(work[:, n % 2, cc * T:(cc + 1) * T], w_in[:, k, col:col + P],
                                        xn_t[:, k, :], start=(k == 0), stop=(k == chunks - 1))
                ins.then_inc(in_ready, 1)

            def project_x(j, par):
                pe.wait_ge(in_taken, (j + 1) * in_pairs)
                for c in range(inner_chunks):
                    if c % half == 0:
                        pe.wait_ge(u_ready, j * 2 + c // half + 1)
                    ins = pe.matmul(work[:, 0, 0:T], w_x[:, c].rearrange("p w r -> p (w r)"), u[:, par, c, :],
                                    start=(c == 0), stop=(c == inner_chunks - 1))
                ins.then_inc(dbc_product, 1)

            def project_dt(j, h):
                if h == 0:
                    pe.wait_ge(dbc_ready, j + 1)
                    pe.wait_ge(low_ready, j + 1)
                else:
                    pe.wait_ge(t_taken, j * 2 + 1)
                for c in range(half):
                    col = (h * half + c) * P
                    ins = pe.matmul(work[:, c // 2, (c % 2) * T:(c % 2 + 1) * T], w_dt[:, col:col + P],
                                    dt_low[:], start=True, stop=True)
                ins.then_inc(dt_product, 1)

            def spread_bc(i, par, g, which):
                if g == 0:
                    pe.wait_ge(low_ready, i + 1)
                pe.wait_ge(bc_ready, i * 2 * groups + 2 * g + which + 1)
                for s in range(SG):
                    row = rank + which * states + g * SG + s
                    ins = pe.matmul(bc_ps[:, which, s * T:(s + 1) * T],
                                    selector[:, row:row + 1].to_broadcast([P, P]), dbc[:, par, :],
                                    start=True, stop=True)
                ins.then_inc(bc_product, 1)

            def project_out(i, par, p, last):
                pe.wait_ge(y_ready, (i + 1) * pairs + p + 1)
                if p == 0:
                    pe.wait_ge(t_taken, (i + (1 if last else 2)) * 2)
                for b in range(group):
                    for c in (2 * p, 2 * p + 1):
                        ins = pe.matmul(work[:, b, :], gate[:, par, c, b * P:(b + 1) * P], w_out[:, c, :],
                                        start=(c == 0), stop=(c == inner_chunks - 1))
                    if p == pairs - 1:
                        ins.then_inc(out_ready, 1)

            def front(j, par):
                for b in range(group):
                    project_heads(j, b)
                turn(j, par)
                for n in range(in_pairs):
                    if n == 0:
                        pe.wait_ge(x_half_loaded, X_HALF_LOADED)
                    if n == pairs:
                        pe.wait_ge(z_half_loaded, Z_HALF_LOADED)
                    project_in(j, n)
                pe.wait_ge(loaded, LOADED)
                project_x(j, par)
                for h in range(2):
                    project_dt(j, h)
                for g in range(2):
                    for which in range(2):
                        spread_bc(j, par, g, which)

            def body(i, par, first, last):
                j = i + 1
                for m in range(units):
                    g, p = m // pairs, m % pairs
                    if g == 0:
                        pe.wait_ge(y_ready, i * pairs + p + 1)
                    pe.wait_ge(y_part, i * units + m + 1)
                    for s in range(SG):
                        ins = pe.matmul(y_ps[:, p, :], ident[:], drive[:, m % 4, s].rearrange("p c t -> p (c t)"),
                                        start=(g == 0 and s == 0), stop=(g == groups - 1 and s == SG - 1))
                    ins.then_inc(summed, 1)
                    if p in (1, 2) and g + 2 < groups:
                        spread_bc(i, par, g + 2, p - 1)
                    if not first and m in PE_OUT_LAST:
                        project_out(i - 1, 1 - par, 2 + PE_OUT_LAST.index(m), False)
                    if not last:
                        if m in PE_HEADS:
                            project_heads(j, PE_HEADS.index(m))
                        if m == PE_TURN:
                            turn(j, 1 - par)
                        if PE_IN <= m < PE_IN + in_pairs:
                            project_in(j, m - PE_IN)
                        if m == PE_X:
                            project_x(j, 1 - par)
                        if m in PE_DT:
                            project_dt(j, PE_DT.index(m))
                        if p in (1, 2) and g + 2 >= groups:
                            spread_bc(j, 1 - par, g + 2 - groups, p - 1)
                    if m in PE_OUT:
                        project_out(i, par, PE_OUT.index(m), last)

            def finish():
                for p in (2, 3):
                    project_out(steps - 1, 1, p, True)

            run_steps(pe, front, body, finish)


def feed_forward(nc, x1_dram, zm_dram, w1_t, b1, w2_t, b2, norm_w, w_gate, w_shared_t, w_expert_t, bias, out):
    batches, _, width = x1_dram.shape
    hidden = w2_t.shape[0]
    gates = w_gate.shape[1]
    chunks, hidden_chunks = width // P, hidden // P
    group = 2
    steps = batches // group
    T = group * P
    LOWEST = -3.4e38
    LAG = 2
    piece = 2
    pieces = hidden_chunks // piece
    assert gates == 7 and steps % 2 == 0

    PE_TURN, PE_GATE, PE_SHARED, PE_EXPERT = 6, 8, (9, 12), (11, 13)
    ACT_SQUARES, ACT_XF, ACT_EXP = 1, 7, 10
    DVE_ADD, DVE_X2, DVE_XF, DVE_GATE, DVE_WEIGHTS, DVE_OUT = 0, 3, 5, 9, 11, (11, 14)

    with ExitStack() as ctx:
        def sb(name, shape, dt=F32):
            return ctx.enter_context(nc.sbuf_tensor(name, shape, dt))

        def psum(name, shape):
            return ctx.enter_context(nc.psum_tensor(name, shape, F32))

        def sem(name):
            return ctx.enter_context(nc.semaphore(name))

        w1_hi, w1_lo = sb("c_w1_hi", [P, chunks, hidden], F32R), sb("c_w1_lo", [P, chunks, hidden], F32R)
        w2_hi, w2_lo = sb("c_w2_hi", [P, hidden_chunks, width], F32R), sb("c_w2_lo", [P, hidden_chunks, width], F32R)
        w_s, w_e = sb("c_w_s", [P, chunks, width]), sb("c_w_e", [P, chunks, width])
        w_g = sb("c_w_g", [P, chunks, gates])
        b1_sb = sb("c_b1", [P, hidden_chunks])
        b2_sb, norm_sb, bias_sb = sb("c_b2", [P, width]), sb("c_norm", [P, width]), sb("c_bias", [P, width])
        ident = sb("c_ident", [P, P])
        eps_ln, eps_rms = sb("c_eps_ln", [P, group]), sb("c_eps_rms", [P, group])
        minus_half = sb("c_minus_half", [P, group])
        wait_taker = sb("c_wait_taker", [P, 1])

        zm = sb("c_zm", [P, 2, group, width])
        x1 = sb("c_x1", [P, group, width])
        zm_hi, zm_lo = sb("c_zm_hi", [P, chunks, T], F32R), sb("c_zm_lo", [P, chunks, T], F32R)
        xf_t = sb("c_xf_t", [P, chunks, T])
        h, h_hi, h_lo = sb("c_h", [P, 4, T]), sb("c_h_hi", [P, 4, T], F32R), sb("c_h_lo", [P, 4, T], F32R)
        mix = sb("c_mix", [P, group, width])
        xf = sb("c_xf", [P, group, width])
        out_sb = xf
        squares, mean_sq = sb("c_squares", [P, width]), sb("c_mean_sq", [P, group])
        rms_rstd, rstd = sb("c_rms_rstd", [P, group]), sb("c_rstd", [P, group])
        stats, moments = sb("c_stats", [P, group, 6]), sb("c_moments", [P, group, 2])
        logits, top = sb("c_logits", [P, group, 8]), sb("c_top", [P, group, 8])
        neg_top, exps, exp_sum = sb("c_neg_top", [P, group]), sb("c_exps", [P, group, 8]), sb("c_exp_sum", [P, group])
        two, two_sum, token_weight = sb("c_two", [P, group, 2]), sb("c_two_sum", [P, group]), sb("c_tw", [P, group])
        w1_raw = tuple(t.rearrange("p b (k o) -> p (b k) o", o=piece * P) for t in (mix[:], xf[:]))
        w2_raw = (xf_t[:].rearrange("p (m k) t -> p m (k t)", m=piece), x1[:])

        ring = psum("c_ring", [P, 2, 512])
        acc = psum("c_acc", [P, group, 512])
        turned_ps = psum("c_turned_ps", [P, group, 512])
        experts_ps = psum("c_experts_ps", [P, 2, 512])

        ready = sem("c_ready")
        zm_loaded, x1_loaded = sem("c_zm_loaded"), sem("c_x1_loaded")
        w1_loaded = (sem("c_w1_even_loaded"), sem("c_w1_odd_loaded"))
        w2_loaded = (sem("c_w2_even_loaded"), sem("c_w2_odd_loaded"))
        consts_loaded, experts_loaded = sem("c_consts_loaded"), sem("c_experts_loaded")
        w1_split, w2_high, w2_split = sem("c_w1_split"), sem("c_w2_high"), sem("c_w2_split")
        zm_turned, zm_hi_ready, zm_lo_ready = sem("c_zm_turned"), sem("c_zm_hi_ready"), sem("c_zm_lo_ready")
        h_product, h_ready = sem("c_h_product"), sem("c_h_ready")
        h_hi_ready, h_lo_ready = sem("c_h_hi_ready"), sem("c_h_lo_ready")
        h_used = sem("c_h_used")
        mix_ready, squared, rms_ready = sem("c_mix_ready"), sem("c_squared"), sem("c_rms")
        x2_ready = sem("c_x2_ready")
        moments_ready, rstd_ready, xf_ready = sem("c_moments_ready"), sem("c_rstd_ready"), sem("c_xf_ready")
        xf_turned, xf_t_ready = sem("c_xf_turned"), sem("c_xf_t_ready")
        gate_ready, gate_taken = sem("c_gate_ready"), sem("c_gate_taken")
        logits_ready, exp_ready = sem("c_logits_ready"), sem("c_exp_ready")
        ffn_ready, ffn_taken = sem("c_ffn_ready"), sem("c_ffn_taken")
        out_stored = sem("c_out_stored")
        dve_order = sem("c_dve_order")

        block = ctx.enter_context(nc.Block())
        x1_v, zm_v, out_v = (t.rearrange("(s b) t d -> s t b d", b=group) for t in (x1_dram, zm_dram, out))

        def run_steps(eng, body):
            body(0, 0, True, False)
            with eng.Fori(0, (steps - 2) // 2) as k:
                body(k * 2 + 1, 1, False, False)
                body(k * 2 + 2, 0, False, False)
            body(steps - 1, 1, False, True)

        @block.sync
        def _(sp):
            sp.sem_inc(out_stored, 16)
            w1_v = w1_t.rearrange("(k p) o -> p k o", p=P)
            w2_v = w2_t.rearrange("(m p) o -> p m o", p=P)
            sp.dma_start(zm[:, 0], zm_v[0]).then_inc(zm_loaded, 16)
            for n in range(pieces):
                if n >= 2:
                    sp.wait_ge(w1_split, n - 1)
                sp.dma_start(w1_raw[n % 2], w1_v[:, :, n * piece * P:(n + 1) * piece * P]
                             ).then_inc(w1_loaded[n % 2], 16)
                if n >= 2:
                    sp.wait_ge(w2_split, n - 1)
                sp.dma_start(w2_raw[n % 2], w2_v[:, n * piece:(n + 1) * piece, :]).then_inc(w2_loaded[n % 2], 16)
                if n == 1:
                    for dst, src in ((b1_sb[:], b1), (b2_sb[:], b2.partition_broadcast(P)),
                                     (norm_sb[:], norm_w.partition_broadcast(P)),
                                     (bias_sb[:], bias.partition_broadcast(P))):
                        sp.dma_start(dst, src).then_inc(consts_loaded, 16)
            sp.wait_ge(w2_split, pieces)
            sp.dma_start(x1[:], x1_v[0]).then_inc(x1_loaded, 16)
            sp.wait_ge(zm_loaded, 16)
            sp.dma_start(zm[:, 1], zm_v[1]).then_inc(zm_loaded, 16)
            for dst, src in ((w_g[:], w_gate.rearrange("(k p) o -> p k o", p=P)),
                             (w_s[:], w_shared_t.rearrange("(k p) o -> p k o", p=P)),
                             (w_e[:], w_expert_t.rearrange("(k p) o -> p k o", p=P))):
                sp.dma_start(dst, src).then_inc(experts_loaded, 16)

            def body(i, par, first, last):
                if first:
                    return
                if not last:
                    sp.wait_ge(mix_ready, i * group + group)
                    sp.dma_start(zm[:, 1 - par], zm_v[i + 1]).then_inc(zm_loaded, 16)
                sp.wait_ge(x2_ready, i)
                sp.dma_start(x1[:], x1_v[i]).then_inc(x1_loaded, 16)
                sp.wait_ge(ffn_taken, i * group + 1)
                sp.dma_start(out_v[i - 1], out_sb[:]).then_inc(out_stored, 16)

            run_steps(sp, body)
            sp.wait_ge(ffn_taken, steps * group + 1)
            sp.dma_start(out_v[steps - 1], out_sb[:]).then_inc(out_stored, 16)
            sp.wait_ge(out_stored, 16 * (steps + 1))

        CONSTS_LOADED, EXPERTS_LOADED = 4 * 16, 3 * 16

        @block.gpsimd
        def _(pool):
            pool.memset(ident[:], 0.0).then_inc(ready, 1)
            pool.memset(eps_ln[:], LN_EPS).then_inc(ready, 1)
            pool.memset(eps_rms[:], RMS_EPS).then_inc(ready, 1)
            pool.memset(minus_half[:], -0.5).then_inc(ready, 1)
            pool.memset(logits[:], LOWEST).then_inc(ready, 1)
            pool.wait_ge(ready, 5)
            pool.affine_select(out=ident[:], in_=ident[:], compare_op=ALU.not_equal, fill=1.0, base=0,
                               pattern=[[-1, P]], channel_multiplier=1).then_inc(ready, 1)
            for n in range(pieces):
                rows = slice(n * piece, (n + 1) * piece)
                pool.wait_ge(w2_high, n + 1)
                pool.tensor_tensor(w2_lo[:, rows, :], w2_raw[n % 2], w2_hi[:, rows, :].bitcast(F32),
                                   ALU.subtract).then_inc(w2_split, 1)

            def make_rstd(n, out, variance, eps, done):
                pool.tensor_tensor(out[:], variance, eps[:], ALU.add).then_inc(done, 1)
                pool.wait_ge(done, n * 2 + 1)
                pool.tensor_tensor(out[:], out[:], minus_half[:], ALU.pow).then_inc(done, 1)

            with pool.Fori(0, steps) as t:
                pool.wait_ge(squared, (t + 1) * group)
                make_rstd(t, rms_rstd, mean_sq[:], eps_rms, rms_ready)
                pool.wait_ge(moments_ready, t + 1)
                make_rstd(t, rstd, moments[:, :, 1], eps_ln, rstd_ready)

        @block.scalar
        def _(act):
            act.sem_inc(h_ready, 2)

            def take_zm(i):
                for b in range(group):
                    act.wait_ge(zm_turned, i * group + b + 1)
                    act.copy(zm_hi[:, :, b * P:(b + 1) * P],
                             turned_ps[:, b, :].rearrange("p (k t) -> p k t", t=P)).then_inc(zm_hi_ready, 1)

            def take_squares(t):
                for b in range(group):
                    act.wait_ge(mix_ready, t * group + b + 1 + group)
                    act.activation(squares[:], mix[:, b, :], ACT.Square, scale=float(width) ** -0.5,
                                   accum_out=mean_sq[:, b:b + 1]).then_inc(squared, 1)
                    act.wait_ge(squared, t * group + b + 1)

            def take_xf(t):
                for b in range(group):
                    act.wait_ge(xf_turned, t * group + b + 1)
                    act.copy(xf_t[:, :, b * P:(b + 1) * P],
                             turned_ps[:, b, :].rearrange("p (k t) -> p k t", t=P)).then_inc(xf_t_ready, 1)

            def exponentials(t):
                act.wait_ge(logits_ready, t + 1)
                for b in range(group):
                    ins = act.activation(exps[:, b, :], top[:, b, :], ACT.Exp, bias=neg_top[:, b:b + 1],
                                         accum_out=exp_sum[:, b:b + 1])
                ins.then_inc(exp_ready, 1)

            take_zm(0)
            act.wait_ge(consts_loaded, CONSTS_LOADED)

            def body(i, par, first, last):
                for m in range(hidden_chunks):
                    act.wait_ge(h_product, i * hidden_chunks + m + 1)
                    act.wait_ge(h_lo_ready, i * hidden_chunks + m + 1)
                    act.activation(h[:, m % 4, :], ring[:, m % 2, 0:T], ACT.Gelu,
                                   bias=b1_sb[:, m:m + 1]).then_inc(h_ready, 1)
                    if first:
                        continue
                    if m == ACT_SQUARES:
                        take_squares(i - 1)
                    if m == ACT_XF:
                        take_xf(i - 1)
                    if m == ACT_EXP:
                        exponentials(i - 1)
                if not last:
                    take_zm(i + 1)

            run_steps(act, body)
            take_squares(steps - 1)
            take_xf(steps - 1)
            exponentials(steps - 1)

        @block.vector
        def _(dve):
            chain = Chain(dve, dve_order)
            dve.sem_inc(h_lo_ready, 4)
            dve.sem_inc(mix_ready, group)
            dve.sem_inc(ffn_taken, 1)
            dve.wait_ge(ready, 6)
            TAIL_LINKS = 2 * group + 10

            def split_weights(n):
                cols, rows = slice(n * piece * P, (n + 1) * piece * P), slice(n * piece, (n + 1) * piece)
                turn = (n // 2 + 1) * 16
                dve.wait_ge(w1_loaded[n % 2], turn)
                chain(dve.tensor_copy(w1_hi[:, :, cols], w1_raw[n % 2]))
                dve.tensor_tensor(w1_lo[:, :, cols], w1_raw[n % 2], w1_hi[:, :, cols].bitcast(F32),
                                  ALU.subtract).then_inc(w1_split, 1)
                dve.wait_ge(w2_loaded[n % 2], turn)
                dve.tensor_copy(w2_hi[:, rows, :], w2_raw[n % 2]).then_inc(w2_high, 1)

            def split_zm(i):
                for b in range(group):
                    cols = slice(b * P, (b + 1) * P)
                    dve.wait_ge(zm_hi_ready, i * group + b + 1)
                    dve.tensor_tensor(zm_lo[:, :, cols], turned_ps[:, b, :].rearrange("p (k t) -> p k t", t=P),
                                      zm_hi[:, :, cols].bitcast(F32), ALU.subtract).then_inc(zm_lo_ready, 1)

            def split_h(i, m):
                n = i * hidden_chunks + m
                dve.wait_ge(h_ready, n + 1 + 2)
                dve.wait_ge(h_used, n + 1)
                dve.tensor_copy(h_hi[:, m % 4, :], h[:, m % 4, :]).then_inc(h_hi_ready, 1)
                dve.wait_ge(h_hi_ready, n + 1)
                dve.tensor_tensor(h_lo[:, m % 4, :], h[:, m % 4, :], h_hi[:, m % 4, :].bitcast(F32),
                                  ALU.subtract).then_inc(h_lo_ready, 1)

            def add_mlp(t, par):
                dve.wait_ge(h_used, (t + 1) * hidden_chunks + 4)
                dve.wait_ge(ffn_taken, t * group + 1)
                for b in range(group):
                    chain(dve.tensor_tensor(mix[:, b, :], acc[:, b, :], zm[:, par, b, :], ALU.add))
                    dve.tensor_tensor(mix[:, b, :], mix[:, b, :], b2_sb[:], ALU.add).then_inc(mix_ready, 1)

            def make_x2(t):
                dve.wait_ge(rms_ready, t * 2 + 2)
                for b in range(group):
                    ins = dve.scalar_tensor_tensor(mix[:, b, :], mix[:, b, :], rms_rstd[:, b:b + 1], norm_sb[:],
                                                   ALU.mult, ALU.mult)
                chain(ins)
                dve.wait_ge(x1_loaded, t * 16 + 16)
                dve.tensor_tensor(mix[:], mix[:], x1[:], ALU.add).then_inc(x2_ready, 1)
                dve.wait_ge(x2_ready, t + 1)
                for b in range(group):
                    ins = dve.bn_stats(stats[:, b, :], mix[:, b, :])
                chain(ins)
                dve.memset(wait_taker[:], 0.0)
                for b in range(group):
                    ins = dve.bn_aggr(moments[:, b, :], stats[:, b, :])
                ins.then_inc(moments_ready, 1)

            def make_xf(t):
                dve.wait_ge(rstd_ready, t * 2 + 2)
                dve.wait_ge(out_stored, t * 16 + 16)
                for b in range(group):
                    ins = dve.tensor_scalar(xf[:, b, :], mix[:, b, :], moments[:, b, 0:1], rstd[:, b:b + 1],
                                            ALU.subtract, ALU.mult)
                ins.then_inc(xf_ready, 1)
                dve.wait_ge(xf_ready, t + 1)
                chain(dve.tensor_tensor(mix[:], mix[:], bias_sb[:].unsqueeze(1).to_broadcast([P, group, width]),
                                        ALU.add))

            def take_gate(t):
                dve.wait_ge(gate_ready, t + 1)
                dve.tensor_copy(logits[:, :, 0:gates],
                                turned_ps[:, 0, 0:group * 8].rearrange("p (b e) -> p b e", e=8)[:, :, 0:gates]
                                ).then_inc(gate_taken, 1)
                dve.wait_ge(gate_taken, t + 1)
                dve.memset(wait_taker[:], 0.0)
                for b in range(group):
                    ins = dve.max(out=top[:, b, :], in_=logits[:, b, :])
                chain(ins)
                dve.tensor_scalar(neg_top[:], top[:, :, 0], -1.0, None, ALU.mult).then_inc(logits_ready, 1)

            def weigh(t):
                dve.wait_ge(exp_ready, t + 1)
                chain(dve.reciprocal(exp_sum[:], exp_sum[:]))
                chain(dve.tensor_tensor(two[:], exps[:, :, 0:2], exp_sum[:].unsqueeze(2).to_broadcast([P, group, 2]),
                                        ALU.mult))
                chain(dve.tensor_reduce(two_sum[:], two[:], AX.X, ALU.add))
                chain(dve.reciprocal(two_sum[:], two_sum[:]))
                chain(dve.tensor_tensor(two[:], two[:], two_sum[:].unsqueeze(2).to_broadcast([P, group, 2]), ALU.mult))
                chain(dve.tensor_reduce(token_weight[:], two[:], AX.X, ALU.add))

            def finish(t, b):
                dve.wait_ge(ffn_ready, t * group + b + 1)
                chain(dve.scalar_tensor_tensor(out_sb[:, b, :], experts_ps[:, 1, :], token_weight[:, b:b + 1],
                                               mix[:, b, :], ALU.mult, ALU.add))
                dve.tensor_tensor(out_sb[:, b, :], out_sb[:, b, :], experts_ps[:, 0, :], ALU.add
                                  ).then_inc(ffn_taken, 1)

            for n in range(2):
                split_weights(n)
            split_zm(0)

            def body(i, par, first, last):
                if not first:
                    chain.base, chain.n = (i - 1) * TAIL_LINKS + pieces, 0
                for m in range(hidden_chunks):
                    split_h(i, m)
                    if first:
                        if m % piece == 0 and m // piece + 2 < pieces:
                            split_weights(m // piece + 2)
                        continue
                    if m == DVE_ADD:
                        add_mlp(i - 1, 1 - par)
                        dve.wait_ge(consts_loaded, CONSTS_LOADED)
                    if m == DVE_X2:
                        make_x2(i - 1)
                    if m == DVE_XF:
                        make_xf(i - 1)
                    if m == DVE_GATE:
                        take_gate(i - 1)
                    if m == DVE_WEIGHTS:
                        weigh(i - 1)
                    if m in DVE_OUT:
                        finish(i - 1, DVE_OUT.index(m))
                assert chain.n == (pieces if first else TAIL_LINKS), chain.n
                if not last:
                    split_zm(i + 1)

            run_steps(dve, body)
            chain.base, chain.n = (steps - 1) * TAIL_LINKS + pieces, 0
            add_mlp(steps - 1, 1)
            make_x2(steps - 1)
            make_xf(steps - 1)
            take_gate(steps - 1)
            weigh(steps - 1)
            for b in range(group):
                finish(steps - 1, b)

        @block.tensor
        def _(pe):
            pe.sem_inc(h_used, 4)
            pe.wait_ge(ready, 6)

            def turn_zm(i, par, waits):
                if waits:
                    pe.wait_ge(gate_taken, i - 1)
                pe.wait_ge(zm_loaded, i * 16 + 16)
                for b in range(group):
                    for k in range(chunks):
                        ins = pe.transpose(turned_ps[:, b, k * P:(k + 1) * P], zm[:, par, b, k * P:(k + 1) * P],
                                           ident[:])
                    ins.then_inc(zm_turned, 1)

            def first_product(i, m, first):
                if m == 0:
                    pe.wait_ge(zm_lo_ready, (i + 1) * group)
                if first and m % piece == 0:
                    pe.wait_ge(w1_split, m // piece + 1)
                pe.wait_ge(h_ready, i * hidden_chunks + m + 1)
                cols = slice(m * P, (m + 1) * P)
                for n, (w, z) in enumerate(((w1_hi, zm_hi), (w1_lo, zm_hi), (w1_hi, zm_lo))):
                    for k in range(chunks):
                        ins = pe.matmul(ring[:, m % 2, 0:T], w[:, k, cols], z[:, k, :], start=(n == 0 and k == 0),
                                        stop=(n == 2 and k == chunks - 1))
                ins.then_inc(h_product, 1)

            def second_product(i, m, first):
                if m == 0:
                    pe.wait_ge(mix_ready, i * group + group)
                if first and m % piece == 0:
                    pe.wait_ge(w2_split, m // piece + 1)
                pe.wait_ge(h_lo_ready, i * hidden_chunks + m + 1 + 4)
                for b in range(group):
                    rows = slice(b * P, (b + 1) * P)
                    for n, (a, w) in enumerate(((h_hi, w2_hi), (h_lo, w2_hi), (h_hi, w2_lo))):
                        ins = pe.matmul(acc[:, b, :], a[:, m % 4, rows], w[:, m, :], start=(m == 0 and n == 0),
                                        stop=(m == hidden_chunks - 1 and n == 2))
                ins.then_inc(h_used, 1)

            def turn_xf(t):
                pe.wait_ge(xf_ready, t + 1)
                for b in range(group):
                    for k in range(chunks):
                        ins = pe.transpose(turned_ps[:, b, k * P:(k + 1) * P], xf[:, b, k * P:(k + 1) * P], ident[:])
                    ins.then_inc(xf_turned, 1)

            def gate(t):
                pe.wait_ge(experts_loaded, EXPERTS_LOADED)
                pe.wait_ge(xf_t_ready, (t + 1) * group)
                for b in range(group):
                    for k in range(chunks):
                        ins = pe.matmul(turned_ps[:, 0, b * 8:b * 8 + gates], xf_t[:, k, b * P:(b + 1) * P],
                                        w_g[:, k, :], start=(k == 0), stop=(k == chunks - 1))
                ins.then_inc(gate_ready, 1)

            def expert(t, b, bank, w):
                if bank == 0:
                    pe.wait_ge(ffn_taken, t * group + b + 1)
                for k in range(chunks):
                    ins = pe.matmul(experts_ps[:, bank, :], xf_t[:, k, b * P:(b + 1) * P], w[:, k, :],
                                    start=(k == 0), stop=(k == chunks - 1))
                if bank == 1:
                    ins.then_inc(ffn_ready, 1)

            turn_zm(0, 0, False)

            def body(i, par, first, last):
                for m in range(hidden_chunks):
                    first_product(i, m, first)
                    if m >= LAG:
                        second_product(i, m - LAG, first)
                    if first:
                        continue
                    if m == PE_TURN:
                        turn_xf(i - 1)
                    if m == PE_GATE:
                        gate(i - 1)
                    if m in PE_SHARED:
                        expert(i - 1, PE_SHARED.index(m), 0, w_s)
                    if m in PE_EXPERT:
                        expert(i - 1, PE_EXPERT.index(m), 1, w_e)
                if not last:
                    turn_zm(i + 1, 1 - par, not first)
                for m in range(hidden_chunks - LAG, hidden_chunks):
                    second_product(i, m, first)

            run_steps(pe, body)
            turn_xf(steps - 1)
            gate(steps - 1)
            for b in range(group):
                for bank, w in enumerate((w_s, w_e)):
                    expert(steps - 1, b, bank, w)


def perceiver_layer(nc, i, out):
    batches, seq, width = i["x"].shape
    heads_shape = (batches, P, width // P, seq)
    q_dram = nc.dram_tensor("q_scratch", heads_shape, F32).ap()
    attn_dram = nc.dram_tensor("attn_scratch", heads_shape, F32).ap()
    x1_dram = nc.dram_tensor("x1_scratch", (batches, seq, width), F32).ap()
    zm_dram = nc.dram_tensor("zm_scratch", (batches, seq, width), F32).ap()
    project_queries(nc, i["x"], i["xattn_wq"], i["xattn_bq"], q_dram)
    cross_attention(nc, i["ctx"], i["xattn_wk"], i["xattn_wv"], i["xattn_bk"], i["xattn_bv"], q_dram, attn_dram,
                    heads=16)
    mamba(nc, i["x"], attn_dram, i["xattn_wo"], i["xattn_bo"], i["in_proj_w"], i["conv_w"], i["conv_b"],
          i["x_proj_w"], i["dt_proj_w"], i["dt_proj_b"], i["A_log"], i["D"], i["out_proj_w"], i["norm1_w"],
          x1_dram, zm_dram)
    feed_forward(nc, x1_dram, zm_dram, i["mlp_w1"], i["mlp_b1"], i["mlp_w2"], i["mlp_b2"], i["norm1_w"],
                 i["W_gate"], i["W_shared"], i["W_expert"], i["bias"], out)


def kernel(**inputs):
    import concourse.bacc as bacc
    from concourse.bass_utils import run_bass_kernel_spmd

    a = {name.removeprefix("L0_").removeprefix("attn_").removeprefix("ffn_"): np.asarray(v)
         for name, v in inputs.items()}

    def by_channel(v):
        return v.reshape((-1, P) + v.shape[1:]).swapaxes(0, 1)

    laid_out = {
        "x": a["x"],
        "ctx": a["ctx_1024"].transpose(0, 2, 1),
        "xattn_wq": a["xattn_wq"].T, "xattn_wk": a["xattn_wk"].T, "xattn_wv": a["xattn_wv"].T,
        "xattn_wo": a["xattn_wo"].T,
        "xattn_bq": by_channel(a["xattn_bq"]), "xattn_bk": by_channel(a["xattn_bk"]),
        "xattn_bv": by_channel(a["xattn_bv"]), "xattn_bo": a["xattn_bo"],
        "in_proj_w": a["in_proj_w"].T, "conv_w": by_channel(a["conv_w"]), "conv_b": by_channel(a["conv_b"]),
        "x_proj_w": a["x_proj_w"].T, "dt_proj_w": a["dt_proj_w"].T, "dt_proj_b": a["dt_proj_b"][None, :],
        "A_log": by_channel(a["A_log"]), "D": by_channel(a["D"]), "out_proj_w": a["out_proj_w"].T,
        "norm1_w": a["norm1_w"], "mlp_w1": a["mlp_w1"].T, "mlp_b1": by_channel(a["mlp_b1"]),
        "mlp_w2": a["mlp_w2"].T, "mlp_b2": a["mlp_b2"],
        "W_gate": a["W_gate"], "W_shared": a["W_shared"].T, "W_expert": a["W_expert"].T, "bias": a["bias"],
    }
    nc = bacc.Bacc("TRN2", target_bir_lowering=False, num_devices=1)
    arrays, aps = {}, {}
    for name, v in laid_out.items():
        arrays[f"in_{name}"] = np.ascontiguousarray(v)
        aps[name] = nc.dram_tensor(f"in_{name}", v.shape, mybir.dt.from_np(v.dtype), kind="ExternalInput").ap()
    out = nc.dram_tensor("out", a["x"].shape, F32, kind="ExternalOutput").ap()
    perceiver_layer(nc, aps, out)
    r = run_bass_kernel_spmd(nc, [arrays], core_ids=[0])
    return r.results[0]["out"]
```
